# Optimizing a Trainium2 kernel written in Bass

```python
import numpy as np
import jax
import jax.numpy as jnp

def _softmax(x, axis=-1):
    return jax.nn.softmax(x, axis=axis)

def _gelu(x):
    return jax.nn.gelu(x, approximate=True)

def _silu(x):
    return jax.nn.silu(x)

def _sigmoid(x):
    return jax.nn.sigmoid(x)

def _layernorm(x, axis=-1, eps=1e-05):
    m = jnp.mean(x, axis=axis, keepdims=True)
    v = jnp.var(x, axis=axis, keepdims=True)
    return (x - m) / jnp.sqrt(v + eps)

def _scatter_add(tgt, idx, src, axis=0):
    return tgt.at[idx].add(src)

def _segment_sum(src, seg, n):
    return jax.ops.segment_sum(src, seg, n)
kernel_name = 'mk_gps_d2_gnn_r8_5b2588'

def setup_inputs(seed: int=0):
    np.random.seed(seed)
    _w = jnp.asarray

    def _rec_inputs():
        import jax
        import jax.numpy as jnp
        _gk = jax.random.key(seed)
        x = -0.0003713 + 1 * jax.random.normal(jax.random.fold_in(_gk, 1), (6250, 256), jnp.float32)
        src = jax.random.randint(jax.random.fold_in(_gk, 2), (100000,), 0, 6250, jnp.int32)
        dst = jax.random.randint(jax.random.fold_in(_gk, 3), (100000,), 0, 6250, jnp.int32)
        _o = jnp.argsort(dst, stable=True)
        src = src[_o]
        dst = dst[_o]
        edge_type_8 = jax.random.randint(jax.random.fold_in(_gk, 13), (100000,), 0, 8, jnp.int32)
        edge_weight1 = jax.random.uniform(jax.random.fold_in(_gk, 14), (100000, 1), jnp.float32, 0.0, 1)
        return (x, src, dst, edge_type_8, edge_weight1)
    x, src, dst, edge_type_8, edge_weight1 = _rec_inputs()

    def _L0_gnn_setup():
        import jax, jax.numpy as jnp
        import numpy as np
        N_NODES = 6250
        N_EDGES = 100000
        IN_FEAT = 256
        OUT_FEAT = 256
        NUM_RELS = 8
        NUM_BASES = 4
        key = jax.random.key(seed)
        ks = jax.random.split(key, 8)
        feat = jax.random.normal(ks[0], (N_NODES, IN_FEAT), dtype=jnp.float32)
        norm = jax.random.uniform(ks[1], (N_EDGES, 1), dtype=jnp.float32)
        src = jax.random.randint(ks[2], (N_EDGES,), 0, N_NODES)
        dst = jax.random.randint(ks[3], (N_EDGES,), 0, N_NODES)
        etypes = jax.random.randint(ks[4], (N_EDGES,), 0, NUM_RELS)
        weight = jax.random.normal(ks[5], (NUM_BASES, IN_FEAT, OUT_FEAT), dtype=jnp.float32) * (2.0 / np.sqrt(IN_FEAT + OUT_FEAT))
        w_comp = jax.random.normal(ks[6], (NUM_RELS, NUM_BASES), dtype=jnp.float32) * (2.0 / np.sqrt(NUM_RELS + NUM_BASES))
        loop_weight = jax.random.normal(ks[7], (IN_FEAT, OUT_FEAT), dtype=jnp.float32) * (2.0 / np.sqrt(IN_FEAT + OUT_FEAT))
        h_bias = jnp.zeros((OUT_FEAT,), dtype=jnp.float32)
        return {'feat': feat, 'weight': weight, 'w_comp': w_comp, 'loop_weight': loop_weight, 'h_bias': h_bias, 'norm': norm, 'src': src, 'dst': dst, 'etypes': etypes}
    _L0_gnn_all = _L0_gnn_setup()
    _L0_gnn_in = {k: v for k, v in _L0_gnn_all.items() if k in ('weight', 'w_comp', 'loop_weight', 'h_bias')}
    del _L0_gnn_all

    def _L0_mix_setup():
        import jax, jax.numpy as jnp
        import numpy as np
        HEADS = 4
        DIM_HEAD = 32
        key = jax.random.key(seed)
        k1, k2, k3 = jax.random.split(key, 3)
        B, L, D = (16, 1024, 256)
        hidden = HEADS * DIM_HEAD
        x = jax.random.normal(k1, (B, L, D), dtype=jnp.float32)
        W_qkv = jax.random.normal(k2, (D, 3 * hidden), dtype=jnp.float32) * D ** (-0.5)
        W_out = jax.random.normal(k3, (hidden, D), dtype=jnp.float32) * hidden ** (-0.5)
        b_out = jnp.zeros((D,), dtype=jnp.float32)
        return {'x': x, 'W_qkv': W_qkv, 'W_out': W_out, 'b_out': b_out}
    _L0_mix_all = _L0_mix_setup()
    _L0_mix_in = {k: v for k, v in _L0_mix_all.items() if k in ('W_qkv', 'W_out', 'b_out')}
    del _L0_mix_all

    def _L0_ffn_setup():
        import jax, jax.numpy as jnp
        import numpy as np
        B, S, D = (8, 512, 256)
        H = 4 * D
        CAPACITY = 0.5
        key = jax.random.key(seed)
        ks = jax.random.split(key, 6)
        x = jax.random.normal(ks[0], (B, S, D), dtype=jnp.float32)
        attention_mask = jnp.zeros((B, 1, 1, S), dtype=jnp.float32)
        wr = jax.random.normal(ks[1], (D, 1), dtype=jnp.float32) * 0.02
        br = jnp.zeros((1,), dtype=jnp.float32)
        w1 = jax.random.normal(ks[2], (D, H), dtype=jnp.float32) * 0.02
        b1 = jnp.zeros((H,), dtype=jnp.float32)
        w2 = jax.random.normal(ks[3], (H, D), dtype=jnp.float32) * 0.02
        b2 = jnp.zeros((D,), dtype=jnp.float32)
        return {'x': x, 'attention_mask': attention_mask, 'wr': wr, 'br': br, 'w1': w1, 'b1': b1, 'w2': w2, 'b2': b2}
    _L0_ffn_all = _L0_ffn_setup()
    _L0_ffn_in = {k: v for k, v in _L0_ffn_all.items() if k in ('attention_mask', 'wr', 'br', 'w1', 'b1', 'w2', 'b2')}
    del _L0_ffn_all

    def _L1_gnn_setup():
        import jax, jax.numpy as jnp
        import numpy as np
        N_NODES = 6250
        N_EDGES = 37500
        DIM = 256
        ALPHA = 0.1

        def gcn_layer(x0, x, edge_idx, W):
            src, dst = (edge_idx[0], edge_idx[1])
            msgs = x[src]
            agg = jax.ops.segment_sum(msgs, dst, num_segments=x.shape[0])
            deg = jax.ops.segment_sum(jnp.ones((src.shape[0],), x.dtype), dst, num_segments=x.shape[0])
            agg = agg / jnp.maximum(deg, 1.0)[:, None]
            h = ALPHA * x0 + (1.0 - ALPHA) * agg
            return h @ W
        key = jax.random.key(seed)
        k1, k2, k3 = jax.random.split(key, 3)
        x = jax.random.normal(k1, (N_NODES, DIM), dtype=jnp.float32)
        edge_idx = jax.random.randint(k2, (2, N_EDGES), 0, N_NODES, dtype=jnp.int64)
        W = jax.random.normal(k3, (DIM, DIM), dtype=jnp.float32) / np.sqrt(DIM)
        return {'drug_cell_pair_feature': x, 'edge_idx': edge_idx, 'W': W}
    _L1_gnn_all = _L1_gnn_setup()
    _L1_gnn_in = {k: v for k, v in _L1_gnn_all.items() if k in ('W',)}
    del _L1_gnn_all

    def _L1_mix_setup():
        import jax, jax.numpy as jnp
        import numpy as np
        import math
        EMBED = 256
        HEADS = 4
        HEAD_DIM = EMBED // HEADS
        OUT_DIM = 256
        LN_EPS = 1e-05

        def _qkv_init(key):
            spread = math.sqrt(3.0 / EMBED)
            gain, delta = (0.01, 0.01)
            w = jax.random.uniform(key, (EMBED, EMBED), minval=-spread, maxval=spread) * gain
            return w + delta * jnp.eye(EMBED, dtype=w.dtype)

        def _layer_norm(x, g, b):
            mu = jnp.mean(x, axis=-1, keepdims=True)
            var = jnp.mean(jnp.square(x - mu), axis=-1, keepdims=True)
            return (x - mu) * jax.lax.rsqrt(var + LN_EPS) * g + b

        def _split_heads(x, B, S):
            return x.reshape(B, S, HEADS, HEAD_DIM).transpose(0, 2, 1, 3)
        key = jax.random.key(seed)
        ks = jax.random.split(key, 6)
        seq = jax.random.normal(ks[0], (4, 1024, EMBED), dtype=jnp.float32)
        wq = _qkv_init(ks[1])
        wk = _qkv_init(ks[2])
        wv = _qkv_init(ks[3])
        bound = 1.0 / math.sqrt(EMBED)
        wo = jax.random.uniform(ks[4], (OUT_DIM, EMBED), minval=-bound, maxval=bound)
        bo = jax.random.uniform(ks[5], (OUT_DIM,), minval=-bound, maxval=bound)
        ln_k_g = jnp.ones((HEAD_DIM,), jnp.float32)
        ln_k_b = jnp.zeros((HEAD_DIM,), jnp.float32)
        ln_v_g = jnp.ones((HEAD_DIM,), jnp.float32)
        ln_v_b = jnp.zeros((HEAD_DIM,), jnp.float32)
        return {'seq': seq, 'wq': wq, 'wk': wk, 'wv': wv, 'wo': wo, 'bo': bo, 'ln_k_g': ln_k_g, 'ln_k_b': ln_k_b, 'ln_v_g': ln_v_g, 'ln_v_b': ln_v_b}
    _L1_mix_all = _L1_mix_setup()
    _L1_mix_in = {k: v for k, v in _L1_mix_all.items() if k in ('wq', 'wk', 'wv', 'wo', 'bo', 'ln_k_g', 'ln_k_b', 'ln_v_g', 'ln_v_b')}
    del _L1_mix_all

    def _L1_ffn_setup():
        import jax, jax.numpy as jnp
        import numpy as np
        B, N, D = (16, 512, 256)
        NUM_EXPERTS, TOP_K, HEADS = (4, 2, 4)
        N_EDGES = 131072
        LN_EPS = 1e-05

        def _layernorm(x, g, b):
            mu = x.mean(-1, keepdims=True)
            var = ((x - mu) ** 2).mean(-1, keepdims=True)
            return (x - mu) * jax.lax.rsqrt(var + LN_EPS) * g + b

        def _forward(x, edge_index, W_gat, att_src, att_dst, b_gat, ln_gamma, ln_beta, W1, b1, W2, b2):
            Bc, Nc, Dc = x.shape
            M = Bc * Nc
            x_flat = x.reshape(M, Dc)
            h = (x_flat @ W_gat).reshape(M, HEADS, NUM_EXPERTS)
            loops = jnp.arange(M, dtype=edge_index.dtype)
            src = jnp.concatenate([edge_index[0], loops])
            dst = jnp.concatenate([edge_index[1], loops])
            a_src = (h * att_src).sum(-1)
            a_dst = (h * att_dst).sum(-1)
            e = jax.nn.leaky_relu(a_src[src] + a_dst[dst], negative_slope=0.2)
            e_max = jax.ops.segment_max(e, dst, num_segments=M)
            ee = jnp.exp(e - e_max[dst])
            denom = jax.ops.segment_sum(ee, dst, num_segments=M)
            alpha = ee / (denom[dst] + 1e-16)
            msg = h[src] * alpha[:, :, None]
            agg = jax.ops.segment_sum(msg, dst, num_segments=M).reshape(M, HEADS * NUM_EXPERTS) + b_gat
            scores = _layernorm(agg, ln_gamma, ln_beta).reshape(M, HEADS, NUM_EXPERTS).mean(1)
            scores = scores.reshape(Bc, Nc, NUM_EXPERTS)
            topk_s, topk_i = jax.lax.top_k(scores, TOP_K)
            w = jax.nn.softmax(topk_s, axis=-1)
            out = jnp.zeros_like(x)
            for ei in range(NUM_EXPERTS):
                g = jnp.where(topk_i == ei, w, 0.0).sum(-1)
                hh = jax.nn.gelu(x @ W1[ei] + b1[ei], approximate=False)
                out = out + g[..., None] * (hh @ W2[ei] + b2[ei])
            return out
        key = jax.random.key(seed)
        ks = jax.random.split(key, 8)
        s = 0.05
        return {'x': jax.random.normal(ks[0], (B, N, D), jnp.float32), 'W_gat': jax.random.normal(ks[1], (D, HEADS * NUM_EXPERTS), jnp.float32) * s, 'att_src': jax.random.normal(ks[2], (HEADS, NUM_EXPERTS), jnp.float32) * s, 'att_dst': jax.random.normal(ks[3], (HEADS, NUM_EXPERTS), jnp.float32) * s, 'b_gat': jnp.zeros((HEADS * NUM_EXPERTS,), jnp.float32), 'ln_gamma': jnp.ones((HEADS * NUM_EXPERTS,), jnp.float32), 'ln_beta': jnp.zeros((HEADS * NUM_EXPERTS,), jnp.float32), 'W1': jax.random.normal(ks[4], (NUM_EXPERTS, D, 2 * D), jnp.float32) * s, 'b1': jnp.zeros((NUM_EXPERTS, 2 * D), jnp.float32), 'W2': jax.random.normal(ks[5], (NUM_EXPERTS, 2 * D, D), jnp.float32) * s, 'b2': jnp.zeros((NUM_EXPERTS, D), jnp.float32), 'edge_index': jax.random.randint(ks[6], (2, N_EDGES), 0, B * N, jnp.int32)}
    _L1_ffn_all = _L1_ffn_setup()
    _L1_ffn_in = {k: v for k, v in _L1_ffn_all.items() if k in ('W_gat', 'att_src', 'att_dst', 'b_gat', 'ln_gamma', 'ln_beta', 'W1', 'b1', 'W2', 'b2', 'edge_index')}
    del _L1_ffn_all
    return {'x': x, 'src': src, 'dst': dst, 'edge_type_8': edge_type_8, 'edge_weight1': edge_weight1, 'L0_gnn_weight': _L0_gnn_in['weight'], 'L0_gnn_w_comp': _L0_gnn_in['w_comp'], 'L0_gnn_loop_weight': _L0_gnn_in['loop_weight'], 'L0_gnn_h_bias': _L0_gnn_in['h_bias'], 'L0_mix_W_qkv': _L0_mix_in['W_qkv'], 'L0_mix_W_out': _L0_mix_in['W_out'], 'L0_mix_b_out': _L0_mix_in['b_out'], 'L0_ffn_attention_mask': _L0_ffn_in['attention_mask'], 'L0_ffn_wr': _L0_ffn_in['wr'], 'L0_ffn_br': _L0_ffn_in['br'], 'L0_ffn_w1': _L0_ffn_in['w1'], 'L0_ffn_b1': _L0_ffn_in['b1'], 'L0_ffn_w2': _L0_ffn_in['w2'], 'L0_ffn_b2': _L0_ffn_in['b2'], 'L1_gnn_W': _L1_gnn_in['W'], 'L1_mix_wq': _L1_mix_in['wq'], 'L1_mix_wk': _L1_mix_in['wk'], 'L1_mix_wv': _L1_mix_in['wv'], 'L1_mix_wo': _L1_mix_in['wo'], 'L1_mix_bo': _L1_mix_in['bo'], 'L1_mix_ln_k_g': _L1_mix_in['ln_k_g'], 'L1_mix_ln_k_b': _L1_mix_in['ln_k_b'], 'L1_mix_ln_v_g': _L1_mix_in['ln_v_g'], 'L1_mix_ln_v_b': _L1_mix_in['ln_v_b'], 'L1_ffn_W_gat': _L1_ffn_in['W_gat'], 'L1_ffn_att_src': _L1_ffn_in['att_src'], 'L1_ffn_att_dst': _L1_ffn_in['att_dst'], 'L1_ffn_b_gat': _L1_ffn_in['b_gat'], 'L1_ffn_ln_gamma': _L1_ffn_in['ln_gamma'], 'L1_ffn_ln_beta': _L1_ffn_in['ln_beta'], 'L1_ffn_W1': _L1_ffn_in['W1'], 'L1_ffn_b1': _L1_ffn_in['b1'], 'L1_ffn_W2': _L1_ffn_in['W2'], 'L1_ffn_b2': _L1_ffn_in['b2'], 'L1_ffn_edge_index': _L1_ffn_in['edge_index']}

def reference(x, src, dst, edge_type_8, edge_weight1, L0_gnn_weight, L0_gnn_w_comp, L0_gnn_loop_weight, L0_gnn_h_bias, L0_mix_W_qkv, L0_mix_W_out, L0_mix_b_out, L0_ffn_attention_mask, L0_ffn_wr, L0_ffn_br, L0_ffn_w1, L0_ffn_b1, L0_ffn_w2, L0_ffn_b2, L1_gnn_W, L1_mix_wq, L1_mix_wk, L1_mix_wv, L1_mix_wo, L1_mix_bo, L1_mix_ln_k_g, L1_mix_ln_k_b, L1_mix_ln_v_g, L1_mix_ln_v_b, L1_ffn_W_gat, L1_ffn_att_src, L1_ffn_att_dst, L1_ffn_b_gat, L1_ffn_ln_gamma, L1_ffn_ln_beta, L1_ffn_W1, L1_ffn_b1, L1_ffn_W2, L1_ffn_b2, L1_ffn_edge_index):
    import jax
    import jax.numpy as jnp

    def _L0_gnn_ref(feat, weight, w_comp, loop_weight, h_bias, norm, src, dst, etypes):
        import jax, jax.numpy as jnp
        import numpy as np
        N_NODES = 6250
        N_EDGES = 100000
        IN_FEAT = 256
        OUT_FEAT = 256
        NUM_RELS = 8
        NUM_BASES = 4
        W = jnp.einsum('rb,bio->rio', w_comp, weight)
        Hr = jnp.einsum('ni,rio->nro', feat, W)
        msg = Hr[src, etypes] * norm
        agg = jax.ops.segment_sum(msg, dst, num_segments=N_NODES)
        out = agg + feat @ loop_weight + h_bias
        return jax.nn.relu(out)

    def _L0_mix_ref(x, W_qkv, W_out, b_out):
        import jax, jax.numpy as jnp
        import numpy as np
        HEADS = 4
        DIM_HEAD = 32
        B, L, D = x.shape
        scale = DIM_HEAD ** (-0.5)
        qkv = jnp.einsum('bld,df->blf', x, W_qkv)
        qkv = qkv.reshape(B, L, 3, HEADS, DIM_HEAD)
        q = jnp.transpose(qkv[:, :, 0], (0, 2, 1, 3)) * scale
        k = jax.nn.softmax(jnp.transpose(qkv[:, :, 1], (0, 2, 1, 3)), axis=2)
        v = jnp.transpose(qkv[:, :, 2], (0, 2, 1, 3))
        context = jnp.einsum('bhld,bhle->bhde', k, v)
        out = jnp.einsum('bhde,bhld->bhle', context, q)
        out = jnp.transpose(out, (0, 2, 1, 3)).reshape(B, L, HEADS * DIM_HEAD)
        return jnp.einsum('blf,fd->bld', out, W_out) + b_out

    def _L0_ffn_ref(x, attention_mask, wr, br, w1, b1, w2, b2):
        import jax, jax.numpy as jnp
        import numpy as np
        B, S, D = (8, 512, 256)
        H = 4 * D
        CAPACITY = 0.5
        b, s, d = x.shape
        weights = (jnp.einsum('bsd,do->bso', x, wr) + br)[..., 0]
        k = max(1, int(CAPACITY * s))
        kk = k - 1 if k > 1 else 1
        _, idx = jax.lax.top_k(weights, k)
        sel_idx = idx[:, :kk]
        sel = jnp.take_along_axis(x, sel_idx[:, :, None], axis=1)
        h = jax.nn.gelu(jnp.einsum('bkd,dh->bkh', sel, w1) + b1)
        y = jnp.einsum('bkh,hd->bkd', h, w2) + b2
        w_sel = jnp.take_along_axis(weights, sel_idx, axis=1)
        y = y * w_sel[..., None]
        batch_idx = jnp.arange(b)[:, None]
        processed = jnp.zeros_like(x).at[batch_idx, sel_idx].set(y)
        return processed + x

    def _L1_gnn_ref(drug_cell_pair_feature, edge_idx, W):
        import jax, jax.numpy as jnp
        import numpy as np
        N_NODES = 6250
        N_EDGES = 37500
        DIM = 256
        ALPHA = 0.1

        def gcn_layer(x0, x, edge_idx, W):
            src, dst = (edge_idx[0], edge_idx[1])
            msgs = x[src]
            agg = jax.ops.segment_sum(msgs, dst, num_segments=x.shape[0])
            deg = jax.ops.segment_sum(jnp.ones((src.shape[0],), x.dtype), dst, num_segments=x.shape[0])
            agg = agg / jnp.maximum(deg, 1.0)[:, None]
            h = ALPHA * x0 + (1.0 - ALPHA) * agg
            return h @ W
        x0 = drug_cell_pair_feature
        out = jax.nn.relu(gcn_layer(x0, x0, edge_idx, W))
        for _ in range(4):
            out = jax.nn.relu(gcn_layer(x0, out, edge_idx, W))
        return out

    def _L1_mix_ref(seq, wq, wk, wv, wo, bo, ln_k_g, ln_k_b, ln_v_g, ln_v_b):
        import jax, jax.numpy as jnp
        import numpy as np
        import math
        EMBED = 256
        HEADS = 4
        HEAD_DIM = EMBED // HEADS
        OUT_DIM = 256
        LN_EPS = 1e-05

        def _qkv_init(key):
            spread = math.sqrt(3.0 / EMBED)
            gain, delta = (0.01, 0.01)
            w = jax.random.uniform(key, (EMBED, EMBED), minval=-spread, maxval=spread) * gain
            return w + delta * jnp.eye(EMBED, dtype=w.dtype)

        def _layer_norm(x, g, b):
            mu = jnp.mean(x, axis=-1, keepdims=True)
            var = jnp.mean(jnp.square(x - mu), axis=-1, keepdims=True)
            return (x - mu) * jax.lax.rsqrt(var + LN_EPS) * g + b

        def _split_heads(x, B, S):
            return x.reshape(B, S, HEADS, HEAD_DIM).transpose(0, 2, 1, 3)
        B, S, _ = seq.shape
        q = _split_heads(seq @ wq.T, B, S)
        k = _split_heads(seq @ wk.T, B, S)
        v = _split_heads(seq @ wv.T, B, S)
        k = _layer_norm(k, ln_k_g, ln_k_b)
        v = _layer_norm(v, ln_v_g, ln_v_b)
        kv = jnp.einsum('bhsd,bhse->bhde', k, v) / S
        ga = jnp.einsum('bhsd,bhde->bhse', q, kv)
        ga = ga.transpose(0, 2, 1, 3).reshape(B, S, EMBED)
        return ga @ wo.T + bo

    def _L1_ffn_ref(x, W_gat, att_src, att_dst, b_gat, ln_gamma, ln_beta, W1, b1, W2, b2, edge_index):
        import jax, jax.numpy as jnp
        import numpy as np
        B, N, D = (16, 512, 256)
        NUM_EXPERTS, TOP_K, HEADS = (4, 2, 4)
        N_EDGES = 131072
        LN_EPS = 1e-05

        def _layernorm(x, g, b):
            mu = x.mean(-1, keepdims=True)
            var = ((x - mu) ** 2).mean(-1, keepdims=True)
            return (x - mu) * jax.lax.rsqrt(var + LN_EPS) * g + b

        def _forward(x, edge_index, W_gat, att_src, att_dst, b_gat, ln_gamma, ln_beta, W1, b1, W2, b2):
            Bc, Nc, Dc = x.shape
            M = Bc * Nc
            x_flat = x.reshape(M, Dc)
            h = (x_flat @ W_gat).reshape(M, HEADS, NUM_EXPERTS)
            loops = jnp.arange(M, dtype=edge_index.dtype)
            src = jnp.concatenate([edge_index[0], loops])
            dst = jnp.concatenate([edge_index[1], loops])
            a_src = (h * att_src).sum(-1)
            a_dst = (h * att_dst).sum(-1)
            e = jax.nn.leaky_relu(a_src[src] + a_dst[dst], negative_slope=0.2)
            e_max = jax.ops.segment_max(e, dst, num_segments=M)
            ee = jnp.exp(e - e_max[dst])
            denom = jax.ops.segment_sum(ee, dst, num_segments=M)
            alpha = ee / (denom[dst] + 1e-16)
            msg = h[src] * alpha[:, :, None]
            agg = jax.ops.segment_sum(msg, dst, num_segments=M).reshape(M, HEADS * NUM_EXPERTS) + b_gat
            scores = _layernorm(agg, ln_gamma, ln_beta).reshape(M, HEADS, NUM_EXPERTS).mean(1)
            scores = scores.reshape(Bc, Nc, NUM_EXPERTS)
            topk_s, topk_i = jax.lax.top_k(scores, TOP_K)
            w = jax.nn.softmax(topk_s, axis=-1)
            out = jnp.zeros_like(x)
            for ei in range(NUM_EXPERTS):
                g = jnp.where(topk_i == ei, w, 0.0).sum(-1)
                hh = jax.nn.gelu(x @ W1[ei] + b1[ei], approximate=False)
                out = out + g[..., None] * (hh @ W2[ei] + b2[ei])
            return out
        return _forward(x, edge_index, W_gat, att_src, att_dst, b_gat, ln_gamma, ln_beta, W1, b1, W2, b2)
    edge_index = jnp.stack([src, dst])
    xn = _layernorm(x, axis=-1)
    x = x + _L0_gnn_ref(xn, L0_gnn_weight, L0_gnn_w_comp, L0_gnn_loop_weight, L0_gnn_h_bias, edge_weight1, src, dst, edge_type_8) + _L0_mix_ref(xn[None], L0_mix_W_qkv, L0_mix_W_out, L0_mix_b_out)[0]
    x = x + _L0_ffn_ref(_layernorm(x, axis=-1)[None], L0_ffn_attention_mask, L0_ffn_wr, L0_ffn_br, L0_ffn_w1, L0_ffn_b1, L0_ffn_w2, L0_ffn_b2)[0]
    xn = _layernorm(x, axis=-1)
    x = x + _L1_gnn_ref(xn, edge_index, L1_gnn_W) + _L1_mix_ref(xn[None], L1_mix_wq, L1_mix_wk, L1_mix_wv, L1_mix_wo, L1_mix_bo, L1_mix_ln_k_g, L1_mix_ln_k_b, L1_mix_ln_v_g, L1_mix_ln_v_b)[0]
    x = x + _L1_ffn_ref(_layernorm(x, axis=-1)[None], L1_ffn_W_gat, L1_ffn_att_src, L1_ffn_att_dst, L1_ffn_b_gat, L1_ffn_ln_gamma, L1_ffn_ln_beta, L1_ffn_W1, L1_ffn_b1, L1_ffn_W2, L1_ffn_b2, L1_ffn_edge_index)[0]
    return x

_drawn_inputs = setup_inputs


def setup_inputs(seed=0):
    import zlib

    import numpy as np

    out = dict(_drawn_inputs(seed))
    spreads = {'L0_gnn_h_bias': (0.0, 0.273),
     'L0_mix_b_out': (0.0, 0.1),
     'L0_ffn_b1': (0.0, 0.8),
     'L0_ffn_b2': (0.0, 0.8),
     'L1_mix_ln_k_g': (1.0, 0.6),
     'L1_mix_ln_k_b': (0.0, 0.8),
     'L1_mix_ln_v_g': (1.0, 0.6),
     'L1_mix_ln_v_b': (0.0, 0.8),
     'L1_ffn_b_gat': (0.0, 0.8),
     'L1_ffn_ln_gamma': (1.0, 0.6),
     'L1_ffn_ln_beta': (0.0, 1.87),
     'L1_ffn_b1': (0.0, 2.0),
     'L1_ffn_b2': (0.0, 2.0)}
    factors = {'L0_ffn_wr': 6.921,
     'L0_ffn_w1': 8.0,
     'L0_ffn_w2': 7.418,
     'L1_gnn_W': 3.438,
     'L1_mix_wq': 8.0,
     'L1_mix_wk': 8.0,
     'L1_mix_wv': 8.0,
     'L1_mix_wo': 8.0,
     'L1_mix_bo': 29.243,
     'L1_ffn_att_src': 34.16,
     'L1_ffn_att_dst': 60.92,
     'L1_ffn_W_gat': 2.739}
    for name, (base, spread) in spreads.items():
        noise = np.random.default_rng([zlib.crc32(name.encode()), seed]).standard_normal(out[name].shape)
        drawn = base * np.exp(spread * noise) if base else spread * noise
        out[name] = jnp.asarray(drawn.astype(out[name].dtype))
    for name, factor in factors.items():
        out[name] = (out[name] * factor).astype(out[name].dtype)
    return out
```

```python
from contextlib import ExitStack

import concourse.bass as bass
from concourse import mybir

ALU = mybir.AluOpType
ACT = mybir.ActivationFunctionType
F32 = mybir.dt.float32
I32 = mybir.dt.int32
AX = mybir.AxisListType.X

P = 128
D = 256
EPS = 1e-5
ALPHA = 0.1
LAYERS = 5
GRP = 4
RING = 16
SCOL = 8
LOG_P = 7


def build(nc, x, src, dst, etype, norm, w_rel, w_comp, w_loop, h_bias, w_qkv, w_mix0, b_mix0,
          w_r, b_r, w_f1, b_f1, w_f2, b_f2, w_gcn, wq, wk, wv, wo, bo, ln_kg, ln_kb, ln_vg, ln_vb,
          w_gat, att_src, att_dst, b_gat, ln_g, ln_b, w_e1, b_e1, w_e2, b_e2, gat_edges, out):
    N = x.shape[0]
    NT = -(-N // P)
    LAST = N - (NT - 1) * P
    NP = NT * P
    E1 = src.shape[0]
    E2 = gat_edges.shape[1]
    R = w_comp.shape[0]
    NB = w_comp.shape[1]
    HID = w_f1.shape[1]
    HB = HID // P
    NX = w_e1.shape[0]
    XH = w_e1.shape[2]
    XB = XH // P
    HEADS = 4
    C20 = 20
    KEEP = int(0.5 * N) - 1
    J1 = -(-E1 // P)
    J2 = -(-E2 // P)
    T1 = -(-((E1 + NT * (P - 1)) // P) // RING) * RING
    T2 = -(-((E2 + NT * (P - 1)) // P) // RING) * RING
    assert NT % 2 == 1 and E2 == P * J2 and R * D == 2048 and D == 2 * P
    W1R, W2R = 3, 2

    def dram(name, shape, dt=F32):
        return nc.dram_tensor(name, shape, dt, kind="Internal").ap()

    bins1 = dram("bins1", (P * T1 + P * J1, W1R), I32)
    bins2 = dram("bins2", (P * T2 + P * J2, W2R), I32)
    hr = dram("hr", (NP, R * D))
    feat = dram("feat", (NP, D))
    rows20 = dram("rows20", (NP, C20))
    hr_rows = hr.rearrange("n (r o) -> (n r) o", r=R)

    with ExitStack() as ctx:
        def sb(name, shape, dt=F32):
            return ctx.enter_context(nc.sbuf_tensor(name, shape, dt))

        def sem(name):
            return ctx.enter_context(nc.semaphore(name))

        TW = NT * D
        big = sb("big", [P, 3 * TW])
        r_agg, r_xt, r_x = big[:, 0:TW], big[:, TW:2 * TW], big[:, 2 * TW:3 * TW]
        agg = r_agg.rearrange("p (t n) -> p t n", t=NT)
        xt = r_xt.rearrange("p (t h n) -> p t h n", t=NT, h=2)
        y0 = r_xt.rearrange("p (t n) -> p t n", t=NT)
        xs = r_x.rearrange("p (t n) -> p t n", t=NT)

        ring = sb("ring", [P, RING, D])
        sel = sb("sel", [P, RING, P])
        tab1 = sb("tab1", [P, T1 + RING, W1R], I32)
        pay2 = sb("pay2", [P, J2 * (W2R + 1)], I32)
        tab2x = pay2[:, 0:(T2 + RING) * W2R].rearrange("p (t w) -> p t w", w=W2R)
        tab2 = pay2[:, 0:T2 * W2R].rearrange("p (t w) -> p t w", w=W2R)
        hit1 = sb("hit1", [1, T1], I32)
        hit2 = sb("hit2", [1, T2], I32)
        ringf = ring[:, :, :].rearrange("p s n -> p (s n)")
        tabf = tab1[:, :, :].rearrange("p t w -> p (t w)").bitcast(F32)
        idx = sb("idx", [P, RING, 1], I32)
        idx2 = idx[:, :, 0]
        scat = sb("scat", [P, 2, SCOL, 4], I32)
        iota_r = sb("iota_r", [P, P])
        ident = sb("ident", [P, P])
        ones = sb("ones", [P, P])
        before = sb("before", [P, P])
        wl = sb("wl", [P, 2, D])
        wm = sb("wm", [P, 2, D])
        brow = sb("brow", [1, 2, D])
        xn = sb("xn", [P, 2, D])
        st = sb("st", [P, NT, 6])
        mean = sb("mean", [P, NT])
        rstd = sb("rstd", [P, NT])
        sm = sb("sm", [P, 12, 64])
        sm_i = sb("sm_i", [P, 2, 64], I32)
        eps_t = sb("eps_t", [P, 1])
        deg = sb("deg", [P, NT])
        coef = sb("coef", [P, NT])
        mask32 = sb("mask32", [P, P])
        mask64 = sb("mask64", [P, P])
        valid = sb("valid", [P, NT])

        pb = [ctx.enter_context(nc.psum_tensor(f"pb{i}", [P, 512], F32)) for i in range(8)]

        def cut(region, at, shape, dt=F32):
            n = 1
            for s in shape:
                n *= s
            v = region[:, at:at + n]
            if dt is not F32:
                v = v.bitcast(dt)
            if len(shape) == 2:
                v = v.rearrange("p (a b) -> p a b", a=shape[0])
            if len(shape) == 3:
                v = v.rearrange("p (a b c) -> p a b c", a=shape[0], b=shape[1])
            return v

        J = max(J1, J2)
        k_dst, k_hi, k_one, k_mask = (cut(r_xt, i * J, [J], I32 if i == 0 else F32) for i in range(4))
        k_scan, k_rank = (cut(r_xt, i * J, [J]) for i in (4, 5))
        k_ti, k_tj, k_src, k_et, k_nm = (cut(r_xt, i * J, [J], F32 if i == 10 else I32)
                                         for i in (6, 7, 8, 9, 10))
        k_spare = {1: cut(r_x, NB * 2 * D, [J1], I32), 2: cut(r_x, NB * 2 * D + J, [J2], I32)}
        w_all = cut(r_agg, 0, [2, R * D])
        hstage = cut(r_agg, 2 * R * D, [2, R * D])
        pay1 = cut(r_agg, 4 * R * D, [J1 * (W1R + 1)], I32)
        FILL = T1 // 8
        fill1 = cut(r_agg, 4 * R * D + J1 * (W1R + 1), [FILL * W1R], I32)
        FILL2 = T2 // 8
        fill2 = cut(r_agg, 4 * R * D + J1 * (W1R + 1) + FILL * W1R, [FILL2 * W2R], I32)
        w_base = cut(r_x, 0, [NB, 2 * D])
        it_row = cut(ringf, 0, [T2])
        it_ge = cut(ringf, T2, [T2])
        m_qkv = cut(ringf, 0, [2, 3 * P])
        m_out, m_cx, m_nr, m_qT, m_a = (cut(ringf, 768 + 256 * i, [D]) for i in range(5))
        m_ek, m_vv = cut(ringf, 2048, [2, P]), cut(ringf, 2304, [2, P])
        x_t1, x_t2 = cut(ringf, 2560, [D]), cut(ringf, 2816, [D])
        m_max = cut(ringf, 3072, [16])
        f_w1, f_w2 = cut(r_agg, 0, [2, HID]), cut(r_agg, 2 * HID, [HB, D])
        f_ht = cut(r_agg, 4 * HID, [HB, 512])
        f_b1, f_wr, f_br = cut(r_agg, 8 * HID, [HB]), cut(r_agg, 8 * HID + 16, [D]), cut(r_agg, 8 * HID + 272, [1])
        f_tmp, f_w = (cut(r_agg, 8 * HID + 512 + 256 * i, [D]) for i in range(2))
        f_ge, f_gt, f_eq, f_pre = (cut(r_agg, 8 * HID + 1280 + 64 * i, [64]) for i in range(4))
        f_key = cut(r_agg, 8 * HID + 1600, [16], I32)
        f_cnt = cut(r_agg, 8 * HID + 1632, [16])
        g_w = [cut(r_agg, 512 * i, [2, D]) for i in range(4)]
        g_kvw, g_wo = cut(r_agg, 2048, [2, 2 * D]), cut(r_agg, 3072, [2, D])
        g_ln = cut(r_agg, 3584, [4, 64])
        g_kv, g_acc = cut(r_agg, 3840, [2, 2 * D]), cut(r_agg, 4864, [2, P])
        g_a = cut(r_agg, 5120, [2, D])
        g_st = cut(r_agg, 5632, [NT * 8, 6])
        g_m, g_r, g_t1, g_t2, g_t3 = (cut(r_agg, 5632 + NT * 48 + NT * 8 * i, [NT * 8]) for i in range(5))
        g_gam, g_bet = (cut(r_agg, 5632 + NT * 88 + 2 * D * i, [8, 64]) for i in range(2))
        r_ax = big[:, 0:2 * TW]
        a_g = cut(r_ax, 0, [T2, C20])
        a_dd = cut(r_ax, T2 * C20, [2, HEADS, P])
        a_selT = cut(r_ax, T2 * C20 + 1024, [RING, P])
        a_g20 = cut(ringf, 0, [RING, C20])
        a_rows = cut(ringf, 320, [NT, C20])
        a_row = cut(ringf, 1300, [5, 16])
        a_wg = cut(ringf, 1380, [2, 16])
        a_am = cut(ringf, 1412, [NT, 8])
        a_mx = cut(ringf, 1804, [NT, 4])
        a_sum = cut(ringf, 2000, [NT, C20])
        a_msg = cut(ringf, 2980, [RING, C20])
        a_z, a_ee, a_vv = (cut(ringf, 3300 + 64 * i, [RING, 4]) for i in range(3))
        a_min = cut(ringf, 3492, [8])
        a_h16 = cut(ringf, 3500, [16])
        e_w1, e_w2 = cut(r_agg, 0, [NX, 2 * XH]), cut(r_agg, 4096, [NX, XB * D])
        e_ht = cut(r_agg, 8192, [2, XB, 512])
        e_b1 = cut(r_agg, 12288, [NX * XB])
        gates = cut(tabf, 0, [NT, NX])
        e_b2 = tabf[0:1, 256:256 + NX * D].rearrange("p (e n) -> p e n", e=NX)
        s_h, s_a, s_b = (cut(r_agg, NT * 16 * i, [NT, 16]) for i in range(3))
        s_sc, s_d, s_e, s_g = (cut(r_agg, NT * (48 + 4 * i), [NT, 4]) for i in range(4))
        s_v = [cut(r_agg, NT * (64 + i), [NT]) for i in range(6)]

        names = {}

        def S(name):
            if name not in names:
                names[name] = sem(name)
            return names[name]

        def tiles(eng, body):
            body(0, 0, 0, True, False)
            body(1, 0, 1, True, False)
            with eng.Fori(1, NT // 2, 1) as pair:
                body(pair * 2, pair * 2, 0, False, False)
                body(pair * 2 + 1, pair * 2, 1, False, False)
            body(NT - 1, NT - 1, 0, False, True)

        def col(v):
            return bass.ds(v, 1)

        def node(a, t):
            return a[:, t, :] if isinstance(t, int) else a[:, col(t), :].rearrange("p a n -> p (a n)")

        def one(a, t):
            return a[:, t:t + 1] if isinstance(t, int) else a[:, col(t)]

        def xtile(t):
            v = r_xt.rearrange("p (t n) -> p t n", t=NT)
            return node(v, t)

        GRAPHS = {
            1: dict(E=E1, J=J1, T=T1, W=W1R, bins=bins1, pay=pay1, hit=hit1),
            2: dict(E=E2, J=J2, T=T2, W=W2R, bins=bins2, pay=pay2[:, :], hit=hit2),
        }
        halves = [(c, min(512, T1 - c)) for c in range(0, T1, 512)]

        def ln_vector(dve, k, extra=None, store_sem=None):
            v = nc.vector
            with dve.Fori(0, NT, 1) as t:
                v.bn_stats(st[:, col(t), :].rearrange("p a n -> p (a n)"), node(xs, t))
            dve.drain()
            me, m2e, mo, m2o = st[:, :, 1], st[:, :, 2], st[:, :, 4], st[:, :, 5]
            a, b, c = sm[:, 0, 0:NT], sm[:, 1, 0:NT], sm[:, 2, 0:NT]
            v.tensor_tensor(a, me, mo, ALU.add)
            v.tensor_tensor(b, me, mo, ALU.subtract)
            v.tensor_tensor(c, m2e, m2o, ALU.add)
            dve.drain()
            v.tensor_scalar(mean[:, :], a, 0.5, None, ALU.mult)
            v.tensor_tensor(b, b, b, ALU.mult)
            v.tensor_scalar(c, c, 1.0 / D, None, ALU.mult)
            dve.drain()
            v.scalar_tensor_tensor(out=c, in0=b, scalar=0.25, in1=c, op0=ALU.mult, op1=ALU.add)
            dve.drain()
            v.tensor_scalar(c, c, EPS, None, ALU.add)
            rsqrt_vector(dve, "ln", rstd[:, :], c, a, b, k + 1)

            def body(t, te, slot, first, last):
                if not first:
                    dve.wait_ge(S("ln_turned"), t + (k * NT - 1))
                    if store_sem is not None:
                        dve.wait_ge(store_sem[slot], 8 * te)
                v.tensor_scalar(xn[:, slot, :], node(xs, t), one(mean, t), one(rstd, t),
                                ALU.subtract, ALU.mult).then_inc(S("ln_normed"), 1)
                if extra is not None:
                    dve.drain()
                    extra(t, slot)
            tiles(dve, body)
            dve.drain()

        def rsqrt_vector(dve, ph, res, var, t1, t2, n=1):
            v = nc.vector
            v.drain().then_inc(S(ph + "_var"), 1)
            dve.wait_ge(S(ph + "_root"), n)
            v.reciprocal(res, t1)
            dve.drain()
            v.tensor_tensor(t2, res, res, ALU.mult)
            dve.drain()
            v.tensor_tensor(t2, t2, var, ALU.mult)
            dve.drain()
            v.tensor_scalar(t2, t2, -0.5, 1.5, ALU.mult, ALU.add)
            dve.drain()
            v.tensor_tensor(res, res, t2, ALU.mult)
            dve.drain()

        def root_scalar(act, ph, var, t1, n=1):
            act.wait_ge(S(ph + "_var"), n)
            nc.scalar.activation(t1, var, ACT.Sqrt).then_inc(S(ph + "_root"), 1)

        def ln_tensor(pe, k):
            def body(t, te, slot, first, last):
                pe.wait_ge(S("ln_normed"), t + (k * NT + 1))
                if not first:
                    pe.wait_ge(S("ln_xt"), t + (k * NT - 1))
                for h in range(2):
                    mm = nc.tensor.transpose(pb[slot][:, h * P:h * P + P], xn[:, slot, h * P:h * P + P],
                                             ident[:, :])
                mm.then_inc(S("ln_turned"), 1)
            tiles(pe, body)

        def ln_scalar(act, k):
            root_scalar(act, "ln", sm[:, 2, 0:NT], sm[:, 0, 0:NT], k + 1)

            def body(t, te, slot, first, last):
                act.wait_ge(S("ln_turned"), t + (k * NT + 1))
                nc.scalar.copy(xtile(t), pb[slot][:, 0:D]).then_inc(S("ln_xt"), 1)
            tiles(act, body)

        def bin_vector(dve, k):
            v = nc.vector
            q = GRAPHS[k]
            n, T, W = q["J"], q["T"], q["W"]
            pay = q["pay"].rearrange("p (j w) -> p j w", w=W + 1)
            d_i, hi, on, mask = k_dst[:, 0:n], k_hi[:, 0:n], k_one[:, 0:n], k_mask[:, 0:n]
            scan, rank, ti, tj = k_scan[:, 0:n], k_rank[:, 0:n], k_ti[:, 0:n], k_tj[:, 0:n]
            s_i = k_src[:, 0:n]
            v.tensor_scalar(ti, d_i, LOG_P, None, ALU.logical_shift_right)
            v.tensor_scalar(tj, d_i, P - 1, None, ALU.bitwise_and)
            v.memset(on, 1.0)
            v.memset(rank, 0.0)
            dve.drain()
            v.tensor_copy(hi, ti)
            v.tensor_copy(pay[:, :, 2].bitcast(F32), tj)
            if k == 1:
                v.scalar_tensor_tensor(out=pay[:, :, 1], in0=s_i, scalar=float(R), in1=k_et[:, 0:n],
                                       op0=ALU.mult, op1=ALU.add)
                v.tensor_copy(pay[:, :, 3].bitcast(F32), k_nm[:, 0:n])
            else:
                v.tensor_scalar(pay[:, :, 1], s_i, float(N - 1), None, ALU.min)
            dve.drain()
            counts, off, tot = sm[:, 0, :], sm[:, 1, :], sm[:, 2, :]
            ntile, incl, base = sm[:, 3, 0:NT], sm[:, 4, 0:NT], sm[:, 5, 0:NT]
            v.memset(counts, 0.0)
            dve.drain()
            with dve.Fori(0, NT, 1) as h:
                v.tensor_scalar(mask, hi, iota_r[:, col(h)], None, ALU.is_equal)
                dve.drain()
                v.tensor_reduce(counts[:, col(h)], mask, AX, ALU.add)
                dve.drain()
            v.drain().then_inc(S("counts"), 1)
            dve.wait_ge(S("offsets"), k)
            v.tensor_scalar(sm_i[:, 0, 0:NT], pb[1][:, 0:NT], float(P - 1), None, ALU.add)
            dve.drain()
            v.tensor_scalar(sm_i[:, 1, 0:NT], sm_i[:, 0, 0:NT], LOG_P, None, ALU.logical_shift_right)
            dve.drain()
            v.tensor_copy(ntile, sm_i[:, 1, 0:NT])
            dve.drain()
            v.tensor_tensor_scan(incl, ones[:, 0:NT], ntile, 0.0, ALU.mult, ALU.add)
            dve.drain()
            v.tensor_tensor(base, incl, ntile, ALU.subtract)
            dve.drain()
            v.tensor_copy(sm[:, 11, 0:NT], base)
            v.scalar_tensor_tensor(out=off[:, 0:NT], in0=base, scalar=float(P), in1=pb[0][:, 0:NT],
                                   op0=ALU.mult, op1=ALU.add)
            v.drain().then_inc(S("base"), 1)
            with dve.Fori(0, NT, 1) as h:
                v.tensor_scalar(mask, hi, iota_r[:, col(h)], None, ALU.is_equal)
                dve.drain()
                v.tensor_tensor_scan(scan, on, mask, off[:, col(h)], ALU.mult, ALU.add)
                dve.drain()
                v.tensor_tensor(scan, scan, mask, ALU.mult)
                dve.drain()
                v.tensor_tensor(rank, rank, scan, ALU.add)
                dve.drain()
            v.tensor_scalar(ti, rank, -1.0, 0.0, ALU.add, ALU.max)
            v.tensor_scalar(mask, rank, 0.0, None, ALU.is_equal)
            dve.drain()
            v.tensor_scalar(tj, ti, LOG_P, None, ALU.logical_shift_right)
            v.tensor_scalar(s_i, ti, P - 1, None, ALU.bitwise_and)
            dve.drain()
            v.scalar_tensor_tensor(out=scan, in0=s_i, scalar=float(T), in1=tj, op0=ALU.mult, op1=ALU.add)
            dve.drain()
            v.tensor_copy(rank, k_spare[k][:, 0:n])
            dve.drain()
            v.tensor_tensor(rank, rank, scan, ALU.subtract)
            dve.drain()
            v.tensor_tensor(rank, rank, mask, ALU.mult)
            dve.drain()
            v.tensor_tensor(pay[:, :, 0], scan, rank, ALU.add)
            v.drain().then_inc(S(f"binned{k}"), 1)
            dve.wait_ge(S("baseT"), k)
            v.tensor_copy(sm[0:NT, 6, 0:1], pb[2][0:NT, 0:1])
            dve.drain()
            v.tensor_scalar(it_ge[0:NT, 0:T], it_row[0:NT, 0:T], sm[0:NT, 6, 0:1], None, ALU.is_ge)
            v.drain().then_inc(S("atleast"), 1)
            dve.wait_ge(S("hits"), k)
            for i, c in enumerate(range(0, T, 512)):
                w = min(512, T - c)
                v.tensor_scalar(q["hit"][0:1, c:c + w], pb[3 + i][0:1, 0:w], -1.0, None, ALU.add)
            v.drain().then_inc(S(f"hit{k}"), 1)

        def bin_tensor(pe, k):
            T = GRAPHS[k]["T"]
            pe.wait_ge(S("counts"), k)
            nc.tensor.matmul(pb[0][:, 0:64], before[:, :], sm[:, 0, :], start=True, stop=True)
            nc.tensor.matmul(pb[1][:, 0:64], ones[:, :], sm[:, 0, :], start=True,
                             stop=True).then_inc(S("offsets"), 1)
            pe.wait_ge(S("base"), k)
            nc.tensor.transpose(pb[2][0:NT, 0:P], sm[:, 11, 0:NT], ident[:, :]).then_inc(S("baseT"), 1)
            pe.wait_ge(S("atleast"), k)
            for i, c in enumerate(range(0, T, 512)):
                w = min(512, T - c)
                mm = nc.tensor.matmul(pb[3 + i][0:1, 0:w], ones[0:NT, 0:1], it_ge[0:NT, c:c + w],
                                      start=True, stop=True)
            mm.then_inc(S("hits"), 1)

        def scatter_plan(k):
            n = GRAPHS[k]["J"]
            return n, n // (2 * SCOL), n % (2 * SCOL)

        def scatter_scalar(act, k):
            q = GRAPHS[k]
            W = q["W"] + 1
            pay = q["pay"].rearrange("p (j w) -> p j w", w=W)
            n, its, rest = scatter_plan(k)
            act.wait_ge(S(f"binned{k}"), 1)

            def body(it, g, cnt, first):
                if not first:
                    act.wait_ge(S(f"scat{k}_{g}"), it * (16 * SCOL))
                at = it * (2 * SCOL) + g * SCOL
                nc.scalar.copy(scat[:, g, 0:cnt, 0:W], pay[:, bass.ds(at, cnt), :]).then_inc(S(f"staged{k}"), 1)
            body(0, 0, SCOL, True)
            body(0, 1, SCOL, True)
            with act.Fori(1, its, 1) as it:
                body(it, 0, SCOL, False)
                body(it, 1, SCOL, False)
            for g in range(2):
                cnt = min(SCOL, rest - g * SCOL)
                if cnt > 0:
                    body(its, g, cnt, False)

        def scatter_pool(pool, k):
            q = GRAPHS[k]
            W = q["W"]
            n, its, rest = scatter_plan(k)
            pool.wait_ge(S(f"filled{k}"), 16 * 8)

            def body(it, g, cnt):
                pool.wait_ge(S(f"staged{k}"), it * 2 + g + 1)
                pool.nop(nofuse=True)
                for c in range(cnt):
                    nc.gpsimd.indirect_dma_start(
                        q["bins"], bass.IndirectOffsetOnAxis(ap=scat[:, g, c, 0:1], axis=0),
                        scat[:, g, c, 1:1 + W], None).then_inc(S(f"scat{k}_{g}"), 16)
            with pool.Fori(0, its, 1) as it:
                body(it, 0, SCOL)
                body(it, 1, SCOL)
            for g in range(2):
                cnt = min(SCOL, rest - g * SCOL)
                if cnt > 0:
                    body(its, g, cnt)

        def scattered(eng, k):
            n, its, rest = scatter_plan(k)
            for g in range(2):
                total = its * SCOL + min(SCOL, max(0, rest - g * SCOL))
                eng.wait_ge(S(f"scat{k}_{g}"), 16 * total)

        NIT1, NIT2 = T1 // RING, T2 // RING
        NG = RING // GRP

        def gather_pool(pool, ph, nit, table, dst_of, layer=None):
            def body(it):
                for g in range(NG):
                    pool.wait_ge(S(ph + "_idx"), it * NG + (g + 1))
                    pool.nop(nofuse=True)
                    for c in range(GRP):
                        s = g * GRP + c
                        nc.gpsimd.indirect_dma_start(
                            dst_of(s), None, table,
                            bass.IndirectOffsetOnAxis(ap=idx[:, s, :], axis=0)).then_inc(S(f"{ph}_got{g}"), 16)
            return body

        def stage_idx(act, ph, tab, it, g, need):
            act.wait_ge(S(ph + "_used"), need)
            at = it * RING + g * GRP
            nc.scalar.copy(idx2[:, g * GRP:g * GRP + GRP],
                           tab[:, bass.ds(at, GRP), 0]).then_inc(S(ph + "_idx"), 1)

        def build_sel(dve, ph, tab, word, it):
            for g in range(NG):
                for c in range(GRP):
                    s = g * GRP + c
                    lo = tab[:, bass.ds(it * RING + s, 1), word].bitcast(F32)
                    ins = nc.vector.tensor_scalar(sel[:, s, :], iota_r[:, :], lo, None, ALU.is_equal)
                ins.then_inc(S(ph + "_sel"), 1)

        block = ctx.enter_context(nc.Block())

        @block.sync
        def _(sp):
            sp.wait_ge(S("edges_cleared"), 1)
            for d, s in ((k_dst, dst), (k_src, src), (k_et, etype), (k_nm, norm)):
                full = (P - 1) * J1
                sp.dma_start(d[0:P - 1, 0:J1], s[0:full].rearrange("(p j) -> p j", j=J1)).then_inc(S("edges1"), 16)
                sp.dma_start(d[P - 1:P, 0:E1 - full],
                             s[full:E1].rearrange("(p j) -> p j", p=1)).then_inc(S("edges1"), 16)
            sp.wait_ge(S("fills"), 1)
            for i in range(8):
                for k, f, FL in ((1, fill1, FILL), (2, fill2, FILL2)):
                    q = GRAPHS[k]
                    rows = q["bins"][0:P * q["T"], :].rearrange("(p t) w -> p (t w)", p=P)
                    n = FL * q["W"]
                    sp.dma_start(rows[:, i * n:(i + 1) * n], f).then_inc(S(f"filled{k}"), 16)
            for i in range(NB):
                sp.dma_start(w_base[:, i, :].rearrange("p (h o) -> p h o", h=2),
                             w_rel[i].rearrange("(h p) o -> p h o", p=P)).then_inc(S("w_rel"), 16)
            sp.dma_start(sm[:, 10, 0:R * NB], w_comp.rearrange("r b -> (r b)").partition_broadcast(P)).then_inc(S("w_rel"), 16)
            sp.dma_start(wl[:, :, :], w_loop.rearrange("(h p) o -> p h o", p=P)).then_inc(S("w_rel"), 16)
            for i, b in enumerate((h_bias, b_mix0)):
                sp.dma_start(brow[0:1, i, :], b.rearrange("(a o) -> a o", a=1)).then_inc(S("w_rel"), 16)
            sp.wait_ge(S("hit1"), 1)
            sp.dma_start(k_src[:, 0:J2], gat_edges[0].rearrange("(p j) -> p j", p=P)).then_inc(S("edges2"), 16)
            sp.dma_start(k_dst[:, 0:J2], gat_edges[1].rearrange("(p j) -> p j", p=P)).then_inc(S("edges2"), 16)
            sp.wait_ge(S("w_all"), 1)
            sp.dma_start(xs[:, 0:NT - 1, :], x[0:(NT - 1) * P, :].rearrange("(t p) d -> p t d", p=P)).then_inc(S("x"), 16)
            sp.dma_start(xs[0:LAST, NT - 1, :], x[(NT - 1) * P:N, :]).then_inc(S("x"), 16)

            def put_hr(t, te, slot, first, last):
                sp.wait_ge(S("hr_act"), 2 * t + 2)
                sp.wait_ge(S("hr_dve"), 2 * t + 2)
                rows = hr[bass.ds(t * P, P), :]
                sp.dma_start(rows, hstage[:, slot, :]).then_inc(S(f"hr_put{slot}"), 16)
            tiles(sp, put_hr)
            scattered(sp, 1)
            sp.dma_start(tab1[:, 0:T1, :], bins1[0:P * T1, :].rearrange("(p t) w -> p t w", p=P)).then_inc(S("tab1"), 16)
            sp.wait_ge(S("rg_done"), 1)
            sp.dma_start(m_qkv, w_qkv.rearrange("(h p) o -> p h o", p=P)).then_inc(S("w_mix0"), 16)
            sp.dma_start(m_out, w_mix0).then_inc(S("w_mix0"), 16)
            sp.wait_ge(S("x1"), 1)
            sp.dma_start(f_w1, w_f1.rearrange("(h p) o -> p h o", p=P)).then_inc(S("w_ffn"), 16)
            sp.dma_start(f_w2, w_f2.rearrange("(b p) o -> p b o", p=P)).then_inc(S("w_ffn"), 16)
            sp.dma_start(f_b1, b_f1).then_inc(S("w_ffn"), 16)
            sp.dma_start(f_wr, w_r.rearrange("d o -> (d o)").partition_broadcast(P)).then_inc(S("w_ffn"), 16)
            sp.dma_start(f_br, b_r.partition_broadcast(P)).then_inc(S("w_ffn"), 16)
            sp.dma_start(brow[0:1, 0, :], b_f2.rearrange("(a o) -> a o", a=1)).then_inc(S("w_ffn"), 16)
            sp.wait_ge(S("x2"), 1)
            for i, w in enumerate((wk, wv, wo, wq)):
                sp.dma_start(g_w[i], w.rearrange("(h p) o -> p h o", p=P)).then_inc(S("w_mix1"), 16)
            sp.dma_start(wl[:, :, :], w_gcn.rearrange("(h p) o -> p h o", p=P)).then_inc(S("w_mix1"), 16)
            sp.dma_start(brow[0:1, 0, :], bo.rearrange("(a o) -> a o", a=1)).then_inc(S("w_mix1"), 16)
            for i, w in enumerate((ln_kg, ln_kb, ln_vg, ln_vb)):
                sp.dma_start(g_ln[:, i, :], w.partition_broadcast(P)).then_inc(S("w_mix1"), 16)

            def put_feat0(t, te, slot, first, last):
                sp.wait_ge(S("ln_normed"), t + (2 * NT + 1))
                sp.dma_start(feat[bass.ds(t * P, P), :], xn[:, slot, :]).then_inc(S(f"f0_put{slot}"), 16)
            tiles(sp, put_feat0)
            scattered(sp, 2)
            sp.dma_start(tab2, bins2[0:P * T2, :].rearrange("(p t) w -> p t w", p=P)).then_inc(S("tab2"), 16)
            with sp.Fori(0, LAYERS, 1) as layer:
                with sp.Fori(0, NT // 7, 1) as c:
                    sp.wait_ge(S("gc_out"), layer * NT + c * 7 + 7)
                    sp.dma_start(feat[bass.ds(c * (7 * P), 7 * P), :].rearrange("(t p) d -> p t d", p=P),
                                 agg[:, bass.ds(c * 7, 7), :]).then_inc(S("gc_put"), 16)
            sp.wait_ge(S("gc_put"), 16 * LAYERS * (NT // 7))
            sp.dma_start(y0[:, :, :], feat[:, :].rearrange("(t p) d -> p t d", p=P)).then_inc(S("f5"), 16)
            sp.dma_start(a_wg, w_gat.rearrange("(h p) o -> p h o", p=P)).then_inc(S("w_gat"), 16)
            for i, w in enumerate((att_src.rearrange("a b -> (a b)"), att_dst.rearrange("a b -> (a b)"), b_gat, ln_g, ln_b)):
                sp.dma_start(a_row[:, i, :], w.partition_broadcast(P)).then_inc(S("w_gat"), 16)
            sp.wait_ge(S("rows"), 1)
            sp.dma_start(rows20.rearrange("(t p) c -> p t c", p=P), a_rows).then_inc(S("rows_put"), 16)
            sp.wait_ge(S("gates"), 1)
            sp.dma_start(e_b1, b_e1).then_inc(S("w_moe"), 16)
            for e in range(NX):
                sp.dma_start(e_w1[:, e, :].rearrange("p (h o) -> p h o", h=2),
                             w_e1[e].rearrange("(h p) o -> p h o", p=P)).then_inc(S("w_moe"), 16)
                sp.dma_start(e_w2[:, e, :].rearrange("p (b o) -> p b o", b=XB),
                             w_e2[e].rearrange("(b p) o -> p b o", p=P)).then_inc(S("w_moe"), 16)
                sp.dma_start(e_b2[0:1, e, :], b_e2[e].rearrange("(a o) -> a o", a=1)).then_inc(S("w_moe"), 16)
            sp.wait_ge(S("x4"), 1)
            sp.dma_start(out[0:(NT - 1) * P, :].rearrange("(t p) d -> p t d", p=P), xs[:, 0:NT - 1, :]).then_inc(S("out"), 16)
            sp.dma_start(out[(NT - 1) * P:N, :], xs[0:LAST, NT - 1, :]).then_inc(S("out"), 16)
            sp.wait_ge(S("out"), 32)

        @block.gpsimd
        def _(pool):
            g = nc.gpsimd
            g.memset(k_dst[:, 0:J1], NX * 4096)
            g.memset(k_src[:, 0:J1], 0)
            g.memset(k_et[:, 0:J1], 0)
            g.memset(k_nm[:, 0:J1], 0.0)
            pool.drain().then_inc(S("edges_cleared"), 1)
            for f, W in ((fill1, W1R), (fill2, W2R)):
                fv = f.rearrange("p (t w) -> p t w", w=W)
                g.memset(f, 0)
                pool.drain()
                g.memset(fv[:, :, 1].bitcast(F32), -1.0)
            pool.drain().then_inc(S("fills"), 1)
            ii = cut(ringf, 3000, [P], I32)
            g.iota(ii, [[1, P]], base=0, channel_multiplier=0)
            g.iota(it_ge.bitcast(I32), [[1, T2]], base=0, channel_multiplier=0)
            g.iota(k_spare[1], [[1, J1]], base=P * T1, channel_multiplier=J1)
            g.iota(k_spare[2], [[1, J2]], base=P * T2, channel_multiplier=J2)
            g.memset(ident[:, :], 0.0)
            g.memset(xs[:, NT - 1, :], 0.0)
            g.memset(tab1[:, T1:T1 + RING, :], 0)
            g.memset(ones[:, :], 1.0)
            g.memset(before[:, :], 1.0)
            g.memset(mask32[:, :], 1.0)
            g.memset(mask64[:, :], 1.0)
            g.memset(valid[:, :], 1.0)
            g.memset(eps_t[:, :], EPS)
            pool.drain()
            g.tensor_copy(iota_r[:, :], ii)
            g.tensor_copy(it_row, it_ge.bitcast(I32))
            g.affine_select(out=ident[:, :], in_=ident[:, :], compare_op=ALU.not_equal, fill=1.0, base=0,
                            pattern=[[1, P]], channel_multiplier=-1)
            g.affine_select(out=before[:, :], in_=before[:, :], compare_op=ALU.is_gt, fill=0.0, base=0,
                            pattern=[[1, P]], channel_multiplier=-1)
            g.affine_select(out=valid[:, :], in_=valid[:, :], compare_op=ALU.is_ge, fill=0.0, base=N - 1,
                            pattern=[[-P, NT]], channel_multiplier=-1)
            for m, w in ((mask32, 32), (mask64, 64)):
                v = m[:, :].rearrange("p (g c) -> p g c", c=w)
                g.affine_select(out=v, in_=v, compare_op=ALU.is_ge, fill=0.0, base=0,
                                pattern=[[-w, P // w], [0, w]], channel_multiplier=1)
                pool.drain()
                g.affine_select(out=v, in_=v, compare_op=ALU.is_ge, fill=0.0, base=w - 1,
                                pattern=[[w, P // w], [0, w]], channel_multiplier=-1)
            pool.drain().then_inc(S("consts"), 5)
            scatter_pool(pool, 1)

            pool.wait_ge(S("hr_put0"), 16 * ((NT + 1) // 2))
            pool.wait_ge(S("hr_put1"), 16 * (NT // 2))
            body = gather_pool(pool, "rg", NIT1, hr_rows, lambda s: ring[:, s, :])
            with pool.Fori(0, NIT1, 1) as it:
                body(it)
            scatter_pool(pool, 2)

            body = gather_pool(pool, "gc", NIT1, feat, lambda s: ring[:, s, :])
            with pool.Fori(0, LAYERS, 1) as layer:
                with pool.Fori(0, NIT1, 1) as it:
                    body(layer * NIT1 + it)

            pool.wait_ge(S("rows_put"), 16)
            body = gather_pool(pool, "ga", NIT2, rows20, lambda s: a_g20[:, s, :])
            with pool.Fori(0, NIT2, 1) as it:
                body(it)

        def stage_pass(act, ph, evac=None, mms=1, start=None):
            def stage(t, slot):
                nc.scalar.copy(xn[:, slot, :], xtile(t)).then_inc(S("st"), 1)
            if start is not None:
                start()
            stage(0, 0)

            def body(t, te, slot, first, last):
                if not last:
                    if not (isinstance(t, int) and t == 0):
                        act.wait_ge(S(ph + "_mm"), t * mms)
                    stage(t + 1, 1 - slot)
                if evac is not None:
                    evac(t, te, slot, first, last)
            tiles(act, body)

        @block.scalar
        def _(act):
            a = nc.scalar
            act.wait_ge(S("consts"), 5)
            scatter_scalar(act, 1)
            ln_scalar(act, 0)

            def hr_evac(t, te, slot, first, last):
                for c in (0, 2):
                    act.wait_ge(S("hr_mm"), t * 4 + c + 1)
                    if c == 0 and not first:
                        act.wait_ge(S(f"hr_put{slot}"), 8 * te)
                    a.copy(hstage[:, slot, c * 512:c * 512 + 512], pb[4 + c][:, :]).then_inc(S("hr_act"), 1)
            stage_pass(act, "hr", hr_evac, mms=4)

            act.wait_ge(S("tab1"), 16)
            for g in range(NG):
                stage_idx(act, "rg", tab1, 0, g, g + 1)
            with act.Fori(0, NIT1, 1) as it:
                for g in range(NG):
                    act.wait_ge(S(f"rg_got{g}"), it * (16 * GRP) + 16 * GRP)
                    for c in range(GRP):
                        s = g * GRP + c
                        w = tab1[:, bass.ds(it * RING + s, 1), 2].bitcast(F32)
                        ins = a.activation(ring[:, s, :], ring[:, s, :], ACT.Copy, scale=w)
                    ins.then_inc(S("rg_scaled"), 1)
                    if g:
                        stage_idx(act, "rg", tab1, it + 1, g - 1, it * NG + (NG + g))
                stage_idx(act, "rg", tab1, it + 1, NG - 1, it * NG + 2 * NG)

            def m0_evac(t, te, slot, first, last):
                act.wait_ge(S("m0_mm"), t + 1)
                if not first:
                    act.wait_ge(S("m0_cx"), t - 1)
                a.activation(m_ek[:, slot, :], pb[slot][:, 0:P], ACT.Exp)
                a.copy(m_vv[:, slot, :], pb[slot][:, P:D])
                act.drain().then_inc(S("m0_ev"), 1)
            act.wait_ge(S("m0_max"), 1)
            stage_pass(act, "m0", m0_evac)
            act.wait_ge(S("m0_mm"), NT)
            stage_pass(act, "x1")
            scatter_scalar(act, 2)

            ln_scalar(act, 1)
            act.wait_ge(S("w_ffn"), 16 * 6)
            act.sem_inc(S("fh_act"), 4)

            def gelu(c, width):
                for b in range(HB):
                    act.wait_ge(S("fh_mm"), c * HB + b + 1)
                    a.activation(f_ht[:, b, 0:width], pb[b % 4][:, 0:width], ACT.Gelu_apprx_tanh,
                                 bias=f_b1[:, b:b + 1]).then_inc(S("fh_act"), 1)
            with act.Fori(0, NT // 4, 1) as c:
                gelu(c, 512)
            gelu(NT // 4, P)

            ln_scalar(act, 2)
            act.wait_ge(S("f0_put0"), 16 * ((NT + 1) // 2))
            act.wait_ge(S("f0_put1"), 16 * (NT // 2))
            stage_pass(act, "k1")
            root_scalar(act, "kv", g_t3, g_t1)
            act.wait_ge(S("k1_mm"), NT)
            stage_pass(act, "k2")
            act.wait_ge(S("k2_mm"), NT)
            stage_pass(act, "y0")

            with act.Fori(0, LAYERS, 1) as layer:
                act.wait_ge(S("gc_tab"), layer + 1)
                with act.Fori(0, NIT1, 1) as it:
                    for g in range(NG):
                        n = layer * (NIT1 * NG) + it * NG
                        act.wait_ge(S("gc_used"), n + (g + 1))
                        nc.scalar.copy(idx2[:, g * GRP:g * GRP + GRP],
                                       tab1[:, bass.ds(it * RING + g * GRP, GRP), 0]).then_inc(S("gc_idx"), 1)
                act.wait_ge(S("gc_summed"), layer + 1)
                base = layer * NT

                def stage(t, slot):
                    a.copy(xn[:, slot, :], node(agg, t)).then_inc(S("gc_st"), 1)

                def finish(t, te, slot, first, last):
                    if not last:
                        act.wait_ge(S("gc_mm"), base + t + 1)
                        stage(t + 1, 1 - slot)
                    act.wait_ge(S("gc_fin"), base + t + 2 + 1)
                    act.nop(nofuse=True)
                    a.activation(node(agg, t), node(agg, t), ACT.Relu).then_inc(S("gc_out"), 1)
                stage(0, 0)
                tiles(act, finish)

            ln_scalar(act, 3)
            stage_pass(act, "gt")
            act.wait_ge(S("tab2"), 16)
            act.wait_ge(S("rows_put"), 16)
            for g in range(NG):
                a.copy(idx2[:, g * GRP:g * GRP + GRP], tab2[:, g * GRP:g * GRP + GRP, 0]).then_inc(S("ga_idx"), 1)
            act.wait_ge(S("gmin"), 1)
            with act.Fori(0, NIT2, 1) as it:
                for g in range(NG):
                    act.wait_ge(S(f"ga_got{g}"), it * (16 * GRP) + 16 * GRP)
                    a.copy(a_g[:, bass.ds(it * RING + g * GRP, GRP), :], a_g20[:, g * GRP:g * GRP + GRP, :])
                    act.drain().then_inc(S("ga_tg"), 1)
                    a.copy(idx2[:, g * GRP:g * GRP + GRP],
                           tab2x[:, bass.ds(it * RING + (g * GRP + RING), GRP), 0]).then_inc(S("ga_idx"), 1)
                for s in range(RING):
                    if s % GRP == 0:
                        act.wait_ge(S("ga_vv"), it * NG + (s // GRP + 1))
                    act.wait_ge(S("ga_dmm"), it * RING + (s + 1))
                    for h in range(HEADS):
                        ins = a.activation(a_dd[:, s % 2, h, :], ident[:, :], ACT.Copy, scale=a_vv[:, s, h:h + 1])
                    ins.then_inc(S("ga_dd"), 1)
            act.wait_ge(S("self_z"), 1)
            a.activation(a_sum[:, :, 16:20], a_mx, ACT.Exp).then_inc(S("self_e"), 1)
            with act.Fori(0, NIT2, 1) as it:
                for g in range(NG):
                    act.wait_ge(S("gb_tp"), it * NG + (g + 1))
                    a.copy(a_selT[:, g * GRP:g * GRP + GRP, :].rearrange("p s n -> p (s n)"),
                           pb[g % 2][:, :]).then_inc(S("gb_selT"), 1)
                act.wait_ge(S("gb_z"), it + 1)
                a.activation(a_ee, a_z, ACT.Exp).then_inc(S("gb_ee"), 1)
            root_scalar(act, "sc", s_v[1], s_v[2])
            act.wait_ge(S("sc_e"), 1)
            a.activation(s_e, s_d, ACT.Exp).then_inc(S("sc_exp"), 1)
            ln_scalar(act, 4)
            act.wait_ge(S("w_moe"), 16 * (3 * NX + 1))
            act.sem_inc(S("eh_act"), 4)

            def xgelu(c, width):
                for e in range(NX):
                    for b in range(XB):
                        n = e * XB + b
                        act.wait_ge(S("eh_mm"), c * (NX * XB) + n + 1)
                        a.activation(e_ht[:, e % 2, b, 0:width], pb[b][:, 0:width], ACT.Gelu,
                                     bias=e_b1[:, n:n + 1]).then_inc(S("eh_act"), 1)
            with act.Fori(0, NT // 4, 1) as c:
                xgelu(c, 512)
            xgelu(NT // 4, P)

        def mm2(out_, slot, rhs, n, last=True, start=True):
            for h in range(2):
                m = nc.tensor.matmul(out_, xn[:, slot, h * P:h * P + P], rhs(h), start=(h == 0 and start),
                                     stop=(h == 1 and last))
            return m

        @block.tensor
        def _(pe):
            te_ = nc.tensor
            pe.wait_ge(S("consts"), 5)
            bin_tensor(pe, 1)
            bin_tensor(pe, 2)
            ln_tensor(pe, 0)
            pe.wait_ge(S("ln_xt"), 1 * NT)

            def hr_body(t, te, slot, first, last):
                pe.wait_ge(S("st"), t + (0 * NT + 1))
                zero = isinstance(t, int) and t == 0
                for c in range(4):
                    if not zero:
                        pe.wait_ge(S("hr_act" if c % 2 == 0 else "hr_dve"), 2 * t - 1 + c // 2)
                    mm2(pb[4 + c][:, :], slot, lambda h: w_all[:, h, c * 512:c * 512 + 512],
                        512).then_inc(S("hr_mm"), 1)
            tiles(pe, hr_body)

            pe.sem_inc(S("rg_used"), NG)
            with pe.Fori(0, NIT1, 1) as it:
                for g in range(NG):
                    pe.wait_ge(S("rg_sel"), it * NG + (g + 1))
                    pe.wait_ge(S("rg_scaled"), it * NG + (g + 1))
                    pe.wait_ge(S("rg_added"), it * NG + (g + 1))
                    for c in range(GRP):
                        s = g * GRP + c
                        k = s % 8
                        te_.matmul(pb[k // 2][:, (k % 2) * D:(k % 2) * D + D], sel[:, s, :], ring[:, s, :],
                                   start=True, stop=True)
                        m = te_.matmul(pb[4 + g % 2][:, c:c + 1], sel[:, s, :], ones[:, 0:1], start=True, stop=True)
                    m.then_inc(S("rg_used"), 1)
            pe.wait_ge(S("w_mix0"), 32)
            pe.wait_ge(S("rg_done"), 1)
            xtv = xt

            def kt(c, slot, first):
                if not first:
                    pe.wait_ge(S("kt_red"), c - 1)
                for h in range(2):
                    m = te_.matmul(pb[slot][:, :].rearrange("p (t n) -> p t n", t=4), m_qkv[:, h, P:2 * P],
                                   xtv[:, bass.ds(c * 4, 4), h, :], start=(h == 0), stop=(h == 1))
                m.then_inc(S("kt_mm"), 1)
            kt(0, 0, True)
            kt(1, 1, True)
            with pe.Fori(1, NT // 8, 1) as c:
                kt(c * 2, 0, False)
                kt(c * 2 + 1, 1, False)
            pe.wait_ge(S("kt_red"), NT // 4 - 1)
            for h in range(2):
                m = te_.matmul(pb[0][:, 0:LAST], m_qkv[:, h, P:2 * P], xtv[:, NT - 1, h, 0:LAST],
                               start=(h == 0), stop=(h == 1))
            m.then_inc(S("kt_mm"), 1)
            pe.wait_ge(S("m0_neg"), 1)
            te_.matmul(pb[2][0:1, 0:P], m_max[:, 14:15], ident[:, :], start=True, stop=True).then_inc(S("m0_row"), 1)
            pe.wait_ge(S("m0_max"), 1)

            def m0_body(t, te, slot, first, last):
                pe.wait_ge(S("st"), t + (1 * NT + 1))
                if not first:
                    pe.wait_ge(S("m0_ev"), t - 1)
                mm2(pb[slot][:, 0:D], slot, lambda h: m_qkv[:, h, P:3 * P], D, last=False)
                te_.matmul(pb[slot][:, 0:D], ones[0:1, :], m_nr[0:1, :], start=False, stop=True).then_inc(S("m0_mm"), 1)
                pe.wait_ge(S("m0_ev"), t + 1)
                if not first:
                    pe.wait_ge(S("m0_add"), t - 1)
                r = LAST if last else P
                te_.matmul(pb[2 + slot][:, 0:P], m_vv[0:r, slot, :], m_ek[0:r, slot, :], start=True, stop=True)
                te_.matmul(pb[2 + slot][:, P:P + 1], m_ek[0:r, slot, :], ones[0:r, 0:1], start=True,
                           stop=True).then_inc(S("m0_cx"), 1)
            tiles(pe, m0_body)
            pe.wait_ge(S("m0_add"), NT)
            for h in range(2):
                m = te_.transpose(pb[0][:, h * P:h * P + P], m_qkv[:, h, 0:P], ident[:, :])
            pe.wait_ge(S("m0_ctx"), 1)
            te_.matmul(pb[1][:, 0:D], m_cx[:, 0:P], m_out[:, :], start=True, stop=True).then_inc(S("m0_a"), 1)
            pe.wait_ge(S("m0_sc"), 1)
            for h in range(2):
                m = te_.matmul(pb[2 + h][:, 0:D], m_qT[:, h * P:h * P + P], m_a[:, :], start=True, stop=True)
            m.then_inc(S("m0_m"), 1)
            pe.wait_ge(S("wm"), 1)

            def x1_body(t, te, slot, first, last):
                pe.wait_ge(S("st"), t + (2 * NT + 1))
                if not first:
                    pe.wait_ge(S("x1_dve"), t - 1)
                for i, w in enumerate((wl, wm)):
                    mm2(pb[2 * i + slot][:, 0:D], slot, lambda h: w[:, h, :], D, last=False)
                    m = te_.matmul(pb[2 * i + slot][:, 0:D], ones[0:1, :], brow[0:1, i, :], start=False, stop=True)
                m.then_inc(S("x1_mm"), 1)
            tiles(pe, x1_body)

            ln_tensor(pe, 1)
            pe.wait_ge(S("w_ffn"), 16 * 6)
            with pe.Fori(0, 32, 1) as i:
                pe.wait_ge(S("th_cnt"), i + 1)
                te_.matmul(pb[7][:, 0:1], ones[:, :], f_cnt[:, 0:1], start=True, stop=True).then_inc(S("th_mm"), 1)
            pe.wait_ge(S("th_eq"), 1)
            te_.matmul(pb[4][:, 0:NT], ones[:, :], f_gt[:, 0:NT], start=True, stop=True)
            te_.matmul(pb[5][:, 0:NT], before[:, :], f_eq[:, 0:NT], start=True, stop=True)
            te_.matmul(pb[6][:, 0:NT], ones[:, :], f_eq[:, 0:NT], start=True, stop=True).then_inc(S("th_pre"), 1)
            pe.wait_ge(S("coef"), 1)
            pe.wait_ge(S("ln_xt"), 2 * NT)

            def ffn(c, n):
                for b in range(HB):
                    pe.wait_ge(S("fh_act"), c * HB + b + 1)
                    for h in range(2):
                        w = f_w1[:, h, b * P:b * P + P]
                        if n == 4:
                            m = te_.matmul(pb[b % 4][:, :].rearrange("p (t n) -> p t n", t=4), w,
                                           xtv[:, bass.ds(c * 4, 4), h, :], start=(h == 0), stop=(h == 1))
                        else:
                            m = te_.matmul(pb[b % 4][:, 0:P], w, xtv[:, NT - 1, h, :], start=(h == 0), stop=(h == 1))
                    m.then_inc(S("fh_mm"), 1)
                for j in range(n):
                    pe.wait_ge(S("fh_act"), c * HB + HB + 4)
                    pe.wait_ge(S("fo_dve"), c * 4 + j + 1)
                    for b in range(HB):
                        te_.matmul(pb[4 + j][:, 0:D], f_ht[:, b, j * P:j * P + P], f_w2[:, b, :], start=(b == 0), stop=False)
                    te_.matmul(pb[4 + j][:, 0:D], ones[0:1, :], brow[0:1, 0, :], start=False,
                               stop=True).then_inc(S("fo_mm"), 1)
            with pe.Fori(0, NT // 4, 1) as c:
                ffn(c, 4)
            ffn(NT // 4, 1)

            pe.wait_ge(S("x2"), 1)
            ln_tensor(pe, 2)
            pe.wait_ge(S("w_mix1"), 16 * 10)
            pe.wait_ge(S("ln_xt"), 3 * NT)
            for i, w in enumerate(g_w[0:3]):
                for ih in range(2):
                    for oh in range(2):
                        at = (0, D, 0)[i] + oh * P
                        m = te_.transpose(pb[(0, 0, 2)[i] + ih][:, at:at + P],
                                          w[:, oh, ih * P:ih * P + P], ident[:, :])
            m.then_inc(S("g_tr"), 1)
            pe.wait_ge(S("g_w"), 1)

            def kv1(t, te, slot, first, last):
                pe.wait_ge(S("st"), t + (3 * NT + 1))
                if not first:
                    pe.wait_ge(S("k1_dve"), t - 1)
                mm2(pb[slot][:, :], slot, lambda h: g_kvw[:, h, :], 512).then_inc(S("k1_mm"), 1)
            tiles(pe, kv1)

            def kv2(t, te, slot, first, last):
                pe.wait_ge(S("st"), t + (4 * NT + 1))
                if not first:
                    pe.wait_ge(S("k2_kv"), t - 1)
                mm2(pb[slot][:, :], slot, lambda h: g_kvw[:, h, :], 512).then_inc(S("k2_mm"), 1)
                pe.wait_ge(S("k2_kv"), t + 1)
                if not first:
                    pe.wait_ge(S("k2_add"), t - 1)
                r = LAST if last else P
                for h in range(2):
                    m = te_.matmul(pb[2 + slot][:, h * P:h * P + P], g_kv[0:r, slot, D + h * P:D + h * P + P],
                                   g_kv[0:r, slot, h * P:h * P + P], start=True, stop=True)
                m.then_inc(S("k2_cx"), 1)
            pe.wait_ge(S("k1_dve"), NT)
            tiles(pe, kv2)
            pe.wait_ge(S("g_ctx"), 1)
            for h in range(2):
                m = te_.matmul(pb[4 + h][:, 0:D], g_acc[:, h, :], g_wo[:, h, :], start=True, stop=True)
            m.then_inc(S("g_am"), 1)
            pe.wait_ge(S("g_a"), 1)
            for ih in range(2):
                for h in range(2):
                    m = te_.matmul(pb[6 + ih][:, 0:D], g_w[3][:, h, ih * P:ih * P + P], g_a[:, h, :],
                                   start=(h == 0), stop=(h == 1))
            m.then_inc(S("g_m"), 1)
            pe.wait_ge(S("g_wm"), 1)

            def y0_body(t, te, slot, first, last):
                pe.wait_ge(S("st"), t + (5 * NT + 1))
                if not first:
                    pe.wait_ge(S("y0_dve"), t - 1)
                mm2(pb[slot][:, 0:D], slot, lambda h: wm[:, h, :], D, last=False)
                te_.matmul(pb[slot][:, 0:D], ones[0:1, :], brow[0:1, 0, :], start=False, stop=True)
                mm2(pb[2 + slot][:, 0:D], slot, lambda h: wl[:, h, :], D).then_inc(S("y0_mm"), 1)
            tiles(pe, y0_body)

            pe.sem_inc(S("gc_used"), NG)
            pe.sem_inc(S("gc_mm"), 1)
            with pe.Fori(0, LAYERS, 1) as layer:
                with pe.Fori(0, NIT1, 1) as it:
                    for g in range(NG):
                        n = layer * (NIT1 * NG) + it * NG
                        pe.wait_ge(S("gc_sel"), n + (g + 1))
                        pe.wait_ge(S(f"gc_got{g}"), (layer * NIT1 + it) * (16 * GRP) + 16 * GRP)
                        pe.wait_ge(S("gc_added"), n + (g + 1))
                        for c in range(GRP):
                            s = g * GRP + c
                            k = s % 8
                            for h in range(2):
                                m = te_.matmul(pb[k // 2][:, (k % 2) * D + h * P:(k % 2) * D + h * P + P],
                                               ring[:, s, h * P:h * P + P], sel[:, s, :], start=True, stop=True)
                        m.then_inc(S("gc_used"), 1)

                def fin(t, te, slot, first, last):
                    pe.wait_ge(S("gc_st"), layer * NT + t + 1)
                    pe.wait_ge(S("gc_fin"), layer * NT + t + 1)
                    mm2(pb[4 + slot][:, 0:D], slot, lambda h: wl[:, h, :], D).then_inc(S("gc_mm"), 1)
                tiles(pe, fin)

            ln_tensor(pe, 3)
            pe.wait_ge(S("w_gat"), 16 * 6)
            pe.wait_ge(S("ln_xt"), 4 * NT)

            def gt(t, te, slot, first, last):
                pe.wait_ge(S("st"), t + (6 * NT + 1))
                if not first:
                    pe.wait_ge(S("gt_dve"), t - 1)
                mm2(pb[slot][:, 0:16], slot, lambda h: a_wg[:, h, :], 16).then_inc(S("gt_mm"), 1)
            tiles(pe, gt)
            pe.wait_ge(S("gm_a"), 1)
            te_.transpose(pb[2][0:4, 0:P], a_min[:, 0:4], ident[:, :]).then_inc(S("gm_t"), 1)
            pe.wait_ge(S("gm_b"), 1)
            te_.matmul(pb[3][:, 0:4], ones[0:4, :], a_min[0:4, 4:8], start=True, stop=True).then_inc(S("gm_m"), 1)
            pe.sem_inc(S("ga_dmm"), 2)
            with pe.Fori(0, NIT2, 1) as it:
                for s in range(RING):
                    if s % GRP == 0:
                        pe.wait_ge(S("ga_sel"), it * NG + (s // GRP + 1))
                    pe.wait_ge(S("ga_dd"), it * RING + (s + 1))
                    pe.wait_ge(S("ga_red"), it * RING + (s + 1))
                    te_.matmul(pb[4 + s % 4][:, :], sel[:, s, :],
                               a_dd[:, s % 2, :, :].rearrange("p h n -> p (h n)"),
                               start=True, stop=True).then_inc(S("ga_dmm"), 1)
            with pe.Fori(0, NIT2, 1) as it:
                _, hits = nc.values_load_multi_w_load_instructions(
                    hit2[0:1, bass.ds(it * RING, RING)], engines=(mybir.EngineType.PE,), min_val=0, max_val=NT - 1)
                for g in range(NG):
                    pe.wait_ge(S("gb_sel"), it * NG + (g + 1))
                    if g >= 2:
                        pe.wait_ge(S("gb_selT"), it * NG + (g - 1))
                    for c in range(GRP):
                        m = te_.transpose(pb[g % 2][:, c * P:c * P + P], sel[:, g * GRP + c, :], ident[:, :])
                    m.then_inc(S("gb_tp"), 1)
                for s in range(RING):
                    if s % GRP == 0:
                        pe.wait_ge(S("gb_selT"), it * NG + (s // GRP + 1))
                    m = te_.matmul(pb[2][:, s * 8:s * 8 + 8], a_selT[:, s, :], node(a_am, hits[s]), start=True, stop=True)
                m.then_inc(S("gb_eg"), 1)
                pe.wait_ge(S("gb_msg"), it + 1)
                for s in range(RING):
                    m = te_.matmul(pb[3][:, s * C20:(s + 1) * C20], sel[:, s, :], a_msg[:, s, :], start=True, stop=True)
                m.then_inc(S("gb_mm"), 1)

            ln_tensor(pe, 4)
            pe.wait_ge(S("w_moe"), 16 * (3 * NX + 1))
            pe.wait_ge(S("ln_xt"), 5 * NT)

            def moe(c, n):
                def hidden(e):
                    for b in range(XB):
                        pe.wait_ge(S("eh_act"), c * (NX * XB) + e * XB + b + 1)
                        for h in range(2):
                            w = e_w1[:, e, h * XH + b * P:h * XH + b * P + P]
                            if n == 4:
                                m = te_.matmul(pb[b][:, :].rearrange("p (t n) -> p t n", t=4), w,
                                               xtv[:, bass.ds(c * 4, 4), h, :], start=(h == 0), stop=(h == 1))
                            else:
                                m = te_.matmul(pb[b][:, 0:P], w, xtv[:, NT - 1, h, :], start=(h == 0), stop=(h == 1))
                        m.then_inc(S("eh_mm"), 1)

                def output(e):
                    pe.wait_ge(S("eh_act"), c * (NX * XB) + (e + 1) * XB + 4)
                    for j in range(n):
                        pe.wait_ge(S("eo_dve"), c * (4 * NX) + e * n + j + 1 + (4 - n))
                        for b in range(XB):
                            te_.matmul(pb[4 + j][:, 0:D], e_ht[:, e % 2, b, j * P:j * P + P],
                                       e_w2[:, e, b * D:(b + 1) * D], start=(b == 0), stop=False)
                        te_.matmul(pb[4 + j][:, 0:D], ones[0:1, :], e_b2[0:1, e, :], start=False,
                                   stop=True).then_inc(S("eo_mm"), 1)
                for e in range(NX):
                    hidden(e)
                    if e:
                        output(e - 1)
                output(NX - 1)
            with pe.Fori(0, NT // 4, 1) as c:
                moe(c, 4)
            moe(NT // 4, 1)

        def bc(a, shape):
            return a.broadcast_to(shape)

        @block.vector
        def _(dve):
            v = nc.vector
            dve.wait_ge(S("consts"), 5)
            dve.wait_ge(S("edges1"), 16 * 8)
            bin_vector(dve, 1)
            dve.wait_ge(S("edges2"), 32)
            bin_vector(dve, 2)
            dve.wait_ge(S("w_rel"), 16 * (NB + 4))
            w4 = w_all.rearrange("p h (r o) -> p h r o", r=R)
            for b in range(NB):
                for r in range(R):
                    c = sm[:, 10, r * NB + b:r * NB + b + 1]
                    base = w_base[:, b, :].rearrange("p (h o) -> p h o", h=2)
                    if b == 0:
                        v.tensor_scalar(w4[:, :, r, :], base, c, None, ALU.mult)
                    else:
                        v.scalar_tensor_tensor(out=w4[:, :, r, :], in0=base, scalar=c, in1=w4[:, :, r, :],
                                               op0=ALU.mult, op1=ALU.add)
                dve.drain()
            v.drain().then_inc(S("w_all"), 1)
            dve.wait_ge(S("x"), 32)
            ln_vector(dve, 0)

            def hr_evac(t, te, slot, first, last):
                for c in (1, 3):
                    dve.wait_ge(S("hr_mm"), t * 4 + c + 1)
                    if c == 1 and not first:
                        dve.wait_ge(S(f"hr_put{slot}"), 8 * te)
                    v.tensor_copy(hstage[:, slot, c * 512:c * 512 + 512], pb[4 + c][:, :]).then_inc(S("hr_dve"), 1)
            tiles(dve, hr_evac)

            n, its, rest = scatter_plan(1)
            dve.wait_ge(S("staged1"), 2 * its + -(-rest // SCOL))
            dve.wait_ge(S("hr_put0"), 16 * ((NT + 1) // 2))
            dve.wait_ge(S("hr_put1"), 16 * (NT // 2))
            dve.wait_ge(S("filled1"), 16 * 8)
            dve.wait_ge(S("filled2"), 16 * 8)
            v.memset(r_agg, 0.0)
            v.memset(deg[:, :], 0.0)
            dve.wait_ge(S("tab1"), 16)
            dve.drain()
            dve.sem_inc(S("rg_added"), 2)

            def hits_of(hit, it):
                return nc.values_load_multi_w_load_instructions(
                    hit[0:1, bass.ds(it * RING, RING)], engines=(mybir.EngineType.DVE,),
                    min_val=0, max_val=NT - 1)[1]

            with dve.Fori(0, NIT1, 1) as it:
                hits = hits_of(hit1, it)
                build_sel(dve, "rg", tab1, 1, it)
                for g in range(NG):
                    dve.wait_ge(S("rg_used"), it * NG + (g + 1 + NG))
                    for c in range(GRP):
                        s = g * GRP + c
                        k = s % 8
                        o, dg = node(agg, hits[s]), one(deg, hits[s])
                        v.tensor_tensor(o, o, pb[k // 2][:, (k % 2) * D:(k % 2) * D + D], ALU.add)
                        v.tensor_tensor(dg, dg, pb[4 + g % 2][:, c:c + 1], ALU.add)
                        dr = v.drain()
                    dr.then_inc(S("rg_added"), 1)
            v.drain().then_inc(S("rg_done"), 1)

            def red(c, slot):
                dve.wait_ge(S("kt_mm"), c + 1)
                v.tensor_reduce(m_max[:, col(c)] if not isinstance(c, int) else m_max[:, c:c + 1],
                                pb[slot][:, :], AX, ALU.max).then_inc(S("kt_red"), 1)
            with dve.Fori(0, NT // 8, 1) as c:
                red(c * 2, 0)
                red(c * 2 + 1, 1)
            dve.wait_ge(S("kt_mm"), NT // 4 + 1)
            v.tensor_reduce(m_max[:, NT // 4:NT // 4 + 1], pb[0][:, 0:LAST], AX, ALU.max)
            v.memset(m_nr[0:1, :], 0.0)
            v.memset(m_cx, 0.0)
            dve.drain()
            v.tensor_reduce(m_max[:, 13:14], m_max[:, 0:NT // 4 + 1], AX, ALU.max)
            dve.drain()
            v.tensor_scalar(m_max[:, 14:15], m_max[:, 13:14], -1.0, None, ALU.mult).then_inc(S("m0_neg"), 1)
            dve.wait_ge(S("m0_row"), 1)
            v.tensor_copy(m_nr[0:1, 0:P], pb[2][0:1, 0:P]).then_inc(S("m0_max"), 1)

            def m0_add(t, te, slot, first, last):
                dve.wait_ge(S("m0_cx"), t + 1)
                v.tensor_tensor(m_cx[:, 0:P + 1], m_cx[:, 0:P + 1], pb[2 + slot][:, 0:P + 1], ALU.add)
                v.drain().then_inc(S("m0_add"), 1)
            tiles(dve, m0_add)
            v.reciprocal(m_max[:, 15:16], m_cx[:, P:P + 1])
            v.tensor_tensor(m_cx[:, 0:P], m_cx[:, 0:P], mask32[:, :], ALU.mult)
            v.drain().then_inc(S("m0_ctx"), 1)
            dve.wait_ge(S("m0_a"), 1)
            v.tensor_scalar(m_a, pb[1][:, 0:D], m_max[:, 15:16], 32.0 ** -0.5, ALU.mult, ALU.mult)
            v.tensor_copy(m_qT, pb[0][:, 0:D])
            v.drain().then_inc(S("m0_sc"), 1)
            dve.wait_ge(S("m0_m"), 1)
            for h in range(2):
                v.tensor_copy(wm[:, h, :], pb[2 + h][:, 0:D])
            v.drain().then_inc(S("wm"), 1)

            def x1(t, te, slot, first, last):
                dve.wait_ge(S("x1_mm"), t + 1)
                v.tensor_tensor(x_t1, node(agg, t), pb[slot][:, 0:D], ALU.add)
                v.tensor_tensor(x_t2, node(xs, t), pb[2 + slot][:, 0:D], ALU.add)
                v.drain().then_inc(S("x1_dve"), 1)
                v.scalar_tensor_tensor(out=node(xs, t), in0=x_t1, scalar=0.0, in1=x_t2, op0=ALU.max, op1=ALU.add)
                dve.drain()
            tiles(dve, x1)
            v.drain().then_inc(S("x1"), 1)
            v.tensor_scalar(deg[:, :], deg[:, :], 1.0, None, ALU.max)
            v.tensor_scalar(tab1[:, 0:T1, 0], tab1[:, 0:T1, 0], R.bit_length() - 1, None, ALU.logical_shift_right)
            dve.drain()
            v.reciprocal(deg[:, :], deg[:, :])
            dve.drain()
            v.tensor_scalar(deg[:, :], deg[:, :], 1.0 - ALPHA, None, ALU.mult)
            dve.wait_ge(S("w_ffn"), 16 * 6)

            def route(t, slot):
                v.tensor_tensor(f_tmp, xn[:, slot, :], f_wr, ALU.mult)
                v.tensor_tensor(node(xs, t), node(xs, t), xn[:, slot, :], ALU.add)
                dve.drain()
                v.tensor_reduce(one(f_w, t), f_tmp, AX, ALU.add)
                dve.drain()
            ln_vector(dve, 1, extra=route)
            w = f_w[:, 0:NT]
            v.tensor_scalar(w, w, f_br[:, 0:1], None, ALU.add)
            key, cand, bit, t_i, one_i, n_i = (f_key[:, i:i + 1] for i in range(6))
            v.memset(key, 0)
            v.memset(one_i, 1)
            dve.drain()
            v.tensor_scalar(bit, one_i, 31, None, ALU.logical_shift_left)
            v.tensor_tensor(w, w, valid[:, :], ALU.mult)
            v.tensor_scalar(f_pre[:, 0:NT], valid[:, :], -1.0, 3.0e38, ALU.add, ALU.mult)
            dve.drain()
            v.tensor_tensor(w, w, f_pre[:, 0:NT], ALU.add)
            dve.drain()

            def threshold_of(k):
                f = f_cnt[:, 2:3].bitcast(I32)
                v.tensor_scalar(t_i, k, 31, -1, ALU.arith_shift_right, ALU.bitwise_xor)
                v.tensor_scalar(n_i, one_i, 31, None, ALU.logical_shift_left)
                dve.drain()
                v.tensor_tensor(t_i, t_i, n_i, ALU.bitwise_or)
                dve.drain()
                v.tensor_tensor(f, k, t_i, ALU.bitwise_xor)
                dve.drain()

            with dve.Fori(0, 32, 1) as i:
                v.tensor_tensor(cand, key, bit, ALU.bitwise_or)
                dve.drain()
                threshold_of(cand)
                v.tensor_scalar(f_ge[:, 0:NT], w, f_cnt[:, 2:3], None, ALU.is_ge)
                dve.drain()
                v.tensor_reduce(f_cnt[:, 0:1], f_ge[:, 0:NT], AX, ALU.add).then_inc(S("th_cnt"), 1)
                dve.wait_ge(S("th_mm"), i + 1)
                v.tensor_scalar(t_i, pb[7][:, 0:1], float(KEEP), -1.0, ALU.is_ge, ALU.mult)
                dve.drain()
                v.tensor_tensor(t_i, t_i, bit, ALU.bitwise_and)
                dve.drain()
                v.tensor_tensor(key, key, t_i, ALU.bitwise_or)
                v.tensor_scalar(bit, bit, 1, None, ALU.logical_shift_right)
                dve.drain()
            threshold_of(key)
            v.tensor_scalar(f_gt[:, 0:NT], w, f_cnt[:, 2:3], None, ALU.is_gt)
            v.tensor_scalar(f_eq[:, 0:NT], w, f_cnt[:, 2:3], None, ALU.is_equal)
            v.drain().then_inc(S("th_eq"), 1)
            dve.wait_ge(S("th_pre"), 1)
            a, b = sm[:, 0, 0:NT], sm[:, 1, 0:NT]
            v.tensor_reduce(f_cnt[:, 3:4], pb[4][:, 0:NT], AX, ALU.add)
            v.tensor_copy(a, pb[6][:, 0:NT])
            dve.drain()
            v.tensor_scalar(f_cnt[:, 4:5], f_cnt[:, 3:4], -1.0, float(KEEP), ALU.mult, ALU.add)
            v.tensor_tensor_scan(b, ones[:, 0:NT], a, 0.0, ALU.mult, ALU.add)
            dve.drain()
            v.tensor_tensor(b, b, a, ALU.subtract)
            dve.drain()
            v.tensor_tensor(b, b, pb[5][:, 0:NT], ALU.add)
            dve.drain()
            v.tensor_scalar(b, b, f_cnt[:, 4:5], None, ALU.is_lt)
            dve.drain()
            v.tensor_tensor(b, b, f_eq[:, 0:NT], ALU.mult)
            dve.drain()
            v.tensor_tensor(b, b, f_gt[:, 0:NT], ALU.add)
            dve.drain()
            v.tensor_tensor(coef[:, :], b, w, ALU.mult)
            v.drain().then_inc(S("coef"), 1)
            dve.sem_inc(S("fo_dve"), 4)

            def ffn_out(c, n):
                for j in range(n):
                    t = c * 4 + j
                    dve.wait_ge(S("fo_mm"), t + 1)
                    v.scalar_tensor_tensor(out=node(xs, t), in0=pb[4 + j][:, 0:D], scalar=one(coef, t), in1=node(xs, t),
                                           op0=ALU.mult, op1=ALU.add).then_inc(S("fo_dve"), 1)
            with dve.Fori(0, NT // 4, 1) as c:
                ffn_out(c, 4)
            ffn_out(NT // 4, 1)
            v.drain().then_inc(S("x2"), 1)
            ln_vector(dve, 2, store_sem=[S("f0_put0"), S("f0_put1")])

            dve.wait_ge(S("g_tr"), 1)
            for h in range(2):
                v.tensor_copy(g_kvw[:, h, :], pb[h][:, :])
                v.tensor_copy(g_wo[:, h, :], pb[2 + h][:, 0:D])
                for i in range(4):
                    v.tensor_copy(g_gam[:, 4 * h + i, :], g_ln[:, 2 * h, :])
                    v.tensor_copy(g_bet[:, 4 * h + i, :], g_ln[:, 2 * h + 1, :])
            v.memset(g_acc, 0.0)
            v.drain().then_inc(S("g_w"), 1)

            def kv_stats(t, te, slot, first, last):
                dve.wait_ge(S("k1_mm"), t + 1)
                for i in range(8):
                    o = g_st[:, t * 8 + i, :] if isinstance(t, int) else node(g_st, t * 8 + i)
                    ins = v.bn_stats(o, pb[slot][:, i * 64:i * 64 + 64])
                ins.then_inc(S("k1_dve"), 1)
            tiles(dve, kv_stats)
            dve.drain()
            v.tensor_tensor(g_m, g_st[:, :, 1], g_st[:, :, 4], ALU.add)
            v.tensor_tensor(g_t1, g_st[:, :, 1], g_st[:, :, 4], ALU.subtract)
            v.tensor_tensor(g_t3, g_st[:, :, 2], g_st[:, :, 5], ALU.add)
            dve.drain()
            v.tensor_scalar(g_m, g_m, 0.5, None, ALU.mult)
            v.tensor_tensor(g_t1, g_t1, g_t1, ALU.mult)
            v.tensor_scalar(g_t3, g_t3, 1.0 / 64, EPS, ALU.mult, ALU.add)
            dve.drain()
            v.scalar_tensor_tensor(out=g_t3, in0=g_t1, scalar=0.25, in1=g_t3, op0=ALU.mult, op1=ALU.add)
            dve.drain()
            rsqrt_vector(dve, "kv", g_r, g_t3, g_t1, g_t2)

            def kv_norm(t, te, slot, first, last):
                dve.wait_ge(S("k2_mm"), t + 1)
                if not first:
                    dve.wait_ge(S("k2_cx"), t - 1)
                o = g_kv[:, slot, :].rearrange("p (g n) -> p g n", g=8)
                sh = [P, 8, 64]
                m = g_m[:, bass.ds(t * 8, 8)].unsqueeze(2)
                r = g_r[:, bass.ds(t * 8, 8)].unsqueeze(2)
                v.tensor_tensor(o, pb[slot][:, :].rearrange("p (g n) -> p g n", g=8), bc(m, sh), ALU.subtract)
                dve.drain()
                v.tensor_tensor(o, o, bc(r, sh), ALU.mult)
                dve.drain()
                v.tensor_tensor(o, o, g_gam, ALU.mult)
                dve.drain()
                v.tensor_tensor(o, o, g_bet, ALU.add).then_inc(S("k2_kv"), 1)
                dve.wait_ge(S("k2_cx"), t + 1)
                acc = g_acc.rearrange("p h n -> p (h n)")
                v.tensor_tensor(acc, acc, pb[2 + slot][:, 0:D], ALU.add)
                v.drain().then_inc(S("k2_add"), 1)
            tiles(dve, kv_norm)
            for h in range(2):
                v.scalar_tensor_tensor(out=g_acc[:, h, :], in0=g_acc[:, h, :], scalar=1.0 / N, in1=mask64[:, :],
                                       op0=ALU.mult, op1=ALU.mult)
            v.drain().then_inc(S("g_ctx"), 1)
            dve.wait_ge(S("g_am"), 1)
            for h in range(2):
                v.tensor_copy(g_a[:, h, :], pb[4 + h][:, 0:D])
            v.drain().then_inc(S("g_a"), 1)
            dve.wait_ge(S("g_m"), 1)
            for h in range(2):
                v.tensor_copy(wm[:, h, :], pb[6 + h][:, 0:D])
            v.drain().then_inc(S("g_wm"), 1)

            def y0_part(t, te, slot, first, last):
                dve.wait_ge(S("y0_mm"), t + 1)
                v.tensor_tensor(node(xs, t), node(xs, t), pb[slot][:, 0:D], ALU.add)
                v.tensor_scalar(node(y0, t), pb[2 + slot][:, 0:D], ALPHA, None, ALU.mult)
                v.drain().then_inc(S("y0_dve"), 1)
            tiles(dve, y0_part)
            v.memset(r_agg, 0.0)
            v.drain().then_inc(S("gc_tab"), 1)
            dve.sem_inc(S("gc_added"), 2)
            dve.sem_inc(S("gc_fin"), 2)

            with dve.Fori(0, LAYERS, 1) as layer:
                with dve.Fori(0, NIT1, 1) as it:
                    n = layer * (NIT1 * NG) + it * NG
                    hits = hits_of(hit1, it)
                    build_sel(dve, "gc", tab1, 1, it)
                    for g in range(NG):
                        dve.wait_ge(S("gc_used"), n + (g + 1 + NG))
                        for c in range(GRP):
                            s = g * GRP + c
                            k = s % 8
                            o = node(agg, hits[s])
                            v.tensor_tensor(o, o, pb[k // 2][:, (k % 2) * D:(k % 2) * D + D], ALU.add)
                            dr = v.drain()
                        dr.then_inc(S("gc_added"), 1)
                v.drain().then_inc(S("gc_summed"), 1)

                def fin(t, te, slot, first, last):
                    dve.wait_ge(S("gc_mm"), layer * NT + t + 1 + 1)
                    v.scalar_tensor_tensor(out=node(agg, t), in0=pb[4 + slot][:, 0:D], scalar=one(deg, t),
                                           in1=node(y0, t), op0=ALU.mult, op1=ALU.add).then_inc(S("gc_fin"), 1)
                tiles(dve, fin)
                dve.wait_ge(S("gc_put"), layer * (16 * (NT // 7)) + 16 * (NT // 7))
                v.memset(r_agg, 0.0)
                v.drain().then_inc(S("gc_tab"), 1)

            dve.wait_ge(S("f5"), 16)
            v.tensor_tensor(r_x, r_x, r_xt, ALU.add)
            dve.drain()
            ln_vector(dve, 3)

            dve.wait_ge(S("w_gat"), 16 * 6)

            def gt(t, te, slot, first, last):
                dve.wait_ge(S("gt_mm"), t + 1)
                o = a_rows[:, t, 0:16] if isinstance(t, int) else a_rows[:, col(t), 0:16].rearrange("p a n -> p (a n)")
                v.tensor_copy(o, pb[slot][:, 0:16]).then_inc(S("gt_dve"), 1)
            tiles(dve, gt)
            dve.drain()
            sh3, sh4 = [P, NT, 16], [P, NT, HEADS]
            tmp = a_sum[:, :, 0:16]
            tmp4 = tmp.rearrange("p t (h e) -> p t h e", h=HEADS)
            for i, o in ((0, a_rows[:, :, 16:20]), (1, a_am[:, :, 0:4])):
                v.tensor_tensor(tmp, a_rows[:, :, 0:16], bc(a_row[:, i, :].unsqueeze(1), sh3), ALU.mult)
                dve.drain()
                v.tensor_reduce(o, tmp4, AX, ALU.add)
                dve.drain()
            v.drain().then_inc(S("rows"), 1)
            v.tensor_reduce(a_min[:, 0:4], a_rows[:, :, 16:20].rearrange("p t h -> p h t"), AX, ALU.min)
            v.drain().then_inc(S("gm_a"), 1)
            dve.wait_ge(S("gm_t"), 1)
            v.tensor_reduce(a_h16[0:4, 0:1], pb[2][0:4, 0:P], AX, ALU.min)
            dve.drain()
            v.tensor_scalar(a_min[0:4, 4:8], ident[0:4, 0:4], a_h16[0:4, 0:1], None, ALU.mult)
            v.drain().then_inc(S("gm_b"), 1)
            dve.wait_ge(S("gm_m"), 1)
            v.tensor_copy(a_min[:, 0:4], pb[3][:, 0:4])
            dve.drain()
            gm = a_min[:, 0:4].unsqueeze(1)
            v.tensor_tensor(a_mx, a_rows[:, :, 16:20], bc(gm, sh4), ALU.subtract)
            v.drain().then_inc(S("gmin"), 1)
            dve.sem_inc(S("ga_red"), 4)
            with dve.Fori(0, NIT2, 1) as it:
                hits = hits_of(hit2, it)
                for g in range(NG):
                    dve.wait_ge(S("ga_tg"), it * NG + (g + 1))
                    v.tensor_tensor(a_vv[:, g * GRP:g * GRP + GRP, :], a_g[:, bass.ds(it * RING + g * GRP, GRP), 16:20],
                                    bc(gm, [P, GRP, 4]), ALU.subtract).then_inc(S("ga_vv"), 1)
                build_sel(dve, "ga", tab2, 1, it)
                for s in range(RING):
                    dve.wait_ge(S("ga_dmm"), it * RING + (s + 1 + 2))
                    v.tensor_reduce(a_z[:, s, :], pb[4 + s % 4][:, :].rearrange("p (h n) -> p h n", h=HEADS), AX,
                                    ALU.max).then_inc(S("ga_red"), 1)
                    dve.drain()
                    o = node(a_mx, hits[s])
                    v.tensor_tensor(o, o, a_z[:, s, :], ALU.max)
            dve.drain()
            v.tensor_tensor(a_mx, a_mx, bc(gm, sh4), ALU.add)
            dve.drain()
            v.tensor_tensor(a_mx, a_mx, a_am[:, :, 0:4], ALU.add)
            dve.drain()
            v.scalar_tensor_tensor(out=a_am[:, :, 4:8], in0=a_mx, scalar=0.2, in1=a_mx, op0=ALU.mult, op1=ALU.max)
            dve.drain()
            v.tensor_tensor(a_mx, a_rows[:, :, 16:20], a_am[:, :, 0:4], ALU.add)
            dve.drain()
            v.scalar_tensor_tensor(out=a_mx, in0=a_mx, scalar=0.2, in1=a_mx, op0=ALU.mult, op1=ALU.max)
            dve.drain()
            v.tensor_tensor(a_mx, a_mx, a_am[:, :, 4:8], ALU.subtract)
            v.drain().then_inc(S("self_z"), 1)
            dve.wait_ge(S("self_e"), 1)
            sh_e = [P, NT, HEADS, 4]
            v.tensor_tensor(tmp4, a_rows[:, :, 0:16].rearrange("p t (h e) -> p t h e", h=HEADS),
                            bc(a_sum[:, :, 16:20].unsqueeze(3), sh_e), ALU.mult)
            dve.drain()
            eg = pb[2][:, 0:RING * 8].rearrange("p (s n) -> p s n", n=8)
            with dve.Fori(0, NIT2, 1) as it:
                hits = hits_of(hit2, it)
                build_sel(dve, "gb", tab2, 1, it)
                dve.wait_ge(S("gb_eg"), it + 1)
                gt_ = a_g[:, bass.ds(it * RING, RING), :]
                v.tensor_tensor(a_z, gt_[:, :, 16:20], eg[:, :, 0:4], ALU.add)
                dve.drain()
                v.scalar_tensor_tensor(out=a_z, in0=a_z, scalar=0.2, in1=a_z, op0=ALU.mult, op1=ALU.max)
                dve.drain()
                v.tensor_tensor(a_z, a_z, eg[:, :, 4:8], ALU.subtract)
                v.drain().then_inc(S("gb_z"), 1)
                dve.wait_ge(S("gb_ee"), it + 1)
                v.tensor_copy(a_msg[:, :, 16:20], a_ee)
                v.tensor_tensor(a_msg[:, :, 0:16].rearrange("p s (h e) -> p s h e", h=HEADS),
                                gt_[:, :, 0:16].rearrange("p s (h e) -> p s h e", h=HEADS),
                                bc(a_ee.unsqueeze(3), [P, RING, HEADS, 4]), ALU.mult)
                v.drain().then_inc(S("gb_msg"), 1)
                dve.wait_ge(S("gb_mm"), it + 1)
                for s in range(RING):
                    o = node(a_sum, hits[s])
                    v.tensor_tensor(o, o, pb[3][:, s * C20:(s + 1) * C20], ALU.add)
                    dve.drain()

            v.tensor_scalar(s_d, a_sum[:, :, 16:20], 1e-16, None, ALU.add)
            dve.drain()
            v.reciprocal(s_e, s_d)
            dve.drain()
            h4 = s_h.rearrange("p t (h e) -> p t h e", h=HEADS)
            v.tensor_tensor(h4, tmp4, bc(s_e.unsqueeze(3), sh_e), ALU.mult)
            dve.drain()
            v.tensor_tensor(s_h, s_h, bc(a_row[:, 2, :].unsqueeze(1), sh3), ALU.add)
            dve.drain()
            v.tensor_reduce(s_v[0], s_h, AX, ALU.add)
            dve.drain()
            v.tensor_scalar(s_v[0], s_v[0], 1.0 / 16, None, ALU.mult)
            dve.drain()
            v.tensor_tensor(s_a, s_h, bc(s_v[0].unsqueeze(2), sh3), ALU.subtract)
            dve.drain()
            v.tensor_tensor(s_b, s_a, s_a, ALU.mult)
            dve.drain()
            v.tensor_reduce(s_v[1], s_b, AX, ALU.add)
            dve.drain()
            v.tensor_scalar(s_v[1], s_v[1], 1.0 / 16, EPS, ALU.mult, ALU.add)
            dve.drain()
            rsqrt_vector(dve, "sc", s_v[0], s_v[1], s_v[2], s_v[3])
            v.tensor_tensor(s_a, s_a, bc(s_v[0].unsqueeze(2), sh3), ALU.mult)
            dve.drain()
            v.tensor_tensor(s_a, s_a, bc(a_row[:, 3, :].unsqueeze(1), sh3), ALU.mult)
            dve.drain()
            v.tensor_tensor(s_a, s_a, bc(a_row[:, 4, :].unsqueeze(1), sh3), ALU.add)
            dve.drain()
            v.tensor_reduce(s_sc, s_a.rearrange("p t (h e) -> p t e h", h=HEADS), AX, ALU.add)
            dve.drain()
            v.tensor_scalar(s_sc, s_sc, 1.0 / HEADS, None, ALU.mult)
            v.memset(s_g, 0.0)
            dve.drain()
            for e in range(NX):
                for f in range(NX):
                    if f != e:
                        v.tensor_tensor(s_v[4], s_sc[:, :, f], s_sc[:, :, e], ALU.is_ge if f < e else ALU.is_gt)
                        dve.drain()
                        v.tensor_tensor(s_g[:, :, e], s_g[:, :, e], s_v[4], ALU.add)
                        dve.drain()
            v.tensor_reduce(s_v[5], s_sc, AX, ALU.max)
            v.tensor_scalar(s_g, s_g, 2.0, None, ALU.is_lt)
            dve.drain()
            v.tensor_tensor(s_d, s_sc, bc(s_v[5].unsqueeze(2), [P, NT, NX]), ALU.subtract)
            v.drain().then_inc(S("sc_e"), 1)
            dve.wait_ge(S("sc_exp"), 1)
            v.tensor_tensor(s_e, s_e, s_g, ALU.mult)
            dve.drain()
            v.tensor_reduce(s_v[4], s_e, AX, ALU.add)
            dve.drain()
            v.reciprocal(s_v[5], s_v[4])
            dve.drain()
            v.tensor_tensor(gates, s_e, bc(s_v[5].unsqueeze(2), [P, NT, NX]), ALU.mult)
            v.drain().then_inc(S("gates"), 1)
            ln_vector(dve, 4)
            dve.sem_inc(S("eo_dve"), 4)

            def moe_out(c, n):
                for e in range(NX):
                    for j in range(n):
                        t = c * 4 + j
                        dve.wait_ge(S("eo_mm"), c * (4 * NX) + e * n + j + 1)
                        gv = gates[:, t, e:e + 1] if isinstance(t, int) else \
                            gates[:, col(t), e:e + 1].rearrange("p a n -> p (a n)")
                        v.scalar_tensor_tensor(out=node(xs, t), in0=pb[4 + j][:, 0:D], scalar=gv, in1=node(xs, t),
                                               op0=ALU.mult, op1=ALU.add)
                        v.drain().then_inc(S("eo_dve"), 1)
            with dve.Fori(0, NT // 4, 1) as c:
                moe_out(c, 4)
            moe_out(NT // 4, 1)
            v.drain().then_inc(S("x4"), 1)


_INS = ['x', 'src', 'dst', 'edge_type_8', 'edge_weight1', 'L0_gnn_weight', 'L0_gnn_w_comp', 'L0_gnn_loop_weight',
        'L0_gnn_h_bias', 'L0_mix_W_qkv', 'L0_mix_W_out', 'L0_mix_b_out', 'L0_ffn_wr', 'L0_ffn_br', 'L0_ffn_w1',
        'L0_ffn_b1', 'L0_ffn_w2', 'L0_ffn_b2', 'L1_gnn_W', 'L1_mix_wq', 'L1_mix_wk', 'L1_mix_wv', 'L1_mix_wo',
        'L1_mix_bo', 'L1_mix_ln_k_g', 'L1_mix_ln_k_b', 'L1_mix_ln_v_g', 'L1_mix_ln_v_b', 'L1_ffn_W_gat',
        'L1_ffn_att_src', 'L1_ffn_att_dst', 'L1_ffn_b_gat', 'L1_ffn_ln_gamma', 'L1_ffn_ln_beta', 'L1_ffn_W1',
        'L1_ffn_b1', 'L1_ffn_W2', 'L1_ffn_b2', 'L1_ffn_edge_index']


def kernel(**inputs):
    import numpy as _np
    import concourse.bacc as _bacc
    from concourse import mybir as _mybir
    from concourse.bass_utils import run_bass_kernel_spmd as _run

    nc = _bacc.Bacc("TRN2", target_bir_lowering=False, num_devices=1, dynamic_dma_scratch_size=4096)
    arrays, args = {}, []
    for name in _INS:
        a = _np.ascontiguousarray(inputs[name])
        if name == 'edge_weight1':
            a = a.reshape(-1)
        if name in ('L0_ffn_b1', 'L1_ffn_b1'):
            a = _np.ascontiguousarray(a.reshape(-1, 128).T)
        arrays[f"in_{name}_dram"] = a
        args.append(nc.dram_tensor(f"in_{name}_dram", a.shape, _mybir.dt.from_np(a.dtype), kind="ExternalInput").ap())
    o = nc.dram_tensor("out_0_dram", inputs['x'].shape, _mybir.dt.float32, kind="ExternalOutput").ap()
    build(nc, *args, o)
    r = _run(nc, [arrays], core_ids=[0])
    return r.results[0]["out_0_dram"]
```

```python
from contextlib import ExitStack

import concourse.bass as bass
from concourse import mybir

ALU = mybir.AluOpType
ACT = mybir.ActivationFunctionType
F32 = mybir.dt.float32
I32 = mybir.dt.int32
BF16 = mybir.dt.bfloat16
AX = mybir.AxisListType.X

P = 128
D = 256
EPS = 1e-5
ALPHA = 0.1
LAYERS = 5
GRP = 4
RING = 16
SCOL = 32
LOG_P = 7
FAR = 2.0 ** 96


def build(nc, x, src, dst, etype, norm, w_rel, w_comp, w_loop, h_bias, w_qkv, w_mix0, b_mix0,
          w_r, b_r, w_f1, b_f1, w_f2, b_f2, w_gcn, wq, wk, wv, wo, bo, ln_kg, ln_kb, ln_vg, ln_vb,
          w_gat, att_src, att_dst, b_gat, ln_g, ln_b, w_e1, b_e1, w_e2, b_e2, gat_edges, out):
    N = x.shape[0]
    NT = -(-N // P)
    LAST = N - (NT - 1) * P
    NP = NT * P
    E1 = src.shape[0]
    E2 = gat_edges.shape[1]
    R = w_comp.shape[0]
    NB = w_comp.shape[1]
    HID = w_f1.shape[1]
    HB = HID // P
    NX = w_e1.shape[0]
    XH = w_e1.shape[2]
    XB = XH // P
    HEADS = 4
    C20 = 20
    KEEP = int(0.5 * N) - 1
    J1 = -(-E1 // P)
    J2 = -(-E2 // P)
    T1 = -(-2 * ((E1 + NT * (2 * P - 1)) // (2 * P)) // RING) * RING
    T2 = -(-2 * ((E2 + NT * (2 * P - 1)) // (2 * P)) // RING) * RING
    assert NT % 2 == 1 and NT % 7 == 0 and T2 % (2 * RING) == 0 and E2 == P * J2 and R * D == 2048 and D == 2 * P
    W1R, W2R = 3, 2

    def dram(name, shape, dt=F32):
        return nc.dram_tensor(name, shape, dt, kind="Internal").ap()

    bins1 = dram("bins1", (P * T1 + P * J1, W1R), I32)
    bins2 = dram("bins2", (P * T2 + P * J2, W2R), I32)
    hr = dram("hr", (NP, R * D))
    feat = dram("feat", (NP, D))
    rows20 = dram("rows20", (NP, C20))
    hr_rows = hr.rearrange("n (r o) -> (n r) o", r=R)

    with ExitStack() as ctx:
        def sb(name, shape, dt=F32):
            return ctx.enter_context(nc.sbuf_tensor(name, shape, dt))

        def sem(name):
            return ctx.enter_context(nc.semaphore(name))

        TW = NT * D
        big = sb("big", [P, 3 * TW])
        r_agg, r_xt, r_x = big[:, 0:TW], big[:, TW:2 * TW], big[:, 2 * TW:3 * TW]
        agg = r_agg.rearrange("p (t n) -> p t n", t=NT)
        xt = r_xt.rearrange("p (t h n) -> p t h n", t=NT, h=2)
        y0 = r_xt.rearrange("p (t n) -> p t n", t=NT)
        xs = r_x.rearrange("p (t n) -> p t n", t=NT)

        ring = sb("ring", [P, RING, D + 1])
        sel = sb("sel", [P, RING, P])
        tab1 = sb("tab1", [P, T1 + RING, W1R], I32)
        pay2 = sb("pay2", [P, J2 * (W2R + 1)], I32)
        tab2x = pay2[:, 0:(T2 + RING) * W2R].rearrange("p (t w) -> p t w", w=W2R)
        tab2 = pay2[:, 0:T2 * W2R].rearrange("p (t w) -> p t w", w=W2R)
        hit1 = sb("hit1", [1, T1 // 2], I32)
        hit2 = sb("hit2", [1, T2 // 2], I32)
        ringf = ring[:, :, :].rearrange("p s n -> p (s n)")
        tabf = tab1[:, :, :].rearrange("p t w -> p (t w)").bitcast(F32)
        idx = sb("idx", [P, RING, 1], I32)
        idx2 = idx[:, :, 0]
        scat = sb("scat", [P, 2, SCOL, 4], I32)
        iota_r = sb("iota_r", [P, P])
        ident = sb("ident", [P, P])
        ones = sb("ones", [P, P])
        before = sb("before", [P, P])
        wl = sb("wl", [P, 2, D])
        wm = sb("wm", [P, 2, D])
        brow = sb("brow", [3, 2, D])
        xn = sb("xn", [P, 2, D])
        st = sb("st", [P, NT, 6])
        mean = sb("mean", [P, NT])
        rstd = sb("rstd", [P, NT])
        sm = sb("sm", [P, 12, 64])
        sm_i = sb("sm_i", [P, 2, 64], I32)
        eps_t = sb("eps_t", [P, 1])
        deg = sb("deg", [P, NT])
        coef = sb("coef", [P, NT])
        mask32 = sb("mask32", [P, P])
        mask64 = sb("mask64", [P, P])
        valid = sb("valid", [P, NT])

        pb = [ctx.enter_context(nc.psum_tensor(f"pb{i}", [P, 512], F32)) for i in range(8)]

        def cut(region, at, shape, dt=F32):
            n = 1
            for s in shape:
                n *= s
            v = region[:, at:at + (n if dt is not BF16 else n // 2)]
            if dt is not F32:
                v = v.bitcast(dt)
            if len(shape) == 2:
                v = v.rearrange("p (a b) -> p a b", a=shape[0])
            if len(shape) == 3:
                v = v.rearrange("p (a b c) -> p a b c", a=shape[0], b=shape[1])
            return v

        k_arr = {1: [cut(r_xt, i * J1, [J1]) for i in range(9)]}
        k_arr[2] = [cut(r, at, [J2]) for r in (ringf, sel[:, :, :].rearrange("p s n -> p (s n)"), tabf)
                    for at in (0, J2)]
        k_dst, k_src, k_et, k_nm = ({k: k_arr[k][i].bitcast(dt) for k in k_arr if i < len(k_arr[k]) and (i < 6 or k == 1)}
                                    for i, dt in ((0, I32), (4, I32), (6, I32), (7, F32)))
        k_spare = {1: k_arr[1][5].bitcast(I32), 2: k_arr[2][5].bitcast(I32)}
        w_all = cut(r_agg, 0, [2, R * D])
        hstage = cut(r_agg, 2 * R * D, [2, R * D])
        pay1 = cut(r_agg, 4 * R * D, [J1 * (W1R + 1)], I32)
        FILL = T1 // 8
        fill1 = cut(r_agg, 4 * R * D + J1 * (W1R + 1), [FILL * W1R], I32)
        FILL2 = T2 // 8
        fill2 = cut(r_agg, 4 * R * D + J1 * (W1R + 1) + FILL * W1R, [FILL2 * W2R], I32)
        w_base = cut(r_x, 0, [NB, 2 * D])
        it_row = cut(ringf, 2 * J2, [T2 // 2])
        it_ge = cut(ringf, 2 * J2 + T2 // 2, [T2 // 2])
        m_qkv = cut(ringf, 0, [2, 3 * P])
        m_out, m_cx, m_nr, m_qT, m_a = (cut(ringf, 768 + 256 * i, [D]) for i in range(5))
        m_ek, m_vv = cut(ringf, 2048, [2, P]), cut(ringf, 2304, [2, P])
        x_t1, x_t2 = cut(ringf, 2560, [D]), cut(ringf, 2816, [D])
        m_max = cut(ringf, 3072, [16])
        b_row3 = ringf[0:3, 3200:3456].bitcast(BF16).rearrange("p (i n) -> p i n", i=2)
        b_neg, b_ones3 = ringf[:, 3456:3458], ringf[0:3, 3520:3584].bitcast(BF16)
        f_w1, f_w2 = cut(r_agg, 0, [2, HID]), cut(r_agg, 2 * HID, [HB, D])
        f_ht = cut(r_agg, 4 * HID, [HB, 512])
        f_b1, f_wr, f_br = cut(r_agg, 8 * HID, [HB]), cut(r_agg, 8 * HID + 16, [D]), cut(r_agg, 8 * HID + 272, [1])
        f_tmp, f_w = (cut(r_agg, 8 * HID + 512 + 256 * i, [D]) for i in range(2))
        f_ge, f_gt, f_eq, f_pre = (cut(r_agg, 8 * HID + 1280 + 64 * i, [64]) for i in range(4))
        f_key = cut(r_agg, 8 * HID + 1600, [16], I32)
        f_cnt = cut(r_agg, 8 * HID + 1632, [16])
        g_w = [cut(r_agg, 512 * i, [2, D]) for i in range(4)]
        g_kvw, g_wo = cut(r_agg, 2048, [2, 2 * D]), cut(r_agg, 3072, [2, D])
        g_ln = cut(r_agg, 3584, [4, 64])
        g_kv, g_acc = cut(r_agg, 3840, [2, 2 * D]), cut(r_agg, 4864, [2, P])
        g_a = cut(r_agg, 5120, [2, D])
        g_st = cut(r_agg, 5632, [NT * 8, 6])
        g_m, g_r, g_t1, g_t2, g_t3 = (cut(r_agg, 5632 + NT * 48 + NT * 8 * i, [NT * 8]) for i in range(5))
        g_gam, g_bet = (cut(r_agg, 5632 + NT * 88 + 2 * D * i, [8, 64]) for i in range(2))
        r_ax = big[:, 0:2 * TW]
        a_g = cut(r_ax, 0, [T2, C20])
        a_selT = cut(r_ax, T2 * C20, [RING, P], BF16)
        a_far = cut(r_ax, T2 * C20 + RING * P, [4 * P], BF16)
        a_nsel = sel[:, :, :].rearrange("p s n -> p (s n)").bitcast(BF16)[:, 0:RING * P].rearrange(
            "p (s n) -> p s n", s=RING)
        a_sel = [sel[:, :, :].rearrange("p s n -> p (s n)").bitcast(BF16)[:, b * RING * P:(b + 1) * RING * P].rearrange(
            "p (s n) -> p s n", s=RING) for b in range(2)]
        a_am3 = tabf[:, 0:NT * 12].bitcast(BF16).rearrange("p (t k c) -> p t (k c)", t=NT, k=3)
        a_msg3 = cut(tabf, NT * 12, [RING, 3 * C20], BF16)
        a_ident = cut(tabf, NT * 12 + RING * 30, [P], BF16)
        a_eg = cut(tabf, NT * 12 + RING * 30 + 64, [RING, 8])
        a_part = cut(tabf, NT * 12 + RING * 38 + 64, [RING // 2, C20])
        a_rest = cut(tabf, NT * 12 + RING * 38 + 64 + RING // 2 * C20, [RING, C20])
        a_res8 = cut(tabf, NT * 12 + RING * 38 + 64 + RING // 2 * C20 + RING * C20, [NT, 8])
        a_lo = [cut(ringf, 3500 + RING * b, [RING]) for b in range(2)]
        a_g20 = cut(ringf, 0, [RING, C20])
        a_rows = cut(ringf, 320, [NT, C20])
        a_row = cut(ringf, 1300, [5, 16])
        a_wg = cut(ringf, 1380, [2, 16])
        a_am = cut(ringf, 1412, [NT, 8])
        a_mx = cut(ringf, 1804, [NT, 4])
        a_sum = cut(ringf, 2000, [NT, C20])
        a_msg = cut(ringf, 2980, [RING, C20])
        a_z, a_z2 = (cut(ringf, 3300 + 64 * i, [RING, 4]) for i in range(2))
        e_w1, e_w2 = cut(r_agg, 0, [NX, 2 * XH]), cut(r_agg, 4096, [NX, XB * D])
        e_ht = cut(r_agg, 8192, [2, XB, 512])
        e_b1 = cut(r_agg, 12288, [NX * XB])
        gates = cut(tabf, 0, [NT, NX])
        e_b2 = tabf[0:3, 256:256 + NX * D].rearrange("p (e n) -> p e n", e=NX)
        e_b3 = tabf[0:3, 256 + NX * D:256 + NX * D + NX * D // 2].bitcast(BF16).rearrange("p (e n) -> p e n", e=NX)
        s_h, s_a, s_b = (cut(r_agg, NT * 16 * i, [NT, 16]) for i in range(3))
        s_sc, s_d, s_e, s_g = (cut(r_agg, NT * (48 + 4 * i), [NT, 4]) for i in range(4))
        s_v = [cut(r_agg, NT * (64 + i), [NT]) for i in range(6)]

        names = {}

        def S(name):
            if name not in names:
                names[name] = sem(name)
            return names[name]

        def tiles(eng, body):
            body(0, 0, 0, True, False)
            body(1, 0, 1, True, False)
            with eng.Fori(1, NT // 2, 1) as pair:
                body(pair * 2, pair * 2, 0, False, False)
                body(pair * 2 + 1, pair * 2, 1, False, False)
            body(NT - 1, NT - 1, 0, False, True)

        def col(v):
            return bass.ds(v, 1)

        def node(a, t):
            return a[:, t, :] if isinstance(t, int) else a[:, col(t), :].rearrange("p a n -> p (a n)")

        def split(dve, parts, a, rest):
            v = nc.vector
            v.tensor_copy(parts[0], a)
            dve.drain()
            v.tensor_tensor(rest, a, parts[0], ALU.subtract)
            dve.drain()
            v.tensor_copy(parts[1], rest)
            dve.drain()
            v.tensor_tensor(parts[2], rest, parts[1], ALU.subtract)

        def split_rows(dve, parts, rows):
            v = nc.vector
            v.tensor_scalar(b_neg, before[:, 1:3], -1.0, None, ALU.add)
            v.memset(b_ones3, 1.0)
            dve.drain()
            for i in range(2):
                v.tensor_copy(parts, rows)
                dve.drain()
                v.scalar_tensor_tensor(out=rows, in0=parts, scalar=b_neg[0:3, i:i + 1], in1=rows,
                                       op0=ALU.mult, op1=ALU.add)
                dve.drain()
            v.tensor_copy(parts, rows)
            dve.drain()

        def bc(a, shape):
            return a.broadcast_to(shape)

        def one(a, t):
            return a[:, t:t + 1] if isinstance(t, int) else a[:, col(t)]

        def xtile(t):
            v = r_xt.rearrange("p (t n) -> p t n", t=NT)
            return node(v, t)

        GRAPHS = {
            1: dict(E=E1, J=J1, T=T1, W=W1R, bins=bins1, pay=pay1, hit=hit1),
            2: dict(E=E2, J=J2, T=T2, W=W2R, bins=bins2, pay=pay2[:, :], hit=hit2),
        }

        def ln_vector(dve, k, extra=None, store_sem=None):
            v = nc.vector
            with dve.Fori(0, NT // 7, 1) as c:
                for j in range(7):
                    t = c * 7 + j
                    v.bn_stats(st[:, col(t), :].rearrange("p a n -> p (a n)"), node(xs, t))
            dve.drain()
            me, m2e, mo, m2o = st[:, :, 1], st[:, :, 2], st[:, :, 4], st[:, :, 5]
            a, b, c = sm[:, 0, 0:NT], sm[:, 1, 0:NT], sm[:, 2, 0:NT]
            v.tensor_tensor(a, me, mo, ALU.add)
            v.tensor_tensor(b, me, mo, ALU.subtract)
            v.tensor_tensor(c, m2e, m2o, ALU.add)
            dve.drain()
            v.tensor_scalar(mean[:, :], a, 0.5, None, ALU.mult)
            v.tensor_tensor(b, b, b, ALU.mult)
            v.tensor_scalar(c, c, 1.0 / D, None, ALU.mult)
            dve.drain()
            v.scalar_tensor_tensor(out=c, in0=b, scalar=0.25, in1=c, op0=ALU.mult, op1=ALU.add)
            dve.drain()
            v.tensor_scalar(c, c, EPS, None, ALU.add)
            rsqrt_vector(dve, "ln", rstd[:, :], c, a, b, k + 1)

            def body(t, te, slot, first, last):
                if not first:
                    dve.wait_ge(S("ln_turned"), t + (k * NT - 1))
                    if store_sem is not None:
                        dve.wait_ge(store_sem[slot], 8 * te)
                v.tensor_scalar(xn[:, slot, :], node(xs, t), one(mean, t), one(rstd, t),
                                ALU.subtract, ALU.mult).then_inc(S("ln_normed"), 1)
                if extra is not None:
                    dve.drain()
                    extra(t, slot)
            tiles(dve, body)
            dve.drain()

        def rsqrt_vector(dve, ph, res, var, t1, t2, n=1):
            v = nc.vector
            v.drain().then_inc(S(ph + "_var"), 1)
            dve.wait_ge(S(ph + "_root"), n)
            v.reciprocal(res, t1)
            dve.drain()
            v.tensor_tensor(t2, res, res, ALU.mult)
            dve.drain()
            v.tensor_tensor(t2, t2, var, ALU.mult)
            dve.drain()
            v.tensor_scalar(t2, t2, -0.5, 1.5, ALU.mult, ALU.add)
            dve.drain()
            v.tensor_tensor(res, res, t2, ALU.mult)
            dve.drain()

        def root_scalar(act, ph, var, t1, n=1):
            act.wait_ge(S(ph + "_var"), n)
            nc.scalar.activation(t1, var, ACT.Sqrt).then_inc(S(ph + "_root"), 1)

        def ln_tensor(pe, k):
            def body(t, te, slot, first, last):
                pe.wait_ge(S("ln_normed"), t + (k * NT + 1))
                if not first:
                    pe.wait_ge(S("ln_xt"), t + (k * NT - 1))
                for h in range(2):
                    mm = nc.tensor.transpose(pb[slot][:, h * P:h * P + P], xn[:, slot, h * P:h * P + P],
                                             ident[:, :])
                mm.then_inc(S("ln_turned"), 1)
            tiles(pe, body)

        def ln_scalar(act, k):
            root_scalar(act, "ln", sm[:, 2, 0:NT], sm[:, 0, 0:NT], k + 1)

            def body(t, te, slot, first, last):
                act.wait_ge(S("ln_turned"), t + (k * NT + 1))
                nc.scalar.copy(xtile(t), pb[slot][:, 0:D]).then_inc(S("ln_xt"), 1)
            tiles(act, body)

        def bin_vector(dve, k):
            v = nc.vector
            q = GRAPHS[k]
            n, T, W = q["J"], q["T"], q["W"]
            pay = q["pay"].rearrange("p (j w) -> p j w", w=W + 1)
            d_i, hi, ti_late = k_dst[k], k_arr[k][0], k_arr[k][0].bitcast(I32)
            ti, mask = k_arr[k][1].bitcast(I32), k_arr[k][1]
            tj, scan = k_arr[k][2].bitcast(I32), k_arr[k][2]
            rank = k_arr[k][3]
            s_i, tj_late = k_src[k], k_arr[k][4].bitcast(I32)
            on = bc(ones[:, 0:1], [P, n])
            v.tensor_scalar(ti, d_i, LOG_P, None, ALU.logical_shift_right)
            v.tensor_scalar(tj, d_i, P - 1, None, ALU.bitwise_and)
            v.memset(rank, 0.0)
            dve.drain()
            v.tensor_copy(hi, ti)
            v.tensor_copy(pay[:, :, 2].bitcast(F32), tj)
            if k == 1:
                v.scalar_tensor_tensor(out=pay[:, :, 1], in0=s_i, scalar=float(R), in1=k_et[1],
                                       op0=ALU.mult, op1=ALU.add)
                v.tensor_copy(pay[:, :, 3].bitcast(F32), k_nm[1])
            else:
                v.tensor_scalar(pay[:, :, 1], s_i, float(N - 1), None, ALU.min)
            dve.drain()
            counts, off, tot = sm[:, 0, :], sm[:, 1, :], sm[:, 2, :]
            ntile, incl, base = sm[:, 3, 0:NT], sm[:, 4, 0:NT], sm[:, 5, 0:NT]
            v.memset(counts, 0.0)
            dve.drain()
            with dve.Fori(0, NT, 1) as h:
                v.tensor_scalar(mask, hi, iota_r[:, col(h)], None, ALU.is_equal)
                dve.drain()
                v.tensor_reduce(counts[:, col(h)], mask, AX, ALU.add)
                dve.drain()
            v.drain().then_inc(S("counts"), 1)
            dve.wait_ge(S("offsets"), k)
            v.tensor_scalar(sm_i[:, 0, 0:NT], pb[1][:, 0:NT], float(2 * P - 1), None, ALU.add)
            dve.drain()
            v.tensor_scalar(sm_i[:, 1, 0:NT], sm_i[:, 0, 0:NT], LOG_P + 1, None, ALU.logical_shift_right)
            dve.drain()
            v.tensor_copy(ntile, sm_i[:, 1, 0:NT])
            dve.drain()
            v.tensor_tensor_scan(incl, ones[:, 0:NT], ntile, 0.0, ALU.mult, ALU.add)
            dve.drain()
            v.tensor_tensor(base, incl, ntile, ALU.subtract)
            dve.drain()
            v.tensor_copy(sm[:, 11, 0:NT], base)
            v.scalar_tensor_tensor(out=off[:, 0:NT], in0=base, scalar=float(2 * P), in1=pb[0][:, 0:NT],
                                   op0=ALU.mult, op1=ALU.add)
            v.drain().then_inc(S("base"), 1)
            with dve.Fori(0, NT, 1) as h:
                v.tensor_scalar(mask, hi, iota_r[:, col(h)], None, ALU.is_equal)
                dve.drain()
                v.tensor_tensor_scan(scan, on, mask, off[:, col(h)], ALU.mult, ALU.add)
                dve.drain()
                v.tensor_tensor(scan, scan, mask, ALU.mult)
                dve.drain()
                v.tensor_tensor(rank, rank, scan, ALU.add)
                dve.drain()
            v.tensor_scalar(ti_late, rank, -1.0, 0.0, ALU.add, ALU.max)
            v.tensor_scalar(mask, rank, 0.0, None, ALU.is_equal)
            dve.drain()
            v.tensor_scalar(tj_late, ti_late, LOG_P, None, ALU.logical_shift_right)
            v.tensor_scalar(tj, ti_late, P - 1, None, ALU.bitwise_and)
            dve.drain()
            v.scalar_tensor_tensor(out=scan, in0=tj, scalar=float(T), in1=tj_late, op0=ALU.mult, op1=ALU.add)
            v.tensor_copy(rank, k_spare[k])
            dve.drain()
            v.tensor_tensor(rank, rank, scan, ALU.subtract)
            dve.drain()
            v.tensor_tensor(rank, rank, mask, ALU.mult)
            dve.drain()
            v.tensor_tensor(pay[:, :, 0], scan, rank, ALU.add)
            v.drain().then_inc(S(f"binned{k}"), 1)
            dve.wait_ge(S("baseT"), k)
            v.tensor_copy(sm[0:NT, 6, 0:1], pb[2][0:NT, 0:1])
            dve.drain()
            v.tensor_scalar(it_ge[0:NT, 0:T // 2], it_row[0:NT, 0:T // 2], sm[0:NT, 6, 0:1], None, ALU.is_ge)
            v.drain().then_inc(S("atleast"), 1)
            dve.wait_ge(S("hits"), k)
            for i, c in enumerate(range(0, T // 2, 512)):
                w = min(512, T // 2 - c)
                v.tensor_scalar(q["hit"][0:1, c:c + w], pb[3 + i][0:1, 0:w], -1.0, None, ALU.add)
            v.drain().then_inc(S(f"hit{k}"), 1)

        def bin_tensor(pe, k):
            T = GRAPHS[k]["T"]
            pe.wait_ge(S("counts"), k)
            nc.tensor.matmul(pb[0][:, 0:64], before[:, :], sm[:, 0, :], start=True, stop=True)
            nc.tensor.matmul(pb[1][:, 0:64], ones[:, :], sm[:, 0, :], start=True,
                             stop=True).then_inc(S("offsets"), 1)
            pe.wait_ge(S("base"), k)
            nc.tensor.transpose(pb[2][0:NT, 0:P], sm[:, 11, 0:NT], ident[:, :]).then_inc(S("baseT"), 1)
            pe.wait_ge(S("atleast"), k)
            for i, c in enumerate(range(0, T // 2, 512)):
                w = min(512, T // 2 - c)
                mm = nc.tensor.matmul(pb[3 + i][0:1, 0:w], ones[0:NT, 0:1], it_ge[0:NT, c:c + w],
                                      start=True, stop=True)
            mm.then_inc(S("hits"), 1)

        def scatter_plan(k):
            n = GRAPHS[k]["J"]
            return n, n // (2 * SCOL), n % (2 * SCOL)

        def scatter_pool(pool, k):
            q = GRAPHS[k]
            W = q["W"]
            pay = q["pay"].rearrange("p (j w) -> p j w", w=W + 1)
            n, its, rest = scatter_plan(k)
            pool.wait_ge(S(f"binned{k}"), 1)
            pool.wait_ge(S(f"filled{k}"), 16 * 8)

            def body(it, g, cnt, first):
                if not first:
                    pool.wait_ge(S(f"scat{k}_{g}"), it * (16 * SCOL))
                at = it * (2 * SCOL) + g * SCOL
                nc.gpsimd.tensor_copy(scat[:, g, 0:cnt, 0:W + 1], pay[:, bass.ds(at, cnt), :])
                pool.drain()
                for c in range(cnt):
                    nc.gpsimd.indirect_dma_start(
                        q["bins"], bass.IndirectOffsetOnAxis(ap=scat[:, g, c, 0:1], axis=0),
                        scat[:, g, c, 1:1 + W], None).then_inc(S(f"scat{k}_{g}"), 16)
            body(0, 0, SCOL, True)
            body(0, 1, SCOL, True)
            with pool.Fori(1, its, 1) as it:
                body(it, 0, SCOL, False)
                body(it, 1, SCOL, False)
            for g in range(2):
                cnt = min(SCOL, rest - g * SCOL)
                if cnt > 0:
                    body(its, g, cnt, False)

        def scattered(eng, k):
            n, its, rest = scatter_plan(k)
            for g in range(2):
                total = its * SCOL + min(SCOL, max(0, rest - g * SCOL))
                eng.wait_ge(S(f"scat{k}_{g}"), 16 * total)

        NIT1, NIT2 = T1 // RING, T2 // RING
        NG = RING // GRP

        def gather_pool(pool, ph, table, dst_of):
            def body(it):
                for g in range(NG):
                    pool.wait_ge(S(ph + "_idx"), it * NG + (g + 1))
                    pool.nop(nofuse=True)
                    for c in range(GRP):
                        s = g * GRP + c
                        nc.gpsimd.indirect_dma_start(
                            dst_of(s), None, table,
                            bass.IndirectOffsetOnAxis(ap=idx[:, s, :], axis=0)).then_inc(S(f"{ph}_got{g}"), 16)
            return body

        def stage_idx(act, ph, tab, it, g, need):
            act.wait_ge(S(ph + "_used"), need)
            at = it * RING + g * GRP
            nc.scalar.copy(idx2[:, g * GRP:g * GRP + GRP],
                           tab[:, bass.ds(at, GRP), 0]).then_inc(S(ph + "_idx"), 1)

        def group_sel(dve, ph, tab, word, it, g, to=sel):
            for c in range(GRP):
                s = g * GRP + c
                lo = tab[:, bass.ds(it * RING + s, 1), word].bitcast(F32)
                ins = nc.vector.tensor_scalar(to[:, s, :], iota_r[:, :], lo, None, ALU.is_equal)
            ins.then_inc(S(ph + "_sel"), 1)

        def build_sel(dve, ph, tab, word, it):
            for g in range(NG):
                group_sel(dve, ph, tab, word, it, g)

        block = ctx.enter_context(nc.Block())

        @block.sync
        def _(sp):
            sp.wait_ge(S("edges_cleared"), 1)
            for d, s in ((k_dst, dst), (k_src, src), (k_et, etype), (k_nm, norm)):
                full = (P - 1) * J1
                d = d[1]
                sp.dma_start(d[0:P - 1, 0:J1], s[0:full].rearrange("(p j) -> p j", j=J1)).then_inc(S("edges1"), 16)
                sp.dma_start(d[P - 1:P, 0:E1 - full],
                             s[full:E1].rearrange("(p j) -> p j", p=1)).then_inc(S("edges1"), 16)
            sp.wait_ge(S("fills"), 1)
            for i in range(8):
                for k, f, FL in ((1, fill1, FILL), (2, fill2, FILL2)):
                    q = GRAPHS[k]
                    rows = q["bins"][0:P * q["T"], :].rearrange("(p t) w -> p (t w)", p=P)
                    n = FL * q["W"]
                    sp.dma_start(rows[:, i * n:(i + 1) * n], f).then_inc(S(f"filled{k}"), 16)
            for i in range(NB):
                sp.dma_start(w_base[:, i, :].rearrange("p (h o) -> p h o", h=2),
                             w_rel[i].rearrange("(h p) o -> p h o", p=P)).then_inc(S("w_rel"), 16)
            sp.dma_start(sm[:, 10, 0:R * NB], w_comp.rearrange("r b -> (r b)").partition_broadcast(P)).then_inc(S("w_rel"), 16)
            sp.dma_start(wl[:, :, :], w_loop.rearrange("(h p) o -> p h o", p=P)).then_inc(S("w_rel"), 16)
            for i, b in enumerate((h_bias, b_mix0)):
                sp.dma_start(brow[:, i, :], b.partition_broadcast(3)).then_inc(S("w_rel"), 16)
            sp.dma_start(k_src[2], gat_edges[0].rearrange("(p j) -> p j", p=P)).then_inc(S("edges2"), 16)
            sp.dma_start(k_dst[2], gat_edges[1].rearrange("(p j) -> p j", p=P)).then_inc(S("edges2"), 16)
            sp.wait_ge(S("w_all"), 1)
            sp.dma_start(xs[:, 0:NT - 1, :], x[0:(NT - 1) * P, :].rearrange("(t p) d -> p t d", p=P)).then_inc(S("x"), 16)
            sp.dma_start(xs[0:LAST, NT - 1, :], x[(NT - 1) * P:N, :]).then_inc(S("x"), 16)

            def put_hr(t, te, slot, first, last):
                sp.wait_ge(S("hr_act"), 4 * t + 4)
                rows = hr[bass.ds(t * P, P), :]
                sp.dma_start(rows, hstage[:, slot, :]).then_inc(S(f"hr_put{slot}"), 16)
            tiles(sp, put_hr)
            scattered(sp, 1)
            sp.wait_ge(S("hit2"), 1)
            sp.dma_start(tab1[:, 0:T1, :], bins1[0:P * T1, :].rearrange("(p t) w -> p t w", p=P)).then_inc(S("tab1"), 16)
            sp.wait_ge(S("rg_done"), 1)
            sp.dma_start(m_qkv, w_qkv.rearrange("(h p) o -> p h o", p=P)).then_inc(S("w_mix0"), 16)
            sp.dma_start(m_out, w_mix0).then_inc(S("w_mix0"), 16)
            sp.wait_ge(S("x1"), 1)
            sp.dma_start(f_w1, w_f1.rearrange("(h p) o -> p h o", p=P)).then_inc(S("w_ffn"), 16)
            sp.dma_start(f_w2, w_f2.rearrange("(b p) o -> p b o", p=P)).then_inc(S("w_ffn"), 16)
            sp.dma_start(f_b1, b_f1).then_inc(S("w_ffn"), 16)
            sp.dma_start(f_wr, w_r.rearrange("d o -> (d o)").partition_broadcast(P)).then_inc(S("w_ffn"), 16)
            sp.dma_start(f_br, b_r.partition_broadcast(P)).then_inc(S("w_ffn"), 16)
            sp.dma_start(brow[:, 0, :], b_f2.partition_broadcast(3)).then_inc(S("w_ffn"), 16)
            sp.wait_ge(S("x2"), 1)
            for i, w in enumerate((wk, wv, wo, wq)):
                sp.dma_start(g_w[i], w.rearrange("(h p) o -> p h o", p=P)).then_inc(S("w_mix1"), 16)
            sp.dma_start(wl[:, :, :], w_gcn.rearrange("(h p) o -> p h o", p=P)).then_inc(S("w_mix1"), 16)
            sp.dma_start(brow[:, 0, :], bo.partition_broadcast(3)).then_inc(S("w_mix1"), 16)
            for i, w in enumerate((ln_kg, ln_kb, ln_vg, ln_vb)):
                sp.dma_start(g_ln[:, i, :], w.partition_broadcast(P)).then_inc(S("w_mix1"), 16)

            def put_feat0(t, te, slot, first, last):
                sp.wait_ge(S("ln_normed"), t + (2 * NT + 1))
                sp.dma_start(feat[bass.ds(t * P, P), :], xn[:, slot, :]).then_inc(S(f"f0_put{slot}"), 16)
            tiles(sp, put_feat0)
            scattered(sp, 2)
            sp.dma_start(tab2, bins2[0:P * T2, :].rearrange("(p t) w -> p t w", p=P)).then_inc(S("tab2"), 16)
            with sp.Fori(0, LAYERS, 1) as layer:
                with sp.Fori(0, NT // 7, 1) as c:
                    sp.wait_ge(S("gc_out"), layer * NT + c * 7 + 7)
                    sp.dma_start(feat[bass.ds(c * (7 * P), 7 * P), :].rearrange("(t p) d -> p t d", p=P),
                                 agg[:, bass.ds(c * 7, 7), :]).then_inc(S("gc_put"), 16)
            sp.wait_ge(S("gc_put"), 16 * LAYERS * (NT // 7))
            sp.dma_start(y0[:, :, :], feat[:, :].rearrange("(t p) d -> p t d", p=P)).then_inc(S("f5"), 16)
            sp.dma_start(a_wg, w_gat.rearrange("(h p) o -> p h o", p=P)).then_inc(S("w_gat"), 16)
            for i, w in enumerate((att_src.rearrange("a b -> (a b)"), att_dst.rearrange("a b -> (a b)"), b_gat, ln_g, ln_b)):
                sp.dma_start(a_row[:, i, :], w.partition_broadcast(P)).then_inc(S("w_gat"), 16)
            sp.wait_ge(S("rows"), 1)
            sp.dma_start(rows20.rearrange("(t p) c -> p t c", p=P), a_rows).then_inc(S("rows_put"), 16)
            sp.wait_ge(S("gates"), 1)
            sp.dma_start(e_b1, b_e1).then_inc(S("w_moe"), 16)
            for e in range(NX):
                sp.dma_start(e_w1[:, e, :].rearrange("p (h o) -> p h o", h=2),
                             w_e1[e].rearrange("(h p) o -> p h o", p=P)).then_inc(S("w_moe"), 16)
                sp.dma_start(e_w2[:, e, :].rearrange("p (b o) -> p b o", b=XB),
                             w_e2[e].rearrange("(b p) o -> p b o", p=P)).then_inc(S("w_moe"), 16)
                sp.dma_start(e_b2[:, e, :], b_e2[e].partition_broadcast(3)).then_inc(S("w_moe"), 16)
            sp.wait_ge(S("x4"), 1)
            sp.dma_start(out[0:(NT - 1) * P, :].rearrange("(t p) d -> p t d", p=P), xs[:, 0:NT - 1, :]).then_inc(S("out"), 16)
            sp.dma_start(out[(NT - 1) * P:N, :], xs[0:LAST, NT - 1, :]).then_inc(S("out"), 16)
            sp.wait_ge(S("out"), 32)

        @block.gpsimd
        def _(pool):
            g = nc.gpsimd
            g.memset(k_dst[1], NX * 4096)
            g.memset(k_src[1], 0)
            g.memset(k_et[1], 0)
            g.memset(k_nm[1], 0.0)
            pool.drain().then_inc(S("edges_cleared"), 1)
            for f, W in ((fill1, W1R), (fill2, W2R)):
                fv = f.rearrange("p (t w) -> p t w", w=W)
                g.memset(f, 0)
                pool.drain()
                g.memset(fv[:, :, 1].bitcast(F32), -1.0)
            pool.drain().then_inc(S("fills"), 1)
            ii = cut(ringf, 2 * J2 + T2, [P], I32)
            g.iota(ii, [[1, P]], base=0, channel_multiplier=0)
            g.iota(it_ge.bitcast(I32), [[1, T2 // 2]], base=0, channel_multiplier=0)
            g.iota(k_spare[1], [[1, J1]], base=P * T1, channel_multiplier=J1)
            g.iota(k_spare[2], [[1, J2]], base=P * T2, channel_multiplier=J2)
            g.memset(ident[:, :], 0.0)
            g.memset(xs[:, NT - 1, :], 0.0)
            g.memset(tab1[:, T1:T1 + RING, :], 0)
            g.memset(ones[:, :], 1.0)
            g.memset(before[:, :], 1.0)
            g.memset(mask32[:, :], 1.0)
            g.memset(mask64[:, :], 1.0)
            g.memset(valid[:, :], 1.0)
            g.memset(eps_t[:, :], EPS)
            pool.drain()
            g.tensor_copy(iota_r[:, :], ii)
            g.tensor_copy(it_row, it_ge.bitcast(I32))
            g.affine_select(out=ident[:, :], in_=ident[:, :], compare_op=ALU.not_equal, fill=1.0, base=0,
                            pattern=[[1, P]], channel_multiplier=-1)
            g.affine_select(out=before[:, :], in_=before[:, :], compare_op=ALU.is_gt, fill=0.0, base=0,
                            pattern=[[1, P]], channel_multiplier=-1)
            g.affine_select(out=valid[:, :], in_=valid[:, :], compare_op=ALU.is_ge, fill=0.0, base=N - 1,
                            pattern=[[-P, NT]], channel_multiplier=-1)
            for m, w in ((mask32, 32), (mask64, 64)):
                v = m[:, :].rearrange("p (g c) -> p g c", c=w)
                g.affine_select(out=v, in_=v, compare_op=ALU.is_ge, fill=0.0, base=0,
                                pattern=[[-w, P // w], [0, w]], channel_multiplier=1)
                pool.drain()
                g.affine_select(out=v, in_=v, compare_op=ALU.is_ge, fill=0.0, base=w - 1,
                                pattern=[[w, P // w], [0, w]], channel_multiplier=-1)
            pool.drain().then_inc(S("consts"), 5)
            scatter_pool(pool, 1)

            pool.wait_ge(S("hr_put0"), 16 * ((NT + 1) // 2))
            pool.wait_ge(S("hr_put1"), 16 * (NT // 2))
            body = gather_pool(pool, "rg", hr_rows, lambda s: ring[:, s, 0:D])
            with pool.Fori(0, NIT1, 1) as it:
                body(it)
            scatter_pool(pool, 2)

            body = gather_pool(pool, "gc", feat, lambda s: ring[:, s, 0:D])
            with pool.Fori(0, LAYERS, 1) as layer:
                with pool.Fori(0, NIT1, 1) as it:
                    body(layer * NIT1 + it)

            pool.wait_ge(S("rows_put"), 16)
            body = gather_pool(pool, "ga", rows20, lambda s: a_g20[:, s, :])
            with pool.Fori(0, NIT2, 1) as it:
                body(it)
            pool.wait_ge(S("ga_dmm"), NIT2 * RING + GRP)
            pool.wait_ge(S("ga_nsel"), NIT2 * NG + NG - 1)
            with pool.Fori(0, NIT2 // 2, 1) as q:
                for b in range(2):
                    n = q * 2 + b
                    pool.wait_ge(S("gb_mm"), n + 1)
                    pool.nop(nofuse=True)
                    g.tensor_copy(a_lo[b], tab2[:, bass.ds(n * RING, RING), 1].bitcast(F32))
                    pool.drain()
                    for s in range(RING):
                        ins = g.tensor_scalar(a_sel[b][:, s, :], iota_r[:, :], a_lo[b][:, s:s + 1], None, ALU.is_equal)
                        if s % GRP == GRP - 1:
                            ins.then_inc(S("gb_sel"), 1)

        def stage_pass(act, ph, evac=None, mms=1, start=None):
            def stage(t, slot):
                nc.scalar.copy(xn[:, slot, :], xtile(t)).then_inc(S("st"), 1)
            if start is not None:
                start()
            stage(0, 0)

            def body(t, te, slot, first, last):
                if not last:
                    if not (isinstance(t, int) and t == 0):
                        act.wait_ge(S(ph + "_mm"), t * mms)
                    stage(t + 1, 1 - slot)
                if evac is not None:
                    evac(t, te, slot, first, last)
            tiles(act, body)

        @block.scalar
        def _(act):
            a = nc.scalar
            act.wait_ge(S("consts"), 5)
            ln_scalar(act, 0)

            def hr_evac(t, te, slot, first, last):
                for c in range(4):
                    act.wait_ge(S("hr_mm"), t * 4 + c + 1)
                    if c == 0 and not first:
                        act.wait_ge(S(f"hr_put{slot}"), 8 * te)
                    a.copy(hstage[:, slot, c * 512:c * 512 + 512], pb[4 + c][:, :]).then_inc(S("hr_act"), 1)
            stage_pass(act, "hr", hr_evac, mms=4)

            act.wait_ge(S("tab1"), 16)
            for g in range(NG - 1):
                stage_idx(act, "rg", tab1, 0, g, g + 1)
            with act.Fori(0, NIT1, 1) as it:
                for g in range(NG):
                    act.wait_ge(S(f"rg_got{g}"), it * (16 * GRP) + 16 * GRP)
                    for c in range(GRP):
                        s = g * GRP + c
                        w = tab1[:, bass.ds(it * RING + s, 1), 2].bitcast(F32)
                        ins = a.activation(ring[:, s, 0:D], ring[:, s, 0:D], ACT.Copy, scale=w)
                    ins.then_inc(S("rg_scaled"), 1)
                    if g:
                        stage_idx(act, "rg", tab1, it + 1, g - 1, it * NG + (NG + g))
                    else:
                        stage_idx(act, "rg", tab1, it, NG - 1, it * NG + NG)

            def m0_evac(t, te, slot, first, last):
                act.wait_ge(S("m0_mm"), t + 1)
                if not first:
                    act.wait_ge(S("m0_cx"), t - 1)
                a.activation(m_ek[:, slot, :], pb[slot][:, 0:P], ACT.Exp)
                a.copy(m_vv[:, slot, :], pb[slot][:, P:D])
                act.drain().then_inc(S("m0_ev"), 1)
            act.wait_ge(S("m0_max"), 1)
            stage_pass(act, "m0", m0_evac)
            act.wait_ge(S("m0_mm"), NT)
            stage_pass(act, "x1")

            ln_scalar(act, 1)
            act.wait_ge(S("w_ffn"), 16 * 6)
            act.sem_inc(S("fh_act"), 4)

            def gelu(c, width):
                for b in range(HB):
                    act.wait_ge(S("fh_mm"), c * HB + b + 1)
                    a.activation(f_ht[:, b, 0:width], pb[b % 4][:, 0:width], ACT.Gelu_apprx_tanh,
                                 bias=f_b1[:, b:b + 1]).then_inc(S("fh_act"), 1)
            with act.Fori(0, NT // 4, 1) as c:
                gelu(c, 512)
            gelu(NT // 4, P)

            ln_scalar(act, 2)
            act.wait_ge(S("f0_put0"), 16 * ((NT + 1) // 2))
            act.wait_ge(S("f0_put1"), 16 * (NT // 2))
            stage_pass(act, "k1")
            root_scalar(act, "kv", g_t3, g_t1)
            act.wait_ge(S("k1_mm"), NT)

            def kv_centre(t, te, slot, first, last):
                act.wait_ge(S("k2_mm"), t + 1)
                if not first:
                    act.wait_ge(S("k2_cx"), t - 1)
                act.nop(nofuse=True)
                for i in range(8):
                    n = t * 8 + i
                    ins = a.activation(g_kv[:, slot, i * 64:i * 64 + 64], pb[slot][:, i * 64:i * 64 + 64],
                                       ACT.Identity, scale=one(g_r, n), bias=one(g_t1, n))
                ins.then_inc(S("k2_nm"), 1)
            act.wait_ge(S("kv_mr"), 1)
            stage_pass(act, "k2", kv_centre)
            act.wait_ge(S("k2_mm"), NT)
            stage_pass(act, "y0")

            with act.Fori(0, LAYERS, 1) as layer:
                act.wait_ge(S("gc_tab"), layer + 1)
                with act.Fori(0, NIT1, 1) as it:
                    for g in range(NG):
                        n = layer * (NIT1 * NG) + it * NG
                        act.wait_ge(S("gc_used"), n + (g + 1))
                        nc.scalar.copy(idx2[:, g * GRP:g * GRP + GRP],
                                       tab1[:, bass.ds(it * RING + g * GRP, GRP), 0]).then_inc(S("gc_idx"), 1)
                act.wait_ge(S("gc_summed"), layer + 1)
                base = layer * NT

                def stage(t, slot):
                    a.copy(xn[:, slot, :], node(agg, t)).then_inc(S("gc_st"), 1)

                def relu(t):
                    act.wait_ge(S("gc_fin"), base + t + 2 + 1)
                    act.nop(nofuse=True)
                    a.activation(node(agg, t), node(agg, t), ACT.Relu).then_inc(S("gc_out"), 1)

                def finish(t, te, slot, first, last):
                    if not last:
                        act.wait_ge(S("gc_mm"), base + t + 1)
                        stage(t + 1, 1 - slot)
                    if not (isinstance(t, int) and t == 0):
                        relu(t - 1)
                    if last:
                        relu(t)
                stage(0, 0)
                tiles(act, finish)

            ln_scalar(act, 3)
            stage_pass(act, "gt")
            act.wait_ge(S("tab2"), 16)
            act.wait_ge(S("rows_put"), 16)

            def ga_stage(it, g):
                a.copy(idx2[:, g * GRP:g * GRP + GRP],
                       tab2x[:, bass.ds(it * RING + g * GRP, GRP), 0]).then_inc(S("ga_idx"), 1)
                for c in range(GRP):
                    s = g * GRP + c
                    ins = a.activation(a_nsel[:, s, :], iota_r[:, :], ACT.Square, scale=-1.0,
                                       bias=tab2x[:, bass.ds(it * RING + s, 1), 1].bitcast(F32))
                ins.then_inc(S("ga_nsel"), 1)
            for g in range(NG - 1):
                ga_stage(0, g)
            with act.Fori(0, NIT2, 1) as it:
                for g in range(NG):
                    act.wait_ge(S(f"ga_got{g}"), it * (16 * GRP) + 16 * GRP)
                    act.nop(nofuse=True)
                    a.copy(a_g[:, bass.ds(it * RING + g * GRP, GRP), :], a_g20[:, g * GRP:g * GRP + GRP, :])
                    act.wait_ge(S("ga_dmm"), it * RING + g * GRP + GRP)
                    act.nop(nofuse=True)
                    if g:
                        ga_stage(it + 1, g - 1)
                    else:
                        ga_stage(it, NG - 1)
            act.wait_ge(S("self_z"), 1)
            a.activation(a_sum[:, :, 16:20], a_mx, ACT.Exp).then_inc(S("self_e"), 1)

            def selT(n):
                for g in range(NG):
                    act.wait_ge(S("gb_tp"), n * NG + (g + 1))
                    a.copy(a_selT[:, g * GRP:g * GRP + GRP, :].rearrange("p s n -> p (s n)"),
                           pb[g % 2][:, :].bitcast(BF16)[:, 0:GRP * P]).then_inc(S("gb_selT"), 1)

            def weights(n):
                act.wait_ge(S("gb_z"), n + 1)
                a.activation(a_msg[:, :, 16:20], a_z, ACT.Exp).then_inc(S("gb_ee"), 1)
            selT(0)
            with act.Fori(0, NIT2 - 1, 1) as n:
                weights(n)
                selT(n + 1)
            weights(NIT2 - 1)
            root_scalar(act, "sc", s_v[1], s_v[2])
            act.wait_ge(S("sc_e"), 1)
            a.activation(s_e, s_d, ACT.Exp).then_inc(S("sc_exp"), 1)
            ln_scalar(act, 4)
            act.wait_ge(S("w_moe"), 16 * (3 * NX + 1))
            act.sem_inc(S("eh_act"), 4)

            def xgelu(c, width):
                for e in range(NX):
                    for b in range(XB):
                        n = e * XB + b
                        act.wait_ge(S("eh_mm"), c * (NX * XB) + n + 1)
                        a.activation(e_ht[:, e % 2, b, 0:width], pb[b][:, 0:width], ACT.Gelu,
                                     bias=e_b1[:, n:n + 1]).then_inc(S("eh_act"), 1)
            with act.Fori(0, NT // 4, 1) as c:
                xgelu(c, 512)
            xgelu(NT // 4, P)

        def mm2(out_, slot, rhs, n, last=True, start=True):
            for h in range(2):
                m = nc.tensor.matmul(out_, xn[:, slot, h * P:h * P + P], rhs(h), start=(h == 0 and start),
                                     stop=(h == 1 and last))
            return m

        @block.tensor
        def _(pe):
            te_ = nc.tensor
            pe.wait_ge(S("consts"), 5)
            bin_tensor(pe, 1)
            ln_tensor(pe, 0)
            pe.wait_ge(S("ln_xt"), 1 * NT)

            def hr_body(t, te, slot, first, last):
                pe.wait_ge(S("st"), t + (0 * NT + 1))
                zero = isinstance(t, int) and t == 0
                for c in range(4):
                    if not zero:
                        pe.wait_ge(S("hr_act"), 4 * t - 3 + c)
                    mm2(pb[4 + c][:, :], slot, lambda h: w_all[:, h, c * 512:c * 512 + 512],
                        512).then_inc(S("hr_mm"), 1)
            tiles(pe, hr_body)
            pe.wait_ge(S("hr_act"), 4 * NT)
            bin_tensor(pe, 2)

            pe.sem_inc(S("rg_used"), NG)
            with pe.Fori(0, NIT1, 1) as it:
                for g in range(NG):
                    pe.wait_ge(S("rg_sel"), it * NG + (g + 1))
                    pe.wait_ge(S("rg_scaled"), it * NG + (g + 1))
                    pe.wait_ge(S("rg_added"), it * NG + (g + 1))
                    for c in range(GRP):
                        s = g * GRP + c
                        k, h = s // 2 % 4, c % 2
                        m = te_.matmul(pb[k][:, 0:D + 1], sel[:, s, :], ring[:, s, :], start=(h == 0), stop=(h == 1))
                    m.then_inc(S("rg_used"), 1)
            pe.wait_ge(S("w_mix0"), 32)
            pe.wait_ge(S("rg_done"), 1)
            xtv = xt

            def kt(c, slot, first):
                if not first:
                    pe.wait_ge(S("kt_red"), c - 1)
                for h in range(2):
                    m = te_.matmul(pb[slot][:, :].rearrange("p (t n) -> p t n", t=4), m_qkv[:, h, P:2 * P],
                                   xtv[:, bass.ds(c * 4, 4), h, :], start=(h == 0), stop=(h == 1))
                m.then_inc(S("kt_mm"), 1)
            kt(0, 0, True)
            kt(1, 1, True)
            with pe.Fori(1, NT // 8, 1) as c:
                kt(c * 2, 0, False)
                kt(c * 2 + 1, 1, False)
            pe.wait_ge(S("kt_red"), NT // 4 - 1)
            for h in range(2):
                m = te_.matmul(pb[0][:, 0:LAST], m_qkv[:, h, P:2 * P], xtv[:, NT - 1, h, 0:LAST],
                               start=(h == 0), stop=(h == 1))
            m.then_inc(S("kt_mm"), 1)
            pe.wait_ge(S("m0_neg"), 1)
            te_.matmul(pb[2][0:1, 0:P], m_max[:, 14:15], ident[:, :], start=True, stop=True).then_inc(S("m0_row"), 1)
            pe.wait_ge(S("m0_max"), 1)

            def m0_kv(t, slot, fresh=False):
                pe.wait_ge(S("st"), t + (1 * NT + 1))
                if not fresh:
                    pe.wait_ge(S("m0_ev"), t - 1)
                mm2(pb[slot][:, 0:D], slot, lambda h: m_qkv[:, h, P:3 * P], D, last=False)
                te_.matmul(pb[slot][:, 0:D], ones[0:1, :], m_nr[0:1, :], start=False, stop=True).then_inc(S("m0_mm"), 1)

            def m0_body(t, te, slot, first, last):
                if not last:
                    m0_kv(t + 1, 1 - slot, fresh=isinstance(t, int) and t == 0)
                pe.wait_ge(S("m0_ev"), t + 1)
                if not first:
                    pe.wait_ge(S("m0_add"), t - 1)
                r = LAST if last else P
                te_.matmul(pb[2 + slot][:, 0:P], m_vv[0:r, slot, :], m_ek[0:r, slot, :], start=True, stop=True)
                te_.matmul(pb[2 + slot][:, P:P + 1], m_ek[0:r, slot, :], ones[0:r, 0:1], start=True,
                           stop=True).then_inc(S("m0_cx"), 1)
            m0_kv(0, 0, fresh=True)
            tiles(pe, m0_body)
            pe.wait_ge(S("m0_add"), NT)
            for h in range(2):
                m = te_.transpose(pb[0][:, h * P:h * P + P], m_qkv[:, h, 0:P], ident[:, :])
            pe.wait_ge(S("m0_ctx"), 1)
            te_.matmul(pb[1][:, 0:D], m_cx[:, 0:P], m_out[:, :], start=True, stop=True).then_inc(S("m0_a"), 1)
            pe.wait_ge(S("m0_sc"), 1)
            for h in range(2):
                m = te_.matmul(pb[2 + h][:, 0:D], m_qT[:, h * P:h * P + P], m_a[:, :], start=True, stop=True)
            m.then_inc(S("m0_m"), 1)
            pe.wait_ge(S("wm"), 1)

            def x1_body(t, te, slot, first, last):
                pe.wait_ge(S("st"), t + (2 * NT + 1))
                if not first:
                    pe.wait_ge(S("x1_dve"), t - 1)
                for i, w in enumerate((wl, wm)):
                    mm2(pb[2 * i + slot][:, 0:D], slot, lambda h: w[:, h, :], D, last=False)
                    m = te_.matmul(pb[2 * i + slot][:, 0:D], b_ones3, b_row3[:, i, :], start=False, stop=True)
                m.then_inc(S("x1_mm"), 1)
            tiles(pe, x1_body)

            ln_tensor(pe, 1)
            pe.wait_ge(S("w_ffn"), 16 * 6)
            with pe.Fori(0, 32, 1) as i:
                pe.wait_ge(S("th_cnt"), i + 1)
                te_.matmul(pb[7][:, 0:1], ones[:, :], f_cnt[:, 0:1], start=True, stop=True).then_inc(S("th_mm"), 1)
            pe.wait_ge(S("th_eq"), 1)
            te_.matmul(pb[4][:, 0:NT], ones[:, :], f_gt[:, 0:NT], start=True, stop=True)
            te_.matmul(pb[5][:, 0:NT], before[:, :], f_eq[:, 0:NT], start=True, stop=True)
            te_.matmul(pb[6][:, 0:NT], ones[:, :], f_eq[:, 0:NT], start=True, stop=True).then_inc(S("th_pre"), 1)
            pe.wait_ge(S("coef"), 1)
            pe.wait_ge(S("ln_xt"), 2 * NT)

            def ffn(c, n):
                for b in range(HB):
                    pe.wait_ge(S("fh_act"), c * HB + b + 1)
                    for h in range(2):
                        w = f_w1[:, h, b * P:b * P + P]
                        if n == 4:
                            m = te_.matmul(pb[b % 4][:, :].rearrange("p (t n) -> p t n", t=4), w,
                                           xtv[:, bass.ds(c * 4, 4), h, :], start=(h == 0), stop=(h == 1))
                        else:
                            m = te_.matmul(pb[b % 4][:, 0:P], w, xtv[:, NT - 1, h, :], start=(h == 0), stop=(h == 1))
                    m.then_inc(S("fh_mm"), 1)
                for j in range(n):
                    pe.wait_ge(S("fh_act"), c * HB + HB + 4)
                    pe.wait_ge(S("fo_dve"), c * 4 + j + 1)
                    for b in range(HB):
                        te_.matmul(pb[4 + j][:, 0:D], f_ht[:, b, j * P:j * P + P], f_w2[:, b, :], start=(b == 0), stop=False)
                    te_.matmul(pb[4 + j][:, 0:D], b_ones3, b_row3[:, 0, :], start=False,
                               stop=True).then_inc(S("fo_mm"), 1)
            with pe.Fori(0, NT // 4, 1) as c:
                ffn(c, 4)
            ffn(NT // 4, 1)

            pe.wait_ge(S("x2"), 1)
            ln_tensor(pe, 2)
            pe.wait_ge(S("w_mix1"), 16 * 10)
            pe.wait_ge(S("ln_xt"), 3 * NT)
            for i, w in enumerate(g_w[0:3]):
                for ih in range(2):
                    for oh in range(2):
                        at = (0, D, 0)[i] + oh * P
                        m = te_.transpose(pb[(0, 0, 2)[i] + ih][:, at:at + P],
                                          w[:, oh, ih * P:ih * P + P], ident[:, :])
            m.then_inc(S("g_tr"), 1)
            pe.wait_ge(S("g_w"), 1)

            def kv1(t, te, slot, first, last):
                pe.wait_ge(S("st"), t + (3 * NT + 1))
                if not first:
                    pe.wait_ge(S("k1_dve"), t - 1)
                mm2(pb[slot][:, :], slot, lambda h: g_kvw[:, h, :], 512).then_inc(S("k1_mm"), 1)
            tiles(pe, kv1)

            def kv2_mm(t, slot, fresh=False):
                pe.wait_ge(S("st"), t + (4 * NT + 1))
                if not fresh:
                    pe.wait_ge(S("k2_kv"), t - 1)
                mm2(pb[slot][:, :], slot, lambda h: g_kvw[:, h, :], 512).then_inc(S("k2_mm"), 1)

            def kv2(t, te, slot, first, last):
                if not last:
                    kv2_mm(t + 1, 1 - slot, fresh=isinstance(t, int) and t == 0)
                pe.wait_ge(S("k2_kv"), t + 1)
                if not first:
                    pe.wait_ge(S("k2_add"), t - 1)
                r = LAST if last else P
                for h in range(2):
                    m = te_.matmul(pb[2 + slot][:, h * P:h * P + P], g_kv[0:r, slot, D + h * P:D + h * P + P],
                                   g_kv[0:r, slot, h * P:h * P + P], start=True, stop=True)
                m.then_inc(S("k2_cx"), 1)
            pe.wait_ge(S("k1_dve"), NT)
            kv2_mm(0, 0, fresh=True)
            tiles(pe, kv2)
            pe.wait_ge(S("g_ctx"), 1)
            for h in range(2):
                m = te_.matmul(pb[4 + h][:, 0:D], g_acc[:, h, :], g_wo[:, h, :], start=True, stop=True)
            m.then_inc(S("g_am"), 1)
            pe.wait_ge(S("g_a"), 1)
            for ih in range(2):
                for h in range(2):
                    m = te_.matmul(pb[6 + ih][:, 0:D], g_w[3][:, h, ih * P:ih * P + P], g_a[:, h, :],
                                   start=(h == 0), stop=(h == 1))
            m.then_inc(S("g_m"), 1)
            pe.wait_ge(S("g_wm"), 1)

            def y0_body(t, te, slot, first, last):
                pe.wait_ge(S("st"), t + (5 * NT + 1))
                if not first:
                    pe.wait_ge(S("y0_dve"), t - 1)
                mm2(pb[slot][:, 0:D], slot, lambda h: wm[:, h, :], D, last=False)
                te_.matmul(pb[slot][:, 0:D], b_ones3, b_row3[:, 0, :], start=False, stop=True)
                mm2(pb[2 + slot][:, 0:D], slot, lambda h: wl[:, h, :], D).then_inc(S("y0_mm"), 1)
            tiles(pe, y0_body)

            pe.sem_inc(S("gc_used"), NG)
            pe.sem_inc(S("gc_mm"), 1)
            with pe.Fori(0, LAYERS, 1) as layer:
                with pe.Fori(0, NIT1, 1) as it:
                    for g in range(NG):
                        n = layer * (NIT1 * NG) + it * NG
                        pe.wait_ge(S("gc_sel"), n + (g + 1))
                        pe.wait_ge(S(f"gc_got{g}"), (layer * NIT1 + it) * (16 * GRP) + 16 * GRP)
                        pe.wait_ge(S("gc_added"), n + (g + 1))
                        for pair in (2 * g, 2 * g + 1):
                            for h in range(2):
                                for s in (2 * pair, 2 * pair + 1):
                                    m = te_.matmul(pb[pair % 4][:, h * P:h * P + P], ring[:, s, h * P:h * P + P],
                                                   sel[:, s, :], start=(s % 2 == 0), stop=(s % 2 == 1))
                        m.then_inc(S("gc_used"), 1)

                def fin(t, te, slot, first, last):
                    pe.wait_ge(S("gc_st"), layer * NT + t + 1)
                    pe.wait_ge(S("gc_fin"), layer * NT + t + 1)
                    mm2(pb[4 + slot][:, 0:D], slot, lambda h: wl[:, h, :], D).then_inc(S("gc_mm"), 1)
                tiles(pe, fin)

            ln_tensor(pe, 3)
            pe.wait_ge(S("w_gat"), 16 * 6)
            pe.wait_ge(S("ln_xt"), 4 * NT)

            def gt(t, te, slot, first, last):
                pe.wait_ge(S("st"), t + (6 * NT + 1))
                if not first:
                    pe.wait_ge(S("gt_dve"), t - 1)
                mm2(pb[slot][:, 0:16], slot, lambda h: a_wg[:, h, :], 16).then_inc(S("gt_mm"), 1)
            tiles(pe, gt)
            pe.wait_ge(S("rows"), 1)
            pe.sem_inc(S("ga_red"), 8)
            pe.sem_inc(S("ga_dmm"), GRP)
            with pe.Fori(0, NIT2, 1) as it:
                for s in range(RING):
                    if s % GRP == 0:
                        g = s // GRP
                        pe.wait_ge(S("ga_nsel"), it * NG + (g + 1))
                        pe.wait_ge(S(f"ga_got{g}"), it * (16 * GRP) + 16 * GRP)
                    pe.wait_ge(S("ga_red"), it * RING + (s + 1))
                    te_.matmul(pb[s % 8][:, :], a_nsel[:, s, :], a_far, start=True, stop=False)
                    for h in range(HEADS):
                        m = te_.matmul(pb[s % 8][:, h * P:h * P + P], bc(a_g20[:, s, 16 + h:17 + h], [P, P]),
                                       ident[:, :], start=False, stop=(h == HEADS - 1))
                    m.then_inc(S("ga_dmm"), 1)

            def turn(n, b, groups=range(NG)):
                for g in groups:
                    pe.wait_ge(S("gb_sel"), n * NG + (g + 1))
                    if g >= 2:
                        pe.wait_ge(S("gb_selT"), n * NG + (g - 1))
                    for c in range(GRP):
                        m = te_.transpose(pb[g % 2][:, :].bitcast(BF16)[:, c * P:c * P + P],
                                          a_sel[b][:, g * GRP + c, :], a_ident)
                    m.then_inc(S("gb_tp"), 1)

            def node_values(n, hits):
                for s in range(RING):
                    if s % GRP == 0:
                        pe.wait_ge(S("gb_selT"), n * NG + (s // GRP + 1))
                    m = te_.matmul(pb[2][:, s * 24:s * 24 + 24], a_selT[:, s, :], node(a_am3, hits[s // 2]),
                                   start=True, stop=True)
                m.then_inc(S("gb_eg"), 1)

            def pe_hits(n):
                return nc.values_load_multi_w_load_instructions(
                    hit2[0:1, bass.ds(n * (RING // 2), RING // 2)], engines=(mybir.EngineType.PE,),
                    min_val=0, max_val=NT - 1)[1]

            def weighted(n, b):
                pe.wait_ge(S("gb_msg"), n + 1)
                for s in range(RING):
                    m = te_.matmul(pb[3 + b][:, s // 2 * (3 * C20):(s // 2 + 1) * (3 * C20)], a_sel[b][:, s, :], a_msg3[:, s, :],
                                   start=(s % 2 == 0), stop=(s % 2 == 1))
                m.then_inc(S("gb_mm"), 1)

            def step(n, b):
                hits = pe_hits(n + 1)
                turn(n + 1, 1 - b, range(NG // 2))
                weighted(n, b)
                turn(n + 1, 1 - b, range(NG // 2, NG))
                node_values(n + 1, hits)
            pe.wait_ge(S("ga_red"), NIT2 * RING + 8)
            pe.sem_inc(S("gb_mm"), 2)
            pe.wait_ge(S("self_z"), 1)
            turn(0, 0)
            node_values(0, pe_hits(0))
            with pe.Fori(0, NIT2 // 2 - 1, 1) as q:
                step(q * 2, 0)
                step(q * 2 + 1, 1)
            step(NIT2 - 2, 0)
            weighted(NIT2 - 1, 1)

            ln_tensor(pe, 4)
            pe.wait_ge(S("w_moe"), 16 * (3 * NX + 1))
            pe.wait_ge(S("ln_xt"), 5 * NT)
            pe.wait_ge(S("moe_b"), 1)

            def moe(c, n):
                def hidden(e):
                    for b in range(XB):
                        pe.wait_ge(S("eh_act"), c * (NX * XB) + e * XB + b + 1)
                        for h in range(2):
                            w = e_w1[:, e, h * XH + b * P:h * XH + b * P + P]
                            if n == 4:
                                m = te_.matmul(pb[b][:, :].rearrange("p (t n) -> p t n", t=4), w,
                                               xtv[:, bass.ds(c * 4, 4), h, :], start=(h == 0), stop=(h == 1))
                            else:
                                m = te_.matmul(pb[b][:, 0:P], w, xtv[:, NT - 1, h, :], start=(h == 0), stop=(h == 1))
                        m.then_inc(S("eh_mm"), 1)

                def output(e):
                    pe.wait_ge(S("eh_act"), c * (NX * XB) + (e + 1) * XB + 4)
                    for j in range(n):
                        pe.wait_ge(S("eo_dve"), c * (4 * NX) + e * n + j + 1 + (4 - n))
                        for b in range(XB):
                            te_.matmul(pb[4 + j][:, 0:D], e_ht[:, e % 2, b, j * P:j * P + P],
                                       e_w2[:, e, b * D:(b + 1) * D], start=(b == 0), stop=False)
                        te_.matmul(pb[4 + j][:, 0:D], b_ones3, e_b3[:, e, :], start=False,
                                   stop=True).then_inc(S("eo_mm"), 1)
                for e in range(NX):
                    hidden(e)
                    if e:
                        output(e - 1)
                output(NX - 1)
            with pe.Fori(0, NT // 4, 1) as c:
                moe(c, 4)
            moe(NT // 4, 1)

        @block.vector
        def _(dve):
            v = nc.vector
            dve.wait_ge(S("consts"), 5)
            dve.wait_ge(S("edges1"), 16 * 8)
            bin_vector(dve, 1)
            dve.wait_ge(S("w_rel"), 16 * (NB + 4))
            w4 = w_all.rearrange("p h (r o) -> p h r o", r=R)
            for b in range(NB):
                for r in range(R):
                    c = sm[:, 10, r * NB + b:r * NB + b + 1]
                    base = w_base[:, b, :].rearrange("p (h o) -> p h o", h=2)
                    if b == 0:
                        v.tensor_scalar(w4[:, :, r, :], base, c, None, ALU.mult)
                    else:
                        v.scalar_tensor_tensor(out=w4[:, :, r, :], in0=base, scalar=c, in1=w4[:, :, r, :],
                                               op0=ALU.mult, op1=ALU.add)
                dve.drain()
            v.drain().then_inc(S("w_all"), 1)
            dve.wait_ge(S("x"), 32)
            ln_vector(dve, 0)
            dve.wait_ge(S("edges2"), 32)
            bin_vector(dve, 2)

            scattered(dve, 1)
            dve.wait_ge(S("hr_put0"), 16 * ((NT + 1) // 2))
            dve.wait_ge(S("hr_put1"), 16 * (NT // 2))
            dve.wait_ge(S("filled1"), 16 * 8)
            dve.wait_ge(S("filled2"), 16 * 8)
            v.memset(r_agg, 0.0)
            v.memset(deg[:, :], 0.0)
            v.memset(ring[:, :, D:D + 1], 1.0)
            dve.wait_ge(S("tab1"), 16)
            dve.drain()
            dve.sem_inc(S("rg_added"), 2)

            def hits_of(hit, it):
                return nc.values_load_multi_w_load_instructions(
                    hit[0:1, bass.ds(it * (RING // 2), RING // 2)], engines=(mybir.EngineType.DVE,),
                    min_val=0, max_val=NT - 1)[1]

            build_sel(dve, "rg", tab1, 1, 0)
            with dve.Fori(0, NIT1, 1) as it:
                hits = hits_of(hit1, it)
                for g in range(NG):
                    dve.wait_ge(S("rg_used"), it * NG + (g + 1 + NG))
                    for pair in (2 * g, 2 * g + 1):
                        o, dg = node(agg, hits[pair]), one(deg, hits[pair])
                        v.tensor_tensor(o, o, pb[pair % 4][:, 0:D], ALU.add)
                        v.tensor_tensor(dg, dg, pb[pair % 4][:, D:D + 1], ALU.add)
                        dr = v.drain()
                    dr.then_inc(S("rg_added"), 1)
                    group_sel(dve, "rg", tab1, 1, it + 1, g)
            v.drain().then_inc(S("rg_done"), 1)

            def red(c, slot):
                dve.wait_ge(S("kt_mm"), c + 1)
                v.tensor_reduce(m_max[:, col(c)] if not isinstance(c, int) else m_max[:, c:c + 1],
                                pb[slot][:, :], AX, ALU.max).then_inc(S("kt_red"), 1)
            with dve.Fori(0, NT // 8, 1) as c:
                red(c * 2, 0)
                red(c * 2 + 1, 1)
            dve.wait_ge(S("kt_mm"), NT // 4 + 1)
            v.tensor_reduce(m_max[:, NT // 4:NT // 4 + 1], pb[0][:, 0:LAST], AX, ALU.max)
            v.memset(m_nr[0:1, :], 0.0)
            v.memset(m_cx, 0.0)
            dve.drain()
            v.tensor_reduce(m_max[:, 13:14], m_max[:, 0:NT // 4 + 1], AX, ALU.max)
            dve.drain()
            v.tensor_scalar(m_max[:, 14:15], m_max[:, 13:14], -1.0, None, ALU.mult).then_inc(S("m0_neg"), 1)
            dve.wait_ge(S("m0_row"), 1)
            v.tensor_copy(m_nr[0:1, 0:P], pb[2][0:1, 0:P]).then_inc(S("m0_max"), 1)

            def m0_add(t, te, slot, first, last):
                dve.wait_ge(S("m0_cx"), t + 1)
                v.tensor_tensor(m_cx[:, 0:P + 1], m_cx[:, 0:P + 1], pb[2 + slot][:, 0:P + 1], ALU.add)
                v.drain().then_inc(S("m0_add"), 1)
            tiles(dve, m0_add)
            v.reciprocal(m_max[:, 15:16], m_cx[:, P:P + 1])
            v.tensor_tensor(m_cx[:, 0:P], m_cx[:, 0:P], mask32[:, :], ALU.mult)
            v.drain().then_inc(S("m0_ctx"), 1)
            dve.wait_ge(S("m0_a"), 1)
            v.tensor_scalar(m_a, pb[1][:, 0:D], m_max[:, 15:16], 32.0 ** -0.5, ALU.mult, ALU.mult)
            v.tensor_copy(m_qT, pb[0][:, 0:D])
            v.drain().then_inc(S("m0_sc"), 1)
            dve.wait_ge(S("m0_m"), 1)
            for h in range(2):
                v.tensor_copy(wm[:, h, :], pb[2 + h][:, 0:D])
            split_rows(dve, b_row3, brow[:, :, :])
            v.drain().then_inc(S("wm"), 1)

            def x1(t, te, slot, first, last):
                dve.wait_ge(S("x1_mm"), t + 1)
                v.tensor_tensor(x_t1, node(agg, t), pb[slot][:, 0:D], ALU.add)
                v.tensor_tensor(x_t2, node(xs, t), pb[2 + slot][:, 0:D], ALU.add)
                v.drain().then_inc(S("x1_dve"), 1)
                v.scalar_tensor_tensor(out=node(xs, t), in0=x_t1, scalar=0.0, in1=x_t2, op0=ALU.max, op1=ALU.add)
                dve.drain()
            tiles(dve, x1)
            v.drain().then_inc(S("x1"), 1)
            v.tensor_scalar(deg[:, :], deg[:, :], 1.0, None, ALU.max)
            v.tensor_scalar(tab1[:, 0:T1, 0], tab1[:, 0:T1, 0], R.bit_length() - 1, None, ALU.logical_shift_right)
            dve.drain()
            v.reciprocal(deg[:, :], deg[:, :])
            dve.drain()
            v.tensor_scalar(deg[:, :], deg[:, :], 1.0 - ALPHA, None, ALU.mult)
            dve.wait_ge(S("w_ffn"), 16 * 6)

            def route(t, slot):
                v.tensor_tensor(f_tmp, xn[:, slot, :], f_wr, ALU.mult)
                v.tensor_tensor(node(xs, t), node(xs, t), xn[:, slot, :], ALU.add)
                dve.drain()
                v.tensor_reduce(one(f_w, t), f_tmp, AX, ALU.add)
                dve.drain()
            ln_vector(dve, 1, extra=route)
            w = f_w[:, 0:NT]
            v.tensor_scalar(w, w, f_br[:, 0:1], None, ALU.add)
            key, cand, bit, t_i, one_i, n_i = (f_key[:, i:i + 1] for i in range(6))
            v.memset(key, 0)
            v.memset(one_i, 1)
            dve.drain()
            v.tensor_scalar(bit, one_i, 31, None, ALU.logical_shift_left)
            v.tensor_tensor(w, w, valid[:, :], ALU.mult)
            v.tensor_scalar(f_pre[:, 0:NT], valid[:, :], -1.0, 3.0e38, ALU.add, ALU.mult)
            dve.drain()
            v.tensor_tensor(w, w, f_pre[:, 0:NT], ALU.add)
            dve.drain()

            def threshold_of(k):
                f = f_cnt[:, 2:3].bitcast(I32)
                v.tensor_scalar(t_i, k, 31, -1, ALU.arith_shift_right, ALU.bitwise_xor)
                v.tensor_scalar(n_i, one_i, 31, None, ALU.logical_shift_left)
                dve.drain()
                v.tensor_tensor(t_i, t_i, n_i, ALU.bitwise_or)
                dve.drain()
                v.tensor_tensor(f, k, t_i, ALU.bitwise_xor)
                dve.drain()

            with dve.Fori(0, 32, 1) as i:
                v.tensor_tensor(cand, key, bit, ALU.bitwise_or)
                dve.drain()
                threshold_of(cand)
                v.tensor_scalar(f_ge[:, 0:NT], w, f_cnt[:, 2:3], None, ALU.is_ge)
                dve.drain()
                v.tensor_reduce(f_cnt[:, 0:1], f_ge[:, 0:NT], AX, ALU.add).then_inc(S("th_cnt"), 1)
                dve.wait_ge(S("th_mm"), i + 1)
                v.tensor_scalar(t_i, pb[7][:, 0:1], float(KEEP), -1.0, ALU.is_ge, ALU.mult)
                dve.drain()
                v.tensor_tensor(t_i, t_i, bit, ALU.bitwise_and)
                dve.drain()
                v.tensor_tensor(key, key, t_i, ALU.bitwise_or)
                v.tensor_scalar(bit, bit, 1, None, ALU.logical_shift_right)
                dve.drain()
            threshold_of(key)
            v.tensor_scalar(f_gt[:, 0:NT], w, f_cnt[:, 2:3], None, ALU.is_gt)
            v.tensor_scalar(f_eq[:, 0:NT], w, f_cnt[:, 2:3], None, ALU.is_equal)
            v.drain().then_inc(S("th_eq"), 1)
            dve.wait_ge(S("th_pre"), 1)
            a, b = sm[:, 0, 0:NT], sm[:, 1, 0:NT]
            v.tensor_reduce(f_cnt[:, 3:4], pb[4][:, 0:NT], AX, ALU.add)
            v.tensor_copy(a, pb[6][:, 0:NT])
            dve.drain()
            v.tensor_scalar(f_cnt[:, 4:5], f_cnt[:, 3:4], -1.0, float(KEEP), ALU.mult, ALU.add)
            v.tensor_tensor_scan(b, ones[:, 0:NT], a, 0.0, ALU.mult, ALU.add)
            dve.drain()
            v.tensor_tensor(b, b, a, ALU.subtract)
            dve.drain()
            v.tensor_tensor(b, b, pb[5][:, 0:NT], ALU.add)
            dve.drain()
            v.tensor_scalar(b, b, f_cnt[:, 4:5], None, ALU.is_lt)
            dve.drain()
            v.tensor_tensor(b, b, f_eq[:, 0:NT], ALU.mult)
            dve.drain()
            v.tensor_tensor(b, b, f_gt[:, 0:NT], ALU.add)
            dve.drain()
            v.tensor_tensor(coef[:, :], b, w, ALU.mult)
            split_rows(dve, b_row3[:, 0, :], brow[:, 0, :])
            v.drain().then_inc(S("coef"), 1)
            dve.sem_inc(S("fo_dve"), 4)

            def ffn_out(c, n):
                for j in range(n):
                    t = c * 4 + j
                    dve.wait_ge(S("fo_mm"), t + 1)
                    v.scalar_tensor_tensor(out=node(xs, t), in0=pb[4 + j][:, 0:D], scalar=one(coef, t), in1=node(xs, t),
                                           op0=ALU.mult, op1=ALU.add).then_inc(S("fo_dve"), 1)
            with dve.Fori(0, NT // 4, 1) as c:
                ffn_out(c, 4)
            ffn_out(NT // 4, 1)
            v.drain().then_inc(S("x2"), 1)
            ln_vector(dve, 2, store_sem=[S("f0_put0"), S("f0_put1")])

            dve.wait_ge(S("g_tr"), 1)
            for h in range(2):
                v.tensor_copy(g_kvw[:, h, :], pb[h][:, :])
                v.tensor_copy(g_wo[:, h, :], pb[2 + h][:, 0:D])
                for i in range(4):
                    v.tensor_copy(g_gam[:, 4 * h + i, :], g_ln[:, 2 * h, :])
                    v.tensor_copy(g_bet[:, 4 * h + i, :], g_ln[:, 2 * h + 1, :])
            v.memset(g_acc, 0.0)
            v.drain().then_inc(S("g_w"), 1)

            def kv_stats(t, te, slot, first, last):
                dve.wait_ge(S("k1_mm"), t + 1)
                for i in range(8):
                    o = g_st[:, t * 8 + i, :] if isinstance(t, int) else node(g_st, t * 8 + i)
                    ins = v.bn_stats(o, pb[slot][:, i * 64:i * 64 + 64])
                ins.then_inc(S("k1_dve"), 1)
            tiles(dve, kv_stats)
            dve.drain()
            v.tensor_tensor(g_m, g_st[:, :, 1], g_st[:, :, 4], ALU.add)
            v.tensor_tensor(g_t1, g_st[:, :, 1], g_st[:, :, 4], ALU.subtract)
            v.tensor_tensor(g_t3, g_st[:, :, 2], g_st[:, :, 5], ALU.add)
            dve.drain()
            v.tensor_scalar(g_m, g_m, 0.5, None, ALU.mult)
            v.tensor_tensor(g_t1, g_t1, g_t1, ALU.mult)
            v.tensor_scalar(g_t3, g_t3, 1.0 / 64, EPS, ALU.mult, ALU.add)
            dve.drain()
            v.scalar_tensor_tensor(out=g_t3, in0=g_t1, scalar=0.25, in1=g_t3, op0=ALU.mult, op1=ALU.add)
            dve.drain()
            rsqrt_vector(dve, "kv", g_r, g_t3, g_t1, g_t2)
            v.scalar_tensor_tensor(out=g_t1, in0=g_m, scalar=-1.0, in1=g_r, op0=ALU.mult, op1=ALU.mult)
            v.drain().then_inc(S("kv_mr"), 1)

            def kv_norm(t, te, slot, first, last):
                dve.wait_ge(S("k2_nm"), t + 1)
                o = g_kv[:, slot, :].rearrange("p (g n) -> p g n", g=8)
                v.tensor_tensor(o, o, g_gam, ALU.mult)
                dve.drain()
                v.tensor_tensor(o, o, g_bet, ALU.add).then_inc(S("k2_kv"), 1)
                if not (isinstance(t, int) and t == 0):
                    add_context(t - 1, 1 - slot)

            def add_context(t, slot):
                dve.wait_ge(S("k2_cx"), t + 1)
                acc = g_acc.rearrange("p h n -> p (h n)")
                v.tensor_tensor(acc, acc, pb[2 + slot][:, 0:D], ALU.add)
                v.drain().then_inc(S("k2_add"), 1)
            tiles(dve, kv_norm)
            add_context(NT - 1, 0)
            for h in range(2):
                v.scalar_tensor_tensor(out=g_acc[:, h, :], in0=g_acc[:, h, :], scalar=1.0 / N, in1=mask64[:, :],
                                       op0=ALU.mult, op1=ALU.mult)
            v.drain().then_inc(S("g_ctx"), 1)
            dve.wait_ge(S("g_am"), 1)
            for h in range(2):
                v.tensor_copy(g_a[:, h, :], pb[4 + h][:, 0:D])
            v.drain().then_inc(S("g_a"), 1)
            dve.wait_ge(S("g_m"), 1)
            for h in range(2):
                v.tensor_copy(wm[:, h, :], pb[6 + h][:, 0:D])
            split_rows(dve, b_row3[:, 0, :], brow[:, 0, :])
            v.drain().then_inc(S("g_wm"), 1)

            def y0_part(t, te, slot, first, last):
                dve.wait_ge(S("y0_mm"), t + 1)
                v.tensor_tensor(node(xs, t), node(xs, t), pb[slot][:, 0:D], ALU.add)
                v.tensor_scalar(node(y0, t), pb[2 + slot][:, 0:D], ALPHA, None, ALU.mult)
                v.drain().then_inc(S("y0_dve"), 1)
            tiles(dve, y0_part)
            dve.drain()
            dve.sem_inc(S("gc_tab"), 1)
            v.memset(r_agg, 0.0)
            dve.drain()
            dve.sem_inc(S("gc_added"), 2)
            dve.sem_inc(S("gc_fin"), 2)

            with dve.Fori(0, LAYERS, 1) as layer:
                with dve.Fori(0, NIT1, 1) as it:
                    n = layer * (NIT1 * NG) + it * NG
                    hits = hits_of(hit1, it)
                    build_sel(dve, "gc", tab1, 1, it)
                    for g in range(NG):
                        dve.wait_ge(S("gc_used"), n + (g + 1 + NG))
                        for pair in (2 * g, 2 * g + 1):
                            o = node(agg, hits[pair])
                            v.tensor_tensor(o, o, pb[pair % 4][:, 0:D], ALU.add)
                            dr = v.drain()
                        dr.then_inc(S("gc_added"), 1)
                v.drain().then_inc(S("gc_summed"), 1)

                def fin(t, te, slot, first, last):
                    dve.wait_ge(S("gc_mm"), layer * NT + t + 1 + 1)
                    v.scalar_tensor_tensor(out=node(agg, t), in0=pb[4 + slot][:, 0:D], scalar=one(deg, t),
                                           in1=node(y0, t), op0=ALU.mult, op1=ALU.add).then_inc(S("gc_fin"), 1)
                tiles(dve, fin)
                dve.wait_ge(S("gc_put"), layer * (16 * (NT // 7)) + 16 * (NT // 7))
                dve.sem_inc(S("gc_tab"), 1)
                v.memset(r_agg, 0.0)
                dve.drain()

            dve.wait_ge(S("f5"), 16)
            v.tensor_tensor(r_x, r_x, r_xt, ALU.add)
            dve.drain()
            ln_vector(dve, 3)

            dve.wait_ge(S("w_gat"), 16 * 6)

            def gt(t, te, slot, first, last):
                dve.wait_ge(S("gt_mm"), t + 1)
                o = a_rows[:, t, 0:16] if isinstance(t, int) else a_rows[:, col(t), 0:16].rearrange("p a n -> p (a n)")
                v.tensor_copy(o, pb[slot][:, 0:16]).then_inc(S("gt_dve"), 1)
            tiles(dve, gt)
            dve.drain()
            sh3, sh4 = [P, NT, 16], [P, NT, HEADS]
            tmp = a_sum[:, :, 0:16]
            tmp4 = tmp.rearrange("p t (h e) -> p t h e", h=HEADS)
            for i, o in ((0, a_rows[:, :, 16:20]), (1, a_am[:, :, 0:4])):
                v.tensor_tensor(tmp, a_rows[:, :, 0:16], bc(a_row[:, i, :].unsqueeze(1), sh3), ALU.mult)
                dve.drain()
                v.tensor_reduce(o, tmp4, AX, ALU.add)
                dve.drain()
            for h in range(HEADS):
                v.tensor_scalar(a_far[:, h * P:h * P + P], ident[:, :], -FAR, None, ALU.mult)
            v.tensor_copy(a_mx, a_rows[:, :, 16:20])
            v.drain().then_inc(S("rows"), 1)
            z4 = a_z.rearrange("p (n e) h -> p n e h", e=2)
            with dve.Fori(0, NIT2, 1) as it:
                hits = hits_of(hit2, it)
                for s in range(RING):
                    dve.wait_ge(S("ga_dmm"), it * RING + (s + 1 + GRP))
                    v.tensor_reduce(a_z[:, s, :], pb[s % 8][:, :].rearrange("p (h n) -> p h n", h=HEADS), AX,
                                    ALU.max).then_inc(S("ga_red"), 1)
                dve.drain()
                v.tensor_tensor(a_z2[:, 0:RING // 2, :], z4[:, :, 0, :], z4[:, :, 1, :], ALU.max)
                dve.drain()
                for pair in range(RING // 2):
                    o = node(a_mx, hits[pair])
                    v.tensor_tensor(o, o, a_z2[:, pair, :], ALU.max)
                    dve.drain()
            v.tensor_tensor(a_mx, a_mx, a_am[:, :, 0:4], ALU.add)
            dve.drain()
            v.scalar_tensor_tensor(out=a_am[:, :, 4:8], in0=a_mx, scalar=0.2, in1=a_mx, op0=ALU.mult, op1=ALU.max)
            dve.drain()
            split(dve, [a_am3[:, :, 8 * i:8 * i + 8] for i in range(3)], a_am, a_res8)
            v.tensor_copy(a_ident, ident[:, :])
            v.tensor_tensor(a_mx, a_rows[:, :, 16:20], a_am[:, :, 0:4], ALU.add)
            dve.drain()
            v.scalar_tensor_tensor(out=a_mx, in0=a_mx, scalar=0.2, in1=a_mx, op0=ALU.mult, op1=ALU.max)
            dve.drain()
            v.tensor_tensor(a_mx, a_mx, a_am[:, :, 4:8], ALU.subtract)
            v.drain().then_inc(S("self_z"), 1)
            dve.wait_ge(S("self_e"), 1)
            sh_e = [P, NT, HEADS, 4]
            v.tensor_tensor(tmp4, a_rows[:, :, 0:16].rearrange("p t (h e) -> p t h e", h=HEADS),
                            bc(a_sum[:, :, 16:20].unsqueeze(3), sh_e), ALU.mult)
            dve.drain()
            eg3 = pb[2][:, 0:RING * 24].rearrange("p (s k c) -> p s c k", k=3, c=8)

            def messages(n):
                dve.wait_ge(S("gb_eg"), n + 1)
                rows = a_g[:, bass.ds(n * RING, RING), :]
                v.tensor_reduce(a_eg, eg3, AX, ALU.add)
                dve.drain()
                v.tensor_tensor(a_z, rows[:, :, 16:20], a_eg[:, :, 0:4], ALU.add)
                dve.drain()
                v.scalar_tensor_tensor(out=a_z, in0=a_z, scalar=0.2, in1=a_z, op0=ALU.mult, op1=ALU.max)
                dve.drain()
                v.tensor_tensor(a_z, a_z, a_eg[:, :, 4:8], ALU.subtract)
                v.drain().then_inc(S("gb_z"), 1)
                dve.wait_ge(S("gb_ee"), n + 1)
                v.tensor_tensor(a_msg[:, :, 0:16].rearrange("p s (h e) -> p s h e", h=HEADS),
                                rows[:, :, 0:16].rearrange("p s (h e) -> p s h e", h=HEADS),
                                bc(a_msg[:, :, 16:20].unsqueeze(3), [P, RING, HEADS, 4]), ALU.mult)
                dve.drain()
                dve.wait_ge(S("gb_mm"), n + 2)
                split(dve, [a_msg3[:, :, C20 * i:C20 * i + C20] for i in range(3)], a_msg, a_rest)
                v.drain().then_inc(S("gb_msg"), 1)

            def add_sums(n, b):
                hits = hits_of(hit2, n)
                dve.wait_ge(S("gb_mm"), n + 3)
                v.tensor_reduce(a_part, pb[3 + b][:, 0:RING // 2 * 3 * C20].rearrange("p (n k c) -> p n c k", k=3, c=C20),
                                AX, ALU.add)
                dve.drain()
                for pair in range(RING // 2):
                    o = node(a_sum, hits[pair])
                    v.tensor_tensor(o, o, a_part[:, pair, :], ALU.add)
                    dve.drain()
            messages(0)
            with dve.Fori(0, NIT2 // 2 - 1, 1) as q:
                for b in range(2):
                    messages(q * 2 + b + 1)
                    add_sums(q * 2 + b, b)
            messages(NIT2 - 1)
            add_sums(NIT2 - 2, 0)
            add_sums(NIT2 - 1, 1)

            v.tensor_scalar(s_d, a_sum[:, :, 16:20], 1e-16, None, ALU.add)
            dve.drain()
            v.reciprocal(s_e, s_d)
            dve.drain()
            h4 = s_h.rearrange("p t (h e) -> p t h e", h=HEADS)
            v.tensor_tensor(h4, tmp4, bc(s_e.unsqueeze(3), sh_e), ALU.mult)
            dve.drain()
            v.tensor_tensor(s_h, s_h, bc(a_row[:, 2, :].unsqueeze(1), sh3), ALU.add)
            dve.drain()
            v.tensor_reduce(s_v[0], s_h, AX, ALU.add)
            dve.drain()
            v.tensor_scalar(s_v[0], s_v[0], 1.0 / 16, None, ALU.mult)
            dve.drain()
            v.tensor_tensor(s_a, s_h, bc(s_v[0].unsqueeze(2), sh3), ALU.subtract)
            dve.drain()
            v.tensor_tensor(s_b, s_a, s_a, ALU.mult)
            dve.drain()
            v.tensor_reduce(s_v[1], s_b, AX, ALU.add)
            dve.drain()
            v.tensor_scalar(s_v[1], s_v[1], 1.0 / 16, EPS, ALU.mult, ALU.add)
            dve.drain()
            rsqrt_vector(dve, "sc", s_v[0], s_v[1], s_v[2], s_v[3])
            v.tensor_tensor(s_a, s_a, bc(s_v[0].unsqueeze(2), sh3), ALU.mult)
            dve.drain()
            v.tensor_tensor(s_a, s_a, bc(a_row[:, 3, :].unsqueeze(1), sh3), ALU.mult)
            dve.drain()
            v.tensor_tensor(s_a, s_a, bc(a_row[:, 4, :].unsqueeze(1), sh3), ALU.add)
            dve.drain()
            v.tensor_reduce(s_sc, s_a.rearrange("p t (h e) -> p t e h", h=HEADS), AX, ALU.add)
            dve.drain()
            v.tensor_scalar(s_sc, s_sc, 1.0 / HEADS, None, ALU.mult)
            v.memset(s_g, 0.0)
            dve.drain()
            for e in range(NX):
                for f in range(NX):
                    if f != e:
                        v.tensor_tensor(s_v[4], s_sc[:, :, f], s_sc[:, :, e], ALU.is_ge if f < e else ALU.is_gt)
                        dve.drain()
                        v.tensor_tensor(s_g[:, :, e], s_g[:, :, e], s_v[4], ALU.add)
                        dve.drain()
            v.tensor_reduce(s_v[5], s_sc, AX, ALU.max)
            v.tensor_scalar(s_g, s_g, 2.0, None, ALU.is_lt)
            dve.drain()
            v.tensor_tensor(s_d, s_sc, bc(s_v[5].unsqueeze(2), [P, NT, NX]), ALU.subtract)
            v.drain().then_inc(S("sc_e"), 1)
            dve.wait_ge(S("sc_exp"), 1)
            v.tensor_tensor(s_e, s_e, s_g, ALU.mult)
            dve.drain()
            v.tensor_reduce(s_v[4], s_e, AX, ALU.add)
            dve.drain()
            v.reciprocal(s_v[5], s_v[4])
            dve.drain()
            v.tensor_tensor(gates, s_e, bc(s_v[5].unsqueeze(2), [P, NT, NX]), ALU.mult)
            v.drain().then_inc(S("gates"), 1)
            ln_vector(dve, 4)
            dve.wait_ge(S("w_moe"), 16 * (3 * NX + 1))
            split_rows(dve, e_b3, e_b2)
            v.drain().then_inc(S("moe_b"), 1)
            dve.sem_inc(S("eo_dve"), 4)

            def moe_out(c, n):
                for e in range(NX):
                    for j in range(n):
                        t = c * 4 + j
                        dve.wait_ge(S("eo_mm"), c * (4 * NX) + e * n + j + 1)
                        gv = gates[:, t, e:e + 1] if isinstance(t, int) else \
                            gates[:, col(t), e:e + 1].rearrange("p a n -> p (a n)")
                        v.scalar_tensor_tensor(out=node(xs, t), in0=pb[4 + j][:, 0:D], scalar=gv, in1=node(xs, t),
                                               op0=ALU.mult, op1=ALU.add)
                        v.drain().then_inc(S("eo_dve"), 1)
            with dve.Fori(0, NT // 4, 1) as c:
                moe_out(c, 4)
            moe_out(NT // 4, 1)
            v.drain().then_inc(S("x4"), 1)


_INS = ['x', 'src', 'dst', 'edge_type_8', 'edge_weight1', 'L0_gnn_weight', 'L0_gnn_w_comp', 'L0_gnn_loop_weight',
        'L0_gnn_h_bias', 'L0_mix_W_qkv', 'L0_mix_W_out', 'L0_mix_b_out', 'L0_ffn_wr', 'L0_ffn_br', 'L0_ffn_w1',
        'L0_ffn_b1', 'L0_ffn_w2', 'L0_ffn_b2', 'L1_gnn_W', 'L1_mix_wq', 'L1_mix_wk', 'L1_mix_wv', 'L1_mix_wo',
        'L1_mix_bo', 'L1_mix_ln_k_g', 'L1_mix_ln_k_b', 'L1_mix_ln_v_g', 'L1_mix_ln_v_b', 'L1_ffn_W_gat',
        'L1_ffn_att_src', 'L1_ffn_att_dst', 'L1_ffn_b_gat', 'L1_ffn_ln_gamma', 'L1_ffn_ln_beta', 'L1_ffn_W1',
        'L1_ffn_b1', 'L1_ffn_W2', 'L1_ffn_b2', 'L1_ffn_edge_index']


def kernel(**inputs):
    import numpy as _np
    import concourse.bacc as _bacc
    from concourse import mybir as _mybir
    from concourse.bass_utils import run_bass_kernel_spmd as _run

    nc = _bacc.Bacc("TRN2", target_bir_lowering=False, num_devices=1, dynamic_dma_scratch_size=4096)
    arrays, args = {}, []
    for name in _INS:
        a = _np.ascontiguousarray(inputs[name])
        if name == 'edge_weight1':
            a = a.reshape(-1)
        if name in ('L0_ffn_b1', 'L1_ffn_b1'):
            a = _np.ascontiguousarray(a.reshape(-1, 128).T)
        arrays[f"in_{name}_dram"] = a
        args.append(nc.dram_tensor(f"in_{name}_dram", a.shape, _mybir.dt.from_np(a.dtype), kind="ExternalInput").ap())
    o = nc.dram_tensor("out_0_dram", inputs['x'].shape, _mybir.dt.float32, kind="ExternalOutput").ap()
    build(nc, *args, o)
    r = _run(nc, [arrays], core_ids=[0])
    return r.results[0]["out_0_dram"]
```
